# Optimizing a Trainium2 kernel written in Bass

```python
import numpy as np
import jax
import jax.numpy as jnp

def _softmax(x, axis=-1):
    return jax.nn.softmax(x, axis=axis)

def _gelu(x):
    return jax.nn.gelu(x, approximate=True)

def _silu(x):
    return jax.nn.silu(x)

def _sigmoid(x):
    return jax.nn.sigmoid(x)

def _layernorm(x, axis=-1, eps=1e-05):
    m = jnp.mean(x, axis=axis, keepdims=True)
    v = jnp.var(x, axis=axis, keepdims=True)
    return (x - m) / jnp.sqrt(v + eps)

def _scatter_add(tgt, idx, src, axis=0):
    return tgt.at[idx].add(src)

def _segment_sum(src, seg, n):
    return jax.ops.segment_sum(src, seg, n)
kernel_name = 'mk_xattn_ffn_d2_seqx_r8_838e70'

def setup_inputs(seed: int=0):
    np.random.seed(seed)
    _w = jnp.asarray

    def _rec_inputs():
        import jax
        import jax.numpy as jnp
        _rk = jax.random.key(seed)
        x = -0.0002928 + 1 * jax.random.normal(jax.random.fold_in(_rk, 1), (128, 64, 128), jnp.float32)
        _lenS = 64 - jax.random.randint(jax.random.fold_in(_rk, 7), (128,), 0, max(1, 64 // 4) + 1, jnp.int32)
        _lenS2 = 64 - jax.random.randint(jax.random.fold_in(_rk, 8), (128,), 0, max(1, 64 // 4) + 1, jnp.int32)
        _ctx_1024P = jax.random.normal(jax.random.fold_in(_rk, 11), (128, 16, 128), jnp.float32)
        _ctx_1024c = jax.random.dirichlet(jax.random.fold_in(_rk, 511), 0.3 * jnp.ones((16,), jnp.float32), (128, 64))
        _ctx_1024t = jnp.einsum('bsk,bkd->bsd', _ctx_1024c, _ctx_1024P)
        _ctx_1024t = _ctx_1024t * jax.lax.rsqrt(jnp.mean(jnp.square(_ctx_1024t)) + 1e-12) * 0.953939
        ctx_1024 = -1.39393e-06 + 0.999914 * (_ctx_1024t + 0.3 * jax.random.normal(jax.random.fold_in(_rk, 611), (128, 64, 128), jnp.float32))
        return (x, ctx_1024)
    x, ctx_1024 = _rec_inputs()

    def _L0_xattn_setup():
        import jax, jax.numpy as jnp
        import numpy as np
        B, S, D, NH = (2, 256, 128, 8)
        DH = D // NH
        EPS = 1e-06
        LN_EPS = 1e-05

        def _mlstm_cell(q, k, v, igate_w, igate_b, fgate_w, fgate_b, ln_scale):
            Slen = q.shape[0]
            ifg = jnp.concatenate([q, k, v], axis=-1)
            ig = (ifg @ igate_w.T + igate_b).T
            fg = (ifg @ fgate_w.T + fgate_b).T
            qh = q.reshape(Slen, NH, DH).transpose(1, 0, 2)
            kh = k.reshape(Slen, NH, DH).transpose(1, 0, 2)
            vh = v.reshape(Slen, NH, DH).transpose(1, 0, 2)
            log_f = jax.nn.log_sigmoid(fg)
            cs = jnp.cumsum(log_f, axis=1)
            fg_mat = cs[:, :, None] - cs[:, None, :]
            mask = jnp.tril(jnp.ones((Slen, Slen), dtype=bool))
            log_fg_mat = jnp.where(mask, fg_mat, -jnp.inf)
            log_D = log_fg_mat + ig[:, None, :]
            max_log_D = jnp.max(log_D, axis=-1, keepdims=True)
            D_mat = jnp.exp(log_D - max_log_D)
            qk = jnp.einsum('hsd,htd->hst', qh, kh) / np.sqrt(DH)
            C = qk * D_mat
            normalizer = jnp.maximum(jnp.abs(C.sum(axis=-1, keepdims=True)), jnp.exp(-max_log_D))
            h = jnp.einsum('hst,htd->hsd', C / (normalizer + EPS), vh)
            h = h.transpose(1, 0, 2).reshape(Slen, D)
            mu = h.mean(axis=-1, keepdims=True)
            var = h.var(axis=-1, keepdims=True)
            return (h - mu) / jnp.sqrt(var + LN_EPS) * ln_scale
        key = jax.random.key(seed)
        ks = jax.random.split(key, 8)
        rnd = lambda k, sh, s=1.0: jax.random.normal(k, sh, dtype=jnp.float32) * s
        return {'q': rnd(ks[0], (B, S, D)), 'k': rnd(ks[1], (B, S, D)), 'v': rnd(ks[2], (B, S, D)), 'igate_w': rnd(ks[3], (NH, 3 * D), 0.02), 'igate_b': jnp.linspace(3.0, 6.0, NH, dtype=jnp.float32), 'fgate_w': rnd(ks[4], (NH, 3 * D), 0.02), 'fgate_b': rnd(ks[5], (NH,), 0.3162278), 'ln_scale': jnp.ones((D,), dtype=jnp.float32)}
    _L0_xattn_all = _L0_xattn_setup()
    _L0_xattn_in = {k: v for k, v in _L0_xattn_all.items() if k in ('igate_w', 'igate_b', 'fgate_w', 'fgate_b', 'ln_scale')}
    del _L0_xattn_all

    def _L0_ffn_setup():
        import jax, jax.numpy as jnp
        import numpy as np
        D, H, E, K, S = (128, 256, 8, 2, 1)
        B, L = (4, 256)
        key = jax.random.key(seed)
        ks = jax.random.split(key, 9)
        std = 0.02
        return {'x': jax.random.normal(ks[0], (B, L, D), dtype=jnp.float32), 'router_w': jax.random.normal(ks[1], (E, D), dtype=jnp.float32) * std, 'experts_bias': jnp.zeros((E,), dtype=jnp.float32), 'w1': jax.random.normal(ks[2], (E, D, H), dtype=jnp.float32) * std, 'w3': jax.random.normal(ks[3], (E, D, H), dtype=jnp.float32) * std, 'w2': jax.random.normal(ks[4], (E, H, D), dtype=jnp.float32) * std, 'sw1': jax.random.normal(ks[5], (S, D, H), dtype=jnp.float32) * std, 'sw3': jax.random.normal(ks[6], (S, D, H), dtype=jnp.float32) * std, 'sw2': jax.random.normal(ks[7], (S, H, D), dtype=jnp.float32) * std}
    _L0_ffn_all = _L0_ffn_setup()
    _L0_ffn_in = {k: v for k, v in _L0_ffn_all.items() if k in ('router_w', 'experts_bias', 'w1', 'w3', 'w2', 'sw1', 'sw3', 'sw2')}
    del _L0_ffn_all

    def _L1_xattn_setup():
        import jax, jax.numpy as jnp
        import numpy as np
        B, S, D = (4, 256, 128)
        H = 16
        HD = D // H
        SCALE = float(HD) ** 0.5

        def _split_heads(x):
            b, s, _ = x.shape
            return x.reshape(b, s, H, HD).transpose(0, 2, 1, 3)
        key = jax.random.key(seed)
        ks = jax.random.split(key, 12)
        lim = 1.0 / np.sqrt(D)

        def lin(kw, kb, out_d, in_d):
            W = jax.random.uniform(kw, (out_d, in_d), jnp.float32, -lim, lim)
            b = jax.random.uniform(kb, (out_d,), jnp.float32, -lim, lim)
            return (W, b)
        Wq, bq = lin(ks[0], ks[1], D, D)
        Wk, bk = lin(ks[2], ks[3], D, D)
        Wv, bv = lin(ks[4], ks[5], D, D)
        Wp, bp = lin(ks[6], ks[7], D, D)
        return {'query': jax.random.normal(ks[8], (B, S, D), jnp.float32), 'key': jax.random.normal(ks[9], (B, S, D), jnp.float32), 'value': jax.random.normal(ks[10], (B, S, D), jnp.float32), 'Wq': Wq, 'bq': bq, 'Wk': Wk, 'bk': bk, 'Wv': Wv, 'bv': bv, 'Wp': Wp, 'bp': bp}
    _L1_xattn_all = _L1_xattn_setup()
    _L1_xattn_in = {k: v for k, v in _L1_xattn_all.items() if k in ('Wq', 'bq', 'Wk', 'bk', 'Wv', 'bv', 'Wp', 'bp')}
    del _L1_xattn_all

    def _L1_ffn_setup():
        import jax, jax.numpy as jnp
        import numpy as np
        D_MODEL = 128
        D_FF = 352
        N_EXPERTS = 8
        key = jax.random.key(seed)
        k_in, k1, k2, k3 = jax.random.split(key, 4)
        scale = 0.02
        inputs = jax.random.normal(k_in, (4, N_EXPERTS * 256, D_MODEL), dtype=jnp.float32)
        w1 = jax.random.normal(k1, (N_EXPERTS, D_MODEL, D_FF), dtype=jnp.float32) * scale
        w3 = jax.random.normal(k3, (N_EXPERTS, D_MODEL, D_FF), dtype=jnp.float32) * scale
        w2 = jax.random.normal(k2, (N_EXPERTS, D_FF, D_MODEL), dtype=jnp.float32) * scale
        return {'inputs': inputs, 'w1': w1, 'w3': w3, 'w2': w2}
    _L1_ffn_all = _L1_ffn_setup()
    _L1_ffn_in = {k: v for k, v in _L1_ffn_all.items() if k in ('w1', 'w3', 'w2')}
    del _L1_ffn_all
    return {'x': x, 'ctx_1024': ctx_1024, 'L0_xattn_igate_w': _L0_xattn_in['igate_w'], 'L0_xattn_igate_b': _L0_xattn_in['igate_b'], 'L0_xattn_fgate_w': _L0_xattn_in['fgate_w'], 'L0_xattn_fgate_b': _L0_xattn_in['fgate_b'], 'L0_xattn_ln_scale': _L0_xattn_in['ln_scale'], 'L0_ffn_router_w': _L0_ffn_in['router_w'], 'L0_ffn_experts_bias': _L0_ffn_in['experts_bias'], 'L0_ffn_w1': _L0_ffn_in['w1'], 'L0_ffn_w3': _L0_ffn_in['w3'], 'L0_ffn_w2': _L0_ffn_in['w2'], 'L0_ffn_sw1': _L0_ffn_in['sw1'], 'L0_ffn_sw3': _L0_ffn_in['sw3'], 'L0_ffn_sw2': _L0_ffn_in['sw2'], 'L1_xattn_Wq': _L1_xattn_in['Wq'], 'L1_xattn_bq': _L1_xattn_in['bq'], 'L1_xattn_Wk': _L1_xattn_in['Wk'], 'L1_xattn_bk': _L1_xattn_in['bk'], 'L1_xattn_Wv': _L1_xattn_in['Wv'], 'L1_xattn_bv': _L1_xattn_in['bv'], 'L1_xattn_Wp': _L1_xattn_in['Wp'], 'L1_xattn_bp': _L1_xattn_in['bp'], 'L1_ffn_w1': _L1_ffn_in['w1'], 'L1_ffn_w3': _L1_ffn_in['w3'], 'L1_ffn_w2': _L1_ffn_in['w2']}

def reference(x, ctx_1024, L0_xattn_igate_w, L0_xattn_igate_b, L0_xattn_fgate_w, L0_xattn_fgate_b, L0_xattn_ln_scale, L0_ffn_router_w, L0_ffn_experts_bias, L0_ffn_w1, L0_ffn_w3, L0_ffn_w2, L0_ffn_sw1, L0_ffn_sw3, L0_ffn_sw2, L1_xattn_Wq, L1_xattn_bq, L1_xattn_Wk, L1_xattn_bk, L1_xattn_Wv, L1_xattn_bv, L1_xattn_Wp, L1_xattn_bp, L1_ffn_w1, L1_ffn_w3, L1_ffn_w2):
    import jax
    import jax.numpy as jnp

    def _L0_xattn_ref(q, k, v, igate_w, igate_b, fgate_w, fgate_b, ln_scale):
        import jax, jax.numpy as jnp
        import numpy as np
        B, S, D, NH = (2, 256, 128, 8)
        DH = D // NH
        EPS = 1e-06
        LN_EPS = 1e-05

        def _mlstm_cell(q, k, v, igate_w, igate_b, fgate_w, fgate_b, ln_scale):
            Slen = q.shape[0]
            ifg = jnp.concatenate([q, k, v], axis=-1)
            ig = (ifg @ igate_w.T + igate_b).T
            fg = (ifg @ fgate_w.T + fgate_b).T
            qh = q.reshape(Slen, NH, DH).transpose(1, 0, 2)
            kh = k.reshape(Slen, NH, DH).transpose(1, 0, 2)
            vh = v.reshape(Slen, NH, DH).transpose(1, 0, 2)
            log_f = jax.nn.log_sigmoid(fg)
            cs = jnp.cumsum(log_f, axis=1)
            fg_mat = cs[:, :, None] - cs[:, None, :]
            mask = jnp.tril(jnp.ones((Slen, Slen), dtype=bool))
            log_fg_mat = jnp.where(mask, fg_mat, -jnp.inf)
            log_D = log_fg_mat + ig[:, None, :]
            max_log_D = jnp.max(log_D, axis=-1, keepdims=True)
            D_mat = jnp.exp(log_D - max_log_D)
            qk = jnp.einsum('hsd,htd->hst', qh, kh) / np.sqrt(DH)
            C = qk * D_mat
            normalizer = jnp.maximum(jnp.abs(C.sum(axis=-1, keepdims=True)), jnp.exp(-max_log_D))
            h = jnp.einsum('hst,htd->hsd', C / (normalizer + EPS), vh)
            h = h.transpose(1, 0, 2).reshape(Slen, D)
            mu = h.mean(axis=-1, keepdims=True)
            var = h.var(axis=-1, keepdims=True)
            return (h - mu) / jnp.sqrt(var + LN_EPS) * ln_scale
        return jax.vmap(lambda qq, kk, vv: _mlstm_cell(qq, kk, vv, igate_w, igate_b, fgate_w, fgate_b, ln_scale))(q, k, v)

    def _L0_ffn_ref(x, router_w, experts_bias, w1, w3, w2, sw1, sw3, sw2):
        import jax, jax.numpy as jnp
        import numpy as np
        D, H, E, K, S = (128, 256, 8, 2, 1)
        B, L = (4, 256)
        b, l, d = x.shape
        xf = x.reshape(-1, d)
        sg = jnp.einsum('td,sdh->tsh', xf, sw1)
        su = jnp.einsum('td,sdh->tsh', xf, sw3)
        shared_out = jnp.einsum('tsh,shd->td', jax.nn.silu(sg) * su, sw2)
        logits = xf @ router_w.T + experts_bias
        rw, sel = jax.lax.top_k(logits, K)
        rw = jax.nn.softmax(rw.astype(jnp.float32), axis=-1).astype(x.dtype)
        cw = (jax.nn.one_hot(sel, E, dtype=x.dtype) * rw[..., None]).sum(axis=1)
        g = jnp.einsum('td,edh->teh', xf, w1)
        u = jnp.einsum('td,edh->teh', xf, w3)
        eo = jax.nn.silu(g) * u
        moe_out = jnp.einsum('te,teh,ehd->td', cw, eo, w2)
        return (moe_out + shared_out).reshape(b, l, d)

    def _L1_xattn_ref(query, key, value, Wq, bq, Wk, bk, Wv, bv, Wp, bp):
        import jax, jax.numpy as jnp
        import numpy as np
        B, S, D = (4, 256, 128)
        H = 16
        HD = D // H
        SCALE = float(HD) ** 0.5

        def _split_heads(x):
            b, s, _ = x.shape
            return x.reshape(b, s, H, HD).transpose(0, 2, 1, 3)
        q = _split_heads(query @ Wq.T + bq)
        k = _split_heads(key @ Wk.T + bk)
        v = _split_heads(value @ Wv.T + bv)
        score = jnp.einsum('bhqd,bhkd->bhqk', q, k) * SCALE
        attn = jax.nn.softmax(score, axis=-1)
        out = jnp.einsum('bhqk,bhkd->bhqd', attn, v)
        out = out.transpose(0, 2, 1, 3).reshape(query.shape[0], query.shape[1], D)
        return out @ Wp.T + bp

    def _L1_ffn_ref(inputs, w1, w3, w2):
        import jax, jax.numpy as jnp
        import numpy as np
        D_MODEL = 128
        D_FF = 352
        N_EXPERTS = 8
        B, T, D = inputs.shape
        E = w1.shape[0]
        C = T // E
        x = inputs.reshape(B, E, C, D)
        gate = jnp.einsum('becd,edf->becf', x, w1)
        up = jnp.einsum('becd,edf->becf', x, w3)
        h = jax.nn.silu(gate) * up
        out = jnp.einsum('becf,efd->becd', h, w2)
        return out.reshape(B, T, D)
    x = x + _L0_xattn_ref(_layernorm(x, axis=-1), ctx_1024, ctx_1024, L0_xattn_igate_w, L0_xattn_igate_b, L0_xattn_fgate_w, L0_xattn_fgate_b, L0_xattn_ln_scale)
    x = x + _L0_ffn_ref(_layernorm(x, axis=-1), L0_ffn_router_w, L0_ffn_experts_bias, L0_ffn_w1, L0_ffn_w3, L0_ffn_w2, L0_ffn_sw1, L0_ffn_sw3, L0_ffn_sw2)
    x = x + _L1_xattn_ref(_layernorm(x, axis=-1), ctx_1024, ctx_1024, L1_xattn_Wq, L1_xattn_bq, L1_xattn_Wk, L1_xattn_bk, L1_xattn_Wv, L1_xattn_bv, L1_xattn_Wp, L1_xattn_bp)
    x = x + _L1_ffn_ref(_layernorm(x, axis=-1), L1_ffn_w1, L1_ffn_w3, L1_ffn_w2)
    return x

_drawn_inputs = setup_inputs


def setup_inputs(seed=0):
    import zlib

    import numpy as np

    out = dict(_drawn_inputs(seed))
    spreads = {'L0_xattn_ln_scale': (1.0, 0.2), 'L0_ffn_experts_bias': (0.0, 0.8)}
    factors = {'L0_ffn_router_w': 8.0,
     'L0_ffn_w1': 8.0,
     'L0_ffn_w3': 8.0,
     'L0_ffn_w2': 8.0,
     'L0_ffn_sw1': 8.0,
     'L0_ffn_sw3': 8.0,
     'L0_ffn_sw2': 8.0,
     'L1_xattn_bq': 16.386,
     'L1_xattn_bk': 64.0,
     'L1_xattn_bv': 9.517,
     'L1_ffn_w1': 8.0,
     'L1_ffn_w3': 8.0,
     'L1_ffn_w2': 8.0,
     'L1_xattn_bp': 6.15}
    for name, (base, spread) in spreads.items():
        noise = np.random.default_rng([zlib.crc32(name.encode()), seed]).standard_normal(out[name].shape)
        drawn = base * np.exp(spread * noise) if base else spread * noise
        out[name] = jnp.asarray(drawn.astype(out[name].dtype))
    for name, factor in factors.items():
        out[name] = (out[name] * factor).astype(out[name].dtype)
    return out
```

```python
from contextlib import ExitStack

import numpy as np

import concourse.bass as bass
from concourse import mybir

F32 = mybir.dt.float32
BF16 = mybir.dt.bfloat16
U32 = mybir.dt.uint32
ACT = mybir.ActivationFunctionType
ALU = mybir.AluOpType
AX = mybir.AxisListType

B, S, D = 128, 64, 128
TOKENS = B * S
P = 128
TILES = 4
GROUP = TILES * P
GB = GROUP // S
GROUPS = TOKENS // GROUP
PAIRS = B // 2
LN_EPS = 1e-5

H0 = 8
DH0 = D // H0
VW0 = DH0 + 1
CELL_EPS = 1e-6
NSPLIT = 3
MASKED = -1.0e30
A_ROW = S
M_ROW = A_ROW + NSPLIT * H0
DECAY_ROWS = M_ROW + NSPLIT * 2

E0, HID0 = 8, 256
UNITS0 = E0 + 1
CH0 = HID0 // P

H1 = 16
DH1 = D // H1
SCALE1 = float(DH1) ** 0.5
HP1 = H1 // 2
VW1 = DH1 + 1

ONE = 1

E1, FF1 = 8, 352
C1 = S // E1
CHUNKS1 = [(c * P, min(P, FF1 - c * P)) for c in range((FF1 + P - 1) // P)]


class Steps:

    def __init__(self, eng, sem):
        self.eng, self.sem, self.base, self.n = eng, sem, 0, 0

    def at(self, base):
        self.base, self.n = base, 0

    def __call__(self, ins):
        self.n += 1
        ins.then_inc(self.sem, 1)
        self.eng.wait_ge(self.sem, ONE + self.base + self.n)


class Room:

    def __init__(self, nc, ctx, sems, phase):
        self.nc, self.ctx, self.sems, self.phase, self.all_sems = nc, ctx, sems, phase, []

    def sb(self, name, shape, dt=F32):
        return self.ctx.enter_context(self.nc.sbuf_tensor(f"{self.phase}_{name}", shape, dt))

    def ps(self, name, shape):
        return self.ctx.enter_context(self.nc.psum_tensor(f"{self.phase}_{name}", shape, F32))

    def sem(self, name):
        self.all_sems.append(self.sems.enter_context(self.nc.semaphore(f"{self.phase}_{name}")))
        return self.all_sems[-1]

    def start_at_one(self, sp):
        for sem in self.all_sems:
            sp.sem_inc(sem, ONE)

    def sem2(self, name):
        return [self.sem(f"{name}{k}") for k in range(2)]


def apart(eng):
    eng.nop(nofuse=True)


class LayerNorm:

    def __init__(self, r):
        self.stats, self.mv, self.rstd = r.sb("stats", [P, TILES, 6]), r.sb("mv", [P, TILES, 2]), r.sb("rstd", [P, TILES])
        self.shifted, self.power, self.shifted_done = r.sb("shifted", [P, TILES]), r.sb("power", [P, TILES]), r.sem("shifted_done")
        self.stats_done, self.var_done, self.rstd_done = r.sem("stats_done"), r.sem("var_done"), r.sem("rstd_done")

    def vector(self, v, n, x, y):
        for t in range(TILES):
            ins = v.bn_stats(self.stats[:, t, :], x[:, t, :])
        ins.then_inc(self.stats_done, 1)
        v.wait_ge(self.stats_done, ONE + n + 1)
        apart(v)
        for t in range(TILES):
            ins = v.bn_aggr(self.mv[:, t, :], self.stats[:, t, :])
        ins.then_inc(self.var_done, 1)
        v.wait_ge(self.rstd_done, ONE + n + 1)
        for t in range(TILES):
            ins = v.tensor_scalar(y[:, t, :], x[:, t, :], self.mv[:, t, 0:1], self.rstd[:, t:t + 1], ALU.subtract, ALU.mult)
        return ins

    def power_const(self, pool):
        pool.memset(self.power[:, :], -0.5).then_inc(self.shifted_done, 1)

    def gpsimd(self, pool, n):
        pool.wait_ge(self.var_done, ONE + n + 1)
        apart(pool)
        pool.tensor_scalar(self.shifted[:, :], self.mv[:, :, 1], LN_EPS, None, ALU.add).then_inc(self.shifted_done, 1)
        pool.wait_ge(self.shifted_done, ONE + n + 2)
        pool.tensor_tensor(self.rstd[:, :], self.shifted[:, :], self.power[:, :], ALU.pow).then_inc(self.rstd_done, 1)


def following(j, k):
    return (j, 1) if k == 0 else (j + 1, 0)


def over_groups(eng, step, n=GROUPS):
    with eng.Fori(0, n // 2 - 1) as j:
        step(j, 0, True)
        step(j, 1, True)
    step(n // 2 - 1, 0, True)
    step(n // 2 - 1, 1, False)


def whole(t):
    return t[(slice(None),) * len(t.shape)]


def tiles_of(dram, g):
    return dram[bass.ds(g * GROUP, GROUP), :].rearrange("(t p) d -> p t d", p=P)


def phase_gates(nc, sems, a, s):
    with ExitStack() as ctx:
        r = Room(nc, ctx, sems, "gates")
        ident = r.sb("ident", [P, P])
        wq, wk, wv = (r.sb(n, [D, 2 * H0]) for n in ("wq", "wk", "wv"))
        bias = r.sb("bias", [2 * H0, 1])
        x = [r.sb(f"x{k}", [P, TILES, D]) for k in range(2)]
        ctxT = [r.sb(f"ctxT{k}", [D, GROUP]) for k in range(2)]
        xn = [r.sb(f"xn{k}", [P, TILES, D]) for k in range(2)]
        xnT = [r.sb(f"xnT{k}", [D, GROUP]) for k in range(2)]
        rows = [r.sb(f"rows{k}", [2 * H0, GROUP]) for k in range(2)]
        ln = LayerNorm(r)
        psT = [r.ps(f"psT{k}", [P, GROUP]) for k in range(2)]
        psG = [r.ps(f"psG{k}", [P, GROUP]) for k in range(2)]
        const_in = r.sem("const_in")
        x_in, ctx_in = r.sem2("x_in"), r.sem2("ctx_in")
        xn_done, turned, xnT_done = r.sem2("xn_done"), r.sem2("turned"), r.sem2("xnT_done")
        summed, rows_done, stored = r.sem2("summed"), r.sem2("rows_done"), r.sem2("stored")
        consts = ((ident, "ident"), (wq, "gate_wq"), (wk, "gate_wk"), (wv, "gate_wv"), (bias, "gate_b"))
        block = ctx.enter_context(nc.Block())

        @block.sync
        def _(sp):
            r.start_at_one(sp)
            for dst, src in consts:
                sp.dma_start(dst[:, :], a[src]).then_inc(const_in, 16)
            with sp.Fori(0, GROUPS // 2) as j:
                for k in range(2):
                    g = 2 * j + k
                    sp.wait_ge(xn_done[k], ONE + j)
                    apart(sp)
                    sp.dma_start(x[k][:, :, :], tiles_of(a["x"], g)).then_inc(x_in[k], 16)
                    sp.wait_ge(summed[k], ONE + j)
                    apart(sp)
                    sp.dma_start(ctxT[k][:, :], a["ctxT"][:, bass.ds(g * GROUP, GROUP)]).then_inc(ctx_in[k], 16)

        @block.vector
        def _(v):
            with v.Fori(0, GROUPS // 2) as j:
                for k in range(2):
                    v.wait_ge(x_in[k], ONE + 16 * j + 16)
                    v.wait_ge(turned[k], ONE + j)
                    ln.vector(v, 2 * j + k, x[k], xn[k]).then_inc(xn_done[k], 1)

        @block.tensor
        def _(pe):
            pe.wait_ge(const_in, ONE + 16 * len(consts))
            with pe.Fori(0, GROUPS // 2) as j:
                for k in range(2):
                    pe.wait_ge(xn_done[k], ONE + j + 1)
                    pe.wait_ge(xnT_done[k], ONE + j)
                    for t in range(TILES):
                        ins = pe.transpose(psT[k][:, t * P:(t + 1) * P], xn[k][:, t, :], ident[:, :])
                    ins.then_inc(turned[k], 1)
                    pe.wait_ge(ctx_in[k], ONE + 16 * j + 16)
                    pe.wait_ge(rows_done[k], ONE + j)
                    pe.matmul(psG[k][0:2 * H0, :], wk[:, :], ctxT[k][:, :], start=True, stop=False)
                    pe.matmul(psG[k][0:2 * H0, :], wv[:, :], ctxT[k][:, :], start=False, stop=False)
                    pe.wait_ge(xnT_done[k], ONE + j + 1)
                    pe.matmul(psG[k][0:2 * H0, :], wq[:, :], xnT[k][:, :], start=False, stop=True).then_inc(summed[k], 1)

        @block.scalar
        def _(act):
            act.wait_ge(const_in, ONE + 16 * len(consts))
            with act.Fori(0, GROUPS // 2) as j:
                for k in range(2):
                    g = 2 * j + k
                    act.wait_ge(stored[k], ONE + 32 * j)
                    act.wait_ge(turned[k], ONE + j + 1)
                    act.activation(xnT[k][:, :], psT[k][:, :], ACT.Copy).then_inc(xnT_done[k], 1)
                    act.wait_ge(xnT_done[k], ONE + j + 1)
                    act.dma_start(s["xnT"][:, bass.ds(g * GROUP, GROUP)], xnT[k][:, :]).then_inc(stored[k], 16)
                    act.wait_ge(summed[k], ONE + j + 1)
                    act.activation(rows[k][:, :], psG[k][0:2 * H0, :], ACT.Identity,
                                   bias=bias[:, 0:1]).then_inc(rows_done[k], 1)
                    act.wait_ge(rows_done[k], ONE + j + 1)
                    act.dma_start(s["gates"][bass.ds(g * GB, GB)].rearrange("b h t -> h b t"),
                                  rows[k][:, :].rearrange("h (b t) -> h b t", b=GB)).then_inc(stored[k], 16)
            for k in range(2):
                act.wait_ge(stored[k], ONE + 32 * (GROUPS // 2))

        @block.gpsimd
        def _(pool):
            ln.power_const(pool)
            with pool.Fori(0, GROUPS) as g:
                ln.gpsimd(pool, g)


def phase_decay(nc, sems, a, s):
    N = H0 * S
    with ExitStack() as ctx:
        r = Room(nc, ctx, sems, "decay")
        ident = r.sb("ident", [P, P])
        keep, drop = r.sb("keep", [B, N]), r.sb("drop", [B, N])
        gates = r.sb("gates", [B, 2 * N])
        ig, fg = gates[:, 0:N], gates[:, N:2 * N]
        t1, t2, t3 = (r.sb(n, [B, N]) for n in ("t1", "t2", "t3"))
        logf, cs, am, peak, neg_max, neg_peak = (r.sb(n, [B, N]) for n in ("logf", "cs", "am", "peak", "nmax", "npeak"))
        m_parts = r.sb("m_parts", [B, NSPLIT, N], BF16)
        a_parts = r.sb("a_parts", [B, NSPLIT, N], BF16)
        rest = r.sb("rest", [B, N])
        floor = r.sb("floor", [P, PAIRS, H0])
        psE = r.ps("psE", [P, H0 * PAIRS])
        loaded, dve_step, for_act, act_step = r.sem("loaded"), r.sem("dve_step"), r.sem("for_act"), r.sem("act_step")
        nmax_done, turned, floor_done = r.sem("nmax_done"), r.sem("turned"), r.sem("floor_done")
        parts_done, stored = r.sem("parts_done"), r.sem("stored")
        block = ctx.enter_context(nc.Block())

        @block.sync
        def _(sp):
            r.start_at_one(sp)
            sp.dma_start(gates[:, :], s["gates"].rearrange("b h t -> b (h t)")).then_inc(loaded, 16)
            sp.dma_start(keep[:, :], a["scan_keep"]).then_inc(loaded, 16)
            sp.dma_start(drop[:, :], a["scan_drop"]).then_inc(loaded, 16)
            sp.dma_start(ident[:, :], a["ident"]).then_inc(loaded, 16)
            sp.wait_ge(floor_done, ONE + 1)
            sp.dma_start(s["floor"], floor[:, :, :]).then_inc(stored, 16)
            sp.wait_ge(parts_done, ONE + 2)
            for n in range(NSPLIT):
                sp.dma_start(s["m_parts"][n], m_parts[:, n, :]).then_inc(stored, 16)
                sp.dma_start(s["a_parts"][n].rearrange("b h t -> b (h t)"), a_parts[:, n, :]).then_inc(stored, 16)
            sp.wait_ge(stored, ONE + 16 * (1 + 2 * NSPLIT))

        @block.vector
        def _(v):
            step = Steps(v, dve_step)
            v.wait_ge(loaded, ONE + 64)
            v.scalar_tensor_tensor(out=t1[:, :], in0=fg, scalar=-1.0, in1=fg, op0=ALU.mult, op1=ALU.max).then_inc(for_act, 1)
            v.wait_ge(act_step, ONE + 1)
            v.tensor_scalar(t3[:, :], t2[:, :], 1.0, None, ALU.add).then_inc(for_act, 1)
            v.wait_ge(act_step, ONE + 2)
            step(v.scalar_tensor_tensor(out=logf[:, :], in0=fg, scalar=0.0, in1=t1[:, :], op0=ALU.min, op1=ALU.subtract))
            step(v.tensor_tensor_scan(cs[:, :], keep[:, :], logf[:, :], 0.0, ALU.mult, ALU.add))
            step(v.tensor_tensor(am[:, :], ig, cs[:, :], ALU.subtract))
            step(v.tensor_tensor_scan(peak[:, :], drop[:, :], am[:, :], 0.0, ALU.add, ALU.max))
            step(v.tensor_scalar(neg_peak[:, :], peak[:, :], -1.0, None, ALU.mult))
            v.tensor_tensor(neg_max[:, :], neg_peak[:, :], cs[:, :], ALU.subtract).then_inc(nmax_done, 1)
            for whole, parts in ((neg_peak, m_parts), (am, a_parts)):
                left = whole
                for n in range(NSPLIT):
                    ins = v.tensor_copy(parts[:, n, :], left[:, :])
                    if n == NSPLIT - 1:
                        ins.then_inc(parts_done, 1)
                        v.wait_ge(parts_done, ONE + (1 if parts is m_parts else 2))
                    else:
                        step(ins)
                        step(v.tensor_tensor(rest[:, :], left[:, :], parts[:, n, :], ALU.subtract))
                        left = rest

        @block.scalar
        def _(act):
            act.wait_ge(for_act, ONE + 1)
            act.activation(t2[:, :], t1[:, :], ACT.Exp, scale=-1.0).then_inc(act_step, 1)
            act.wait_ge(for_act, ONE + 2)
            act.activation(t1[:, :], t3[:, :], ACT.Ln).then_inc(act_step, 1)
            act.wait_ge(turned, ONE + 1)
            act.activation(floor[:, :, :], psE[:, :].rearrange("p (h i) -> p i h", h=H0), ACT.Exp).then_inc(floor_done, 1)

        @block.tensor
        def _(pe):
            pe.wait_ge(loaded, ONE + 64)
            pe.wait_ge(nmax_done, ONE + 1)
            for h in range(H0):
                for b2 in range(2):
                    ins = pe.matmul(psE[b2 * S:(b2 + 1) * S, h * PAIRS:(h + 1) * PAIRS], neg_max[:, h * S:(h + 1) * S],
                                    ident[:, b2::2], start=True, stop=True)
            ins.then_inc(turned, 1)


def phase_mlstm(nc, sems, a, s):
    N = H0 * S
    with ExitStack() as ctx:
        r = Room(nc, ctx, sems, "mlstm")
        ln_scale = r.sb("ln_scale", [P, D])
        keysT = [r.sb(f"keysT{k}", [D, GROUP]) for k in range(2)]
        qheads = [r.sb(f"qheads{k}", [D, GB, H0, S]) for k in range(2)]
        vals = [r.sb(f"vals{k}", [P, TILES, H0 * VW0]) for k in range(2)]
        x = [r.sb(f"x{k}", [P, TILES, D]) for k in range(2)]
        floor = [r.sb(f"floor{k}", [P, TILES, H0]) for k in range(2)]
        dk = [r.sb(f"dk{k}", [DECAY_ROWS, GROUP], BF16) for k in range(2)]
        dq = [r.sb(f"dq{k}", [DECAY_ROWS, TILES, N], BF16) for k in range(2)]
        decay = [r.sb(f"decay{k}", [P, N]) for k in range(2)]
        cT = [r.sb(f"cT{k}", [P, N]) for k in range(2)]
        norm, inv = r.sb("norm", [P, TILES, H0]), r.sb("inv", [P, TILES, H0])
        h = r.sb("h", [P, TILES, D])
        y, ys = r.sb("y", [P, TILES, D]), r.sb("ys", [P, TILES, D])
        out = [r.sb(f"out{k}", [P, TILES, D]) for k in range(2)]
        ln = LayerNorm(r)
        psA = [r.ps(f"psA{k}", [P, N]) for k in range(2)]
        psS = [r.ps(f"psS{k}", [P, N]) for k in range(2)]
        psV = [[r.ps(f"psV{k}{i}", [P, 512]) for i in range(2)] for k in range(2)]
        const_in, zeroed = r.sem("const_in"), r.sem("zeroed")
        pe_in, q_in, tail_in = r.sem2("pe_in"), r.sem2("q_in"), r.sem2("tail_in")
        arg_done, qk_done, decay_done, cT_done = (r.sem2(n) for n in ("arg", "qk", "decay", "cT"))
        cT_used = r.sem2("cT_used")
        group_done = r.sem2("group_done")
        h_done, tail_done, stored = (r.sem2(n) for n in ("h_done", "tail", "stored"))
        dve_step = r.sem("dve_step")
        TAIL_STEPS = 6
        block = ctx.enter_context(nc.Block())

        @block.sync
        def _(sp):
            r.start_at_one(sp)
            sp.dma_start(ln_scale[:, :], a["ln_scale"]).then_inc(const_in, 16)
            for k in range(2):
                sp.dma_start(dk[k][:, :], a["decay_keys"].bitcast(BF16)).then_inc(const_in, 16)
                sp.dma_start(dq[k][:, :, :], a["decay_queries"].bitcast(BF16)).then_inc(const_in, 16)
            sp.wait_ge(const_in, ONE + 16 * 5)

            def load(j, k):
                g = 2 * j + k
                sp.wait_ge(group_done[k], ONE + j)
                apart(sp)
                sp.dma_start(keysT[k][:, :], a["ctxT"][:, bass.ds(g * GROUP, GROUP)]).then_inc(pe_in[k], 16)
                for h_ in range(H0):
                    sp.dma_start(qheads[k][h_ * DH0:(h_ + 1) * DH0, :, h_, :],
                                 s["xnT"][h_ * DH0:(h_ + 1) * DH0, bass.ds(g * GROUP, GROUP)].rearrange(
                                     "d (b t) -> d b t", b=GB)).then_inc(q_in[k], 16)
                sp.dma_start(vals[k][:, :, :], a["ctx_ones"][bass.ds(g * GROUP, GROUP), :].rearrange(
                    "(t p) d -> p t d", p=P)).then_inc(pe_in[k], 16)
                for n in range(NSPLIT):
                    sp.dma_start(dk[k][A_ROW + n * H0:A_ROW + (n + 1) * H0, :].rearrange("h (b t) -> h b t", b=GB),
                                 s["a_parts"][n, bass.ds(g * GB, GB)].rearrange("b h t -> h b t")).then_inc(pe_in[k], 16)
                    sp.dma_start(dq[k][M_ROW + 2 * n:M_ROW + 2 * n + 2, :, :],
                                 s["m_parts"][n, bass.ds(g * GB, GB), :].rearrange("(i c) n -> c i n", c=2)).then_inc(pe_in[k], 16)
                sp.wait_ge(tail_done[k], ONE + j)
                apart(sp)
                sp.dma_start(x[k][:, :, :], tiles_of(a["x"], g)).then_inc(tail_in[k], 16)
                sp.dma_start(floor[k][:, :, :], s["floor"][:, bass.ds(g * TILES, TILES), :]).then_inc(tail_in[k], 16)

            def step(j, k, more):
                if more:
                    load(*following(j, k))
                sp.wait_ge(tail_done[k], ONE + j + 1)
                apart(sp)
                sp.dma_start(tiles_of(s["x1"], 2 * j + k), out[k][:, :, :]).then_inc(stored[k], 16)

            sp.wait_ge(zeroed, ONE + 2)
            load(0, 0)
            over_groups(sp, step)
            for k in range(2):
                sp.wait_ge(stored[k], ONE + 16 * (GROUPS // 2))

        @block.gpsimd
        def _(pool):
            for k in range(2):
                pool.memset(qheads[k][:, :, :, :], 0.0).then_inc(zeroed, 1)
            pool.wait_ge(zeroed, ONE + 2)

            ln.power_const(pool)
            with pool.Fori(0, GROUPS) as g:
                ln.gpsimd(pool, g)

        @block.tensor
        def _(pe):
            def scores(g, j, k, i):
                c = i % 2
                n = 2 * g + i // 2
                pe.wait_ge(decay_done[c], ONE + n)
                pe.matmul(psA[c][:, :], dk[k][:, i * P:(i + 1) * P], dq[k][:, i, :], start=True, stop=True).then_inc(arg_done[c], 1)
                pe.wait_ge(cT_done[c], ONE + n)
                for b2 in range(2):
                    b = 2 * i + b2
                    ins = pe.matmul(psS[c][b2 * S:(b2 + 1) * S, :], keysT[k][:, b * S:(b + 1) * S],
                                    qheads[k][:, b, :, :].rearrange("p h t -> p (h t)"), start=True, stop=True)
                ins.then_inc(qk_done[c], 1)

            def values(g, j, k, i):
                c = i % 2
                pe.wait_ge(cT_done[c], ONE + 2 * g + i // 2 + 1)
                apart(pe)
                for h_ in range(H0):
                    for b2 in range(2):
                        at = (i % 2) * H0 * VW0 + h_ * VW0
                        rows = slice(b2 * S, (b2 + 1) * S)
                        ins = pe.matmul(psV[k][i // 2][rows, at:at + VW0], cT[c][rows, h_ * S:(h_ + 1) * S],
                                        vals[k][rows, i, h_ * VW0:(h_ + 1) * VW0], start=True, stop=True)
                ins.then_inc(group_done[k] if i == TILES - 1 else cT_used[c], 1)

            with pe.Fori(0, GROUPS // 2) as j:
                for k in range(2):
                    g = 2 * j + k
                    pe.wait_ge(pe_in[k], ONE + 16 * (2 + 2 * NSPLIT) * (j + 1))
                    pe.wait_ge(q_in[k], ONE + 16 * H0 * (j + 1))
                    scores(g, j, k, 0)
                    scores(g, j, k, 1)
                    pe.wait_ge(h_done[k], ONE + j)
                    values(g, j, k, 0)
                    scores(g, j, k, 2)
                    values(g, j, k, 1)
                    scores(g, j, k, 3)
                    values(g, j, k, 2)
                    values(g, j, k, 3)

        @block.scalar
        def _(act):
            with act.Fori(0, GROUPS // 2) as j:
                for k in range(2):
                    g = 2 * j + k
                    for i in range(TILES):
                        c, n = i % 2, 2 * g + i // 2
                        act.wait_ge(arg_done[c], ONE + n + 1)
                        act.wait_ge(cT_done[c], ONE + n)
                        act.activation(decay[c][:, :], psA[c][:, :], ACT.Exp).then_inc(decay_done[c], 1)

        @block.vector
        def _(v):
            step = Steps(v, dve_step)
            v.wait_ge(const_in, ONE + 16 * 5)
            with v.Fori(0, GROUPS // 2) as j:
                for k in range(2):
                    g = 2 * j + k
                    for i in range(TILES):
                        c, n = i % 2, 2 * g + i // 2
                        v.wait_ge(qk_done[c], ONE + n + 1)
                        v.wait_ge(decay_done[c], ONE + n + 1)
                        if i == 1:
                            v.wait_ge(group_done[1 - k], ONE + j + k)
                        elif i == 3:
                            v.wait_ge(cT_used[1], ONE + g + 1)
                        else:
                            v.wait_ge(cT_used[0], ONE + n)
                        v.scalar_tensor_tensor(out=cT[c][:, :], in0=psS[c][:, :], scalar=float(DH0) ** -0.5,
                                               in1=decay[c][:, :], op0=ALU.mult, op1=ALU.mult).then_inc(cT_done[c], 1)
                    step.at(g * TAIL_STEPS)
                    v.wait_ge(group_done[k], ONE + j + 1)
                    v.wait_ge(tail_in[k], ONE + 32 * (j + 1))
                    hv = [psV[k][i][:, 0:2 * H0 * VW0].rearrange("p (t h w) -> p t h w", t=2, h=H0) for i in range(2)]
                    for i in range(2):
                        ins = v.scalar_tensor_tensor(out=norm[:, 2 * i:2 * i + 2, :], in0=hv[i][:, :, :, DH0], scalar=-1.0,
                                                     in1=floor[k][:, 2 * i:2 * i + 2, :], op0=ALU.mult, op1=ALU.max)
                    step(ins)
                    for i in range(2):
                        ins = v.tensor_tensor(norm[:, 2 * i:2 * i + 2, :], hv[i][:, :, :, DH0], norm[:, 2 * i:2 * i + 2, :], ALU.max)
                    step(ins)
                    step(v.tensor_scalar(norm[:, :, :], norm[:, :, :], CELL_EPS, None, ALU.add))
                    step(v.reciprocal(inv[:, :, :], norm[:, :, :]))
                    for i in range(2):
                        iv = inv[:, 2 * i:2 * i + 2, :].rearrange("p t h -> p (t h)").unsqueeze(2).to_broadcast([P, 2 * H0, DH0])
                        ins = v.tensor_tensor(h[:, 2 * i:2 * i + 2, :].rearrange("p t (h w) -> p (t h) w", h=H0),
                                              psV[k][i][:, 0:2 * H0 * VW0].rearrange("p (h w) -> p h w", w=VW0)[:, :, 0:DH0],
                                              iv, ALU.mult)
                    ins.then_inc(h_done[k], 1)
                    v.wait_ge(h_done[k], ONE + j + 1)
                    step(ln.vector(v, g, h, y))
                    step(v.tensor_tensor(ys[:, :, :], y[:, :, :], ln_scale[:, :].unsqueeze(1).to_broadcast([P, TILES, D]), ALU.mult))
                    v.wait_ge(stored[k], ONE + 16 * j)
                    ins = v.tensor_tensor(out[k][:, :, :], x[k][:, :, :], ys[:, :, :], ALU.add)
                    ins.then_inc(tail_done[k], 1)


def phase_experts(nc, sems, a, s):
    with ExitStack() as ctx:
        r = Room(nc, ctx, sems, "experts")
        ident = r.sb("ident", [P, P])
        router, bias, iota = r.sb("router", [D, E0]), r.sb("bias", [P, E0]), r.sb("iota", [P, E0])
        w1, w3 = r.sb("w1", [D, UNITS0, HID0]), r.sb("w3", [D, UNITS0, HID0])
        w2 = r.sb("w2", [P, UNITS0 * CH0, D])
        x = [r.sb(f"x{k}", [P, TILES, D]) for k in range(2)]
        xn = [r.sb(f"xn{k}", [P, TILES, D]) for k in range(2)]
        xnT = [r.sb(f"xnT{k}", [D, GROUP]) for k in range(2)]
        ln = LayerNorm(r)
        logits, top = r.sb("logits", [P, TILES, E0]), r.sb("top", [P, TILES, 8])
        where, wheref = r.sb("where", [P, TILES, 8], U32), r.sb("wheref", [P, TILES, 8])
        gap, tanh = r.sb("gap", [P, TILES]), r.sb("tanh", [P, TILES])
        share = r.sb("share", [P, 2, TILES])
        pick = r.sb("pick", [P, 2, TILES, E0])
        cw = [r.sb(f"cw{k}", [P, TILES, E0]) for k in range(2)]
        act_g = [r.sb(f"act_g{c}", [P, GROUP]) for c in range(CH0)]
        hT = [[r.sb(f"hT{u}{c}", [P, GROUP]) for c in range(CH0)] for u in range(2)]
        psT, psR = r.ps("psT", [P, GROUP]), r.ps("psR", [P, 512])
        psG = [r.ps(f"psG{c}", [P, GROUP]) for c in range(CH0)]
        psU = [r.ps(f"psU{c}", [P, GROUP]) for c in range(CH0)]
        psY = [r.ps(f"psY{u}", [P, TILES, D]) for u in range(2)]
        const_in = r.sem("const_in")
        x_in, xn_done, turned, xnT_done = r.sem2("x_in"), r.sem2("xn"), r.sem("turned"), r.sem2("xnT")
        routed, gap_done, tanh_done = r.sem("routed"), r.sem("gap"), r.sem("tanh")
        up_done, silu_done, h_done, y_done = r.sem2("up"), r.sem2("silu"), r.sem2("h"), r.sem("y")
        added, stored, xnT_used = r.sem("added"), r.sem2("stored"), r.sem2("xnT_used")
        front_step = r.sem("front_step")
        consts = ((ident, "ident"), (router, "router"), (bias, "router_b"), (iota, "iota"), (w1, "w1"), (w3, "w3"), (w2, "w2"))
        LN_AT, ROUTE_AT = 2, 4
        ROUTE_STEPS = 8
        block = ctx.enter_context(nc.Block())

        @block.sync
        def _(sp):
            r.start_at_one(sp)
            for dst, src in consts:
                sp.dma_start(whole(dst), a[src]).then_inc(const_in, 16)

            def load(j, k):
                sp.wait_ge(stored[k], ONE + 16 * j)
                apart(sp)
                sp.dma_start(x[k][:, :, :], tiles_of(s["x1"], 2 * j + k)).then_inc(x_in[k], 16)

            def step(j, k, more):
                if more:
                    load(*following(j, k))
                sp.wait_ge(added, ONE + (2 * j + k + 1) * UNITS0)
                apart(sp)
                sp.dma_start(tiles_of(s["x2"], 2 * j + k), x[k][:, :, :]).then_inc(stored[k], 16)

            load(0, 0)
            over_groups(sp, step)
            for k in range(2):
                sp.wait_ge(stored[k], ONE + 16 * (GROUPS // 2))

        @block.gpsimd
        def _(pool):
            ln.power_const(pool)
            with pool.Fori(0, GROUPS) as g:
                ln.gpsimd(pool, g)

        @block.tensor
        def _(pe):
            def turn(j, k):
                pe.wait_ge(xn_done[k], ONE + j + 1)
                pe.wait_ge(xnT_done[1 - k], ONE + j + k)
                for t in range(TILES):
                    ins = pe.transpose(psT[:, t * P:(t + 1) * P], xn[k][:, t, :], ident[:, :])
                ins.then_inc(turned, 1)

            def route(j, k):
                pe.wait_ge(xnT_done[k], ONE + j + 1)
                pe.wait_ge(gap_done, ONE + 2 * j + k)
                for t in range(TILES):
                    ins = pe.matmul(psR[:, t * E0:(t + 1) * E0], xnT[k][:, t * P:(t + 1) * P], router[:, :], start=True, stop=True)
                ins.then_inc(routed, 1)

            def up(g, k, e):
                for c in range(CH0):
                    pe.wait_ge(h_done[c], ONE + g * UNITS0 + e)
                    pe.matmul(psG[c][:, :], w1[:, e, c * P:(c + 1) * P], xnT[k][:, :], start=True, stop=True)
                    pe.matmul(psU[c][:, :], w3[:, e, c * P:(c + 1) * P], xnT[k][:, :], start=True, stop=True).then_inc(up_done[c], 1)

            def down(g, k, e):
                n = g * UNITS0 + e
                u = (k * UNITS0 + e) % 2
                for c in range(CH0):
                    pe.wait_ge(h_done[c], ONE + n + 1)
                if e >= 2:
                    pe.wait_ge(added, ONE + n - 1)
                else:
                    pe.wait_ge(added, ONE + g * UNITS0)
                for t in range(TILES):
                    for c in range(CH0):
                        ins = pe.matmul(psY[u][:, t, :], hT[u][c][:, t * P:(t + 1) * P], w2[:, e * CH0 + c, :],
                                        start=(c == 0), stop=(c == CH0 - 1))
                ins.then_inc(y_done, 1)

            def step(j, k, more):
                g = 2 * j + k
                for e in range(UNITS0):
                    up(g, k, e)
                    if e:
                        down(g, k, e - 1)
                    if more and e == LN_AT:
                        turn(*following(j, k))
                    if more and e == ROUTE_AT:
                        route(*following(j, k))
                down(g, k, UNITS0 - 1)

            pe.wait_ge(const_in, ONE + 16 * len(consts))
            turn(0, 0)
            route(0, 0)
            over_groups(pe, step)

        @block.scalar
        def _(act):
            def xnT_out(j, k):
                act.wait_ge(turned, ONE + 2 * j + k + 1)
                act.wait_ge(stored[k], ONE + 16 * j)
                act.activation(xnT[k][:, :], psT[:, :], ACT.Copy).then_inc(xnT_done[k], 1)

            def tanh_of_gap(j, k):
                act.wait_ge(gap_done, ONE + 2 * j + k + 1)
                act.activation(tanh[:, :], gap[:, :], ACT.Tanh, scale=0.5).then_inc(tanh_done, 1)

            def step(j, k, more):
                g = 2 * j + k
                for e in range(UNITS0):
                    for c in range(CH0):
                        act.wait_ge(up_done[c], ONE + g * UNITS0 + e + 1)
                        act.wait_ge(h_done[c], ONE + g * UNITS0 + e)
                        act.activation(act_g[c][:, :], psG[c][:, :], ACT.Silu).then_inc(silu_done[c], 1)
                    if more and e == LN_AT:
                        xnT_out(*following(j, k))
                    if more and e == ROUTE_AT:
                        tanh_of_gap(*following(j, k))

            xnT_out(0, 0)
            tanh_of_gap(0, 0)
            over_groups(act, step)

        @block.vector
        def _(v):
            step_ = Steps(v, front_step)

            def norm(j, k):
                v.wait_ge(x_in[k], ONE + 16 * (j + 1))
                ln.vector(v, 2 * j + k, x[k], xn[k]).then_inc(xn_done[k], 1)

            def gap_of(j, k):
                step_.at((2 * j + k) * ROUTE_STEPS)
                v.wait_ge(routed, ONE + 2 * j + k + 1)
                step_(v.tensor_tensor(logits[:, :, :], psR[:, 0:TILES * E0].rearrange("p (t e) -> p t e", t=TILES),
                                      bias[:, :].unsqueeze(1).to_broadcast([P, TILES, E0]), ALU.add))
                apart(v)
                for t in range(TILES):
                    ins = v.max(top[:, t, :], logits[:, t, :])
                step_(ins)
                v.tensor_tensor(gap[:, :], top[:, :, 0], top[:, :, 1], ALU.subtract).then_inc(gap_done, 1)
                for t in range(TILES):
                    ins = v.max_index(where[:, t, :], top[:, t, :], logits[:, t, :])
                step_(ins)
                step_(v.tensor_copy(wheref[:, :, :], where[:, :, :]))

            def weights(j, k):
                v.wait_ge(tanh_done, ONE + 2 * j + k + 1)
                step_(v.tensor_scalar(share[:, 0, :], tanh[:, :], 0.5, 0.5, ALU.mult, ALU.add))
                step_(v.tensor_scalar(share[:, 1, :], tanh[:, :], -0.5, 0.5, ALU.mult, ALU.add))
                for n in range(2):
                    for t in range(TILES):
                        ins = v.tensor_scalar(pick[:, n, t, :], iota[:, :], wheref[:, t, n:n + 1], share[:, n, t:t + 1],
                                              ALU.is_equal, ALU.mult)
                step_(ins)
                step_(v.tensor_tensor(cw[k][:, :, :], pick[:, 0, :, :], pick[:, 1, :, :], ALU.add))

            def gated(g, k, e):
                for c in range(CH0):
                    u = (k * UNITS0 + e) % 2
                    n = g * UNITS0 + e
                    v.wait_ge(silu_done[c], ONE + n + 1)
                    v.wait_ge(y_done, ONE + (n - 1 if e >= 1 else g * UNITS0))
                    v.tensor_tensor(hT[u][c][:, :], act_g[c][:, :], psU[c][:, :], ALU.mult).then_inc(h_done[c], 1)

            def add(g, k, e):
                n = g * UNITS0 + e
                u = (k * UNITS0 + e) % 2
                v.wait_ge(y_done, ONE + n + 1)
                v.wait_ge(added, ONE + n)
                if e == E0:
                    ins = v.tensor_tensor(x[k][:, :, :], psY[u][:, :, :], x[k][:, :, :], ALU.add)
                else:
                    for t in range(TILES):
                        ins = v.scalar_tensor_tensor(out=x[k][:, t, :], in0=psY[u][:, t, :], scalar=cw[k][:, t, e:e + 1],
                                                     in1=x[k][:, t, :], op0=ALU.mult, op1=ALU.add)
                ins.then_inc(added, 1)

            def step(j, k, more):
                g = 2 * j + k
                for e in range(UNITS0):
                    gated(g, k, e)
                    if e:
                        add(g, k, e - 1)
                    if more and e == LN_AT - 1:
                        norm(*following(j, k))
                    if more and e == ROUTE_AT:
                        gap_of(*following(j, k))
                    if more and e == ROUTE_AT + 1:
                        weights(*following(j, k))
                add(g, k, UNITS0 - 1)

            v.wait_ge(const_in, ONE + 16 * len(consts))
            norm(0, 0)
            gap_of(0, 0)
            weights(0, 0)
            over_groups(v, step)


def phase_attention(nc, sems, a, s):
    FRONT, TAIL = 5, 2
    NS = H1 * S
    with ExitStack() as ctx:
        r = Room(nc, ctx, sems, "attn")
        ident = r.sb("ident", [P, P])
        wq, wk, wv, wp = (r.sb(n, [D, D]) for n in ("wq", "wk", "wv", "wp"))
        bq, bk = r.sb("bq", [D, 1]), r.sb("bk", [D, 1])
        bv, bp = r.sb("bv", [P, D]), r.sb("bp", [P, D])
        x = [r.sb(f"x{k}", [P, TILES, D]) for k in range(2)]
        xb = [r.sb(f"xb{k}", [P, TILES, D]) for k in range(2)]
        ctxT = [r.sb(f"ctxT{k}", [D, GROUP]) for k in range(2)]
        xn, xnT = r.sb("xn", [P, TILES, D]), r.sb("xnT", [D, GROUP])
        ln = LayerNorm(r)
        qT = [r.sb(f"qT{k}", [D, GROUP]) for k in range(2)]
        kT = r.sb("kT", [D, GROUP])
        kheads = [r.sb(f"kheads{k}", [D, GB, H1, S]) for k in range(2)]
        vheads = [r.sb(f"vheads{k}", [P, GB, HP1, 2, VW1]) for k in range(2)]
        peak = [r.sb(f"peak{c}", [P, H1]) for c in range(2)]
        low = [r.sb(f"low{c}", [P, NS]) for c in range(2)]
        prob = [r.sb(f"prob{c}", [P, NS]) for c in range(2)]
        probT = [r.sb(f"probT{c}", [P, HP1, P]) for c in range(2)]
        inv = [r.sb(f"inv{c}", [P, H1]) for c in range(2)]
        heads, headsT = r.sb("heads", [P, TILES, D]), r.sb("headsT", [P, GROUP])
        out = [r.sb(f"out{k}", [P, TILES, D]) for k in range(2)]
        psS = [r.ps(f"psS{c}", [P, NS]) for c in range(2)]
        psP = [r.ps(f"psP{n}", [P, 4, P]) for n in range(2)]
        psO, psM = r.ps("psO", [P, 512]), r.ps("psM", [P, 512])
        const_in, blank, xb_done = r.sem("const_in"), r.sem("blank"), r.sem2("xb")
        x_in, ctx_in, xn_done, q_done, k_done, kheads_in, v_done = (
            r.sem2(n) for n in ("x_in", "ctx_in", "xn", "q", "k", "kheads", "v"))
        psM_full, xnT_done, headsT_done = r.sem("psM_full"), r.sem("xnT"), r.sem("headsT")
        scores_end = r.sem2("scores_end")
        scores_done, low_done, prob_done, turned = (r.sem2(n) for n in ("scores", "low", "prob", "turned"))
        probT_act, probT_dve, values_done, heads_done = (r.sem(n) for n in ("probT_act", "probT_dve", "values", "heads"))
        out_done, stored, peak_step = r.sem2("out"), r.sem2("stored"), r.sem("peak_step")
        consts = ((ident, "ident"), (wq, "wq"), (wk, "wk"), (wv, "wv"), (wp, "wp"), (bq, "bq"), (bk, "bk"), (bv, "bv"), (bp, "bp"))
        block = ctx.enter_context(nc.Block())

        def used(g):
            return FRONT + g * (FRONT + TAIL)

        @block.sync
        def _(sp):
            r.start_at_one(sp)
            for dst, src in consts:
                sp.dma_start(whole(dst), a[src]).then_inc(const_in, 16)

            def load(j, k):
                g = 2 * j + k
                sp.wait_ge(stored[k], ONE + 16 * GB * j)
                apart(sp)
                sp.dma_start(x[k][:, :, :], tiles_of(s["x2"], g)).then_inc(x_in[k], 16)
                sp.wait_ge(v_done[k], ONE + 2 * j)
                apart(sp)
                sp.dma_start(ctxT[k][:, :], a["ctxT"][:, bass.ds(g * GROUP, GROUP)]).then_inc(ctx_in[k], 16)

            def spread_keys(j, k):
                sp.wait_ge(k_done[k], ONE + j + 1)
                apart(sp)
                sp.wait_ge(scores_end[k], ONE + j)
                apart(sp)
                for h in range(H1):
                    sp.dma_start(kheads[k][h * DH1:(h + 1) * DH1, :, h, :],
                                 kT[h * DH1:(h + 1) * DH1, :].rearrange("d (b t) -> d b t", b=GB)).then_inc(kheads_in[k], 16)

            def step(j, k, more):
                if more:
                    load(*following(j, k))
                    spread_keys(*following(j, k))
                g = 2 * j + k
                sp.wait_ge(out_done[k], ONE + j + 1)
                apart(sp)
                rows = s["x3"].rearrange("(e b c) d -> b e c d", e=E1, b=B)
                for b in range(GB):
                    i, b2 = b // 2, b % 2
                    sp.dma_start(rows[bass.ds(g * GB + b, 1)].rearrange("b e c d -> (b e) c d"),
                                 out[k][b2 * S:(b2 + 1) * S, i, :]).then_inc(stored[k], 16)

            load(0, 0)
            sp.wait_ge(blank, ONE + 8)
            spread_keys(0, 0)
            over_groups(sp, step)
            for k in range(2):
                sp.wait_ge(stored[k], ONE + 16 * GB * (GROUPS // 2))

        @block.gpsimd
        def _(pool):
            def front(j, k):
                ln.gpsimd(pool, 2 * j + k)
                pool.wait_ge(x_in[k], ONE + 16 * (j + 1))
                pool.wait_ge(stored[k], ONE + 16 * GB * j)
                pool.tensor_tensor(xb[k][:, :, :], x[k][:, :, :], bp[:, :].unsqueeze(1).to_broadcast([P, TILES, D]),
                                   ALU.add).then_inc(xb_done[k], 1)

            def step(j, k, more):
                if more:
                    front(*following(j, k))

            ln.power_const(pool)
            for k in range(2):
                pool.memset(kheads[k][:, :, :, :], 0.0).then_inc(blank, 1)
                pool.memset(vheads[k][:, :, :, :, :], 0.0).then_inc(blank, 1)
            pool.wait_ge(blank, ONE + 4)
            for k in range(2):
                for n in range(2):
                    pool.memset(vheads[k][n * S:(n + 1) * S, :, :, n, DH1:VW1], 1.0).then_inc(blank, 1)
                    pool.wait_ge(blank, ONE + 5 + 2 * k + n)
            pool.wait_ge(const_in, ONE + 16 * len(consts))
            front(0, 0)
            over_groups(pool, step)

        @block.tensor
        def _(pe):
            def turn(j, k):
                pe.wait_ge(xn_done[k], ONE + j + 1)
                pe.wait_ge(out_done[k], ONE + j)
                for t in range(TILES):
                    ins = pe.transpose(psM[:, t * P:(t + 1) * P], xn[:, t, :], ident[:, :])
                ins.then_inc(psM_full, 1)

            def q_and_k(j, k):
                pe.wait_ge(xnT_done, ONE + 2 * j + k + 1)
                pe.matmul(psM[:, :], wq[:, :], xnT[:, :], start=True, stop=True).then_inc(psM_full, 1)
                pe.wait_ge(ctx_in[k], ONE + 16 * (j + 1))
                pe.wait_ge(q_done[k], ONE + j + 1)
                pe.matmul(psM[:, :], wk[:, :], ctxT[k][:, :], start=True, stop=True).then_inc(psM_full, 1)

            def v(j, k):
                pe.wait_ge(k_done[k], ONE + j + 1)
                for n in range(2):
                    pe.wait_ge(v_done[k], ONE + 2 * j + n)
                    for b in range(4):
                        rows = ctxT[k][:, (4 * n + b) * S:(4 * n + b + 1) * S]
                        for half in range(2):
                            ins = pe.matmul(psM[half * S:(half + 1) * S, b * D:(b + 1) * D], rows, wv[:, :], start=True, stop=True)
                    ins.then_inc(psM_full, 1)

            def scores(g, k, i):
                c, n = i % 2, 2 * g + i // 2
                pe.wait_ge(low_done[c], ONE + n)
                for h in range(2):
                    for b2 in range(2):
                        b = 2 * i + b2
                        ins = pe.matmul(psS[c][b2 * S:(b2 + 1) * S, h * 512:(h + 1) * 512], qT[k][:, b * S:(b + 1) * S],
                                        kheads[k][:, b, h * HP1:(h + 1) * HP1, :].rearrange("p h t -> p (h t)"), start=True, stop=True)
                ins.then_inc(scores_end[k] if i == TILES - 1 else scores_done[c], 1)

            def turn_prob(g, k, i):
                c, n = i % 2, 2 * g + i // 2
                pe.wait_ge(prob_done[c], ONE + n + 1)
                pe.wait_ge(probT_act, ONE + 4 * g + i)
                pe.wait_ge(probT_dve, ONE + 4 * g + i)
                for m in range(HP1):
                    ins = pe.transpose(psP[m // 4][:, m % 4, :], prob[c][:, m * P:(m + 1) * P], ident[:, :])
                ins.then_inc(turned[c], 1)

            def values(g, k, i):
                c = i % 2
                pe.wait_ge(probT_act, ONE + 4 * g + i + 1)
                pe.wait_ge(probT_dve, ONE + 4 * g + i + 1)
                pe.wait_ge(heads_done, ONE + 4 * g + i)
                for m in range(HP1):
                    for b2 in range(2):
                        ins = pe.matmul(psO[b2 * S:(b2 + 1) * S, m * 2 * VW1:(m + 1) * 2 * VW1], probT[c][:, m, b2 * S:(b2 + 1) * S],
                                        vheads[k][:, 2 * i + b2, m, :, :].rearrange("p n w -> p (n w)"), start=True, stop=True)
                ins.then_inc(values_done, 1)

            def project(j, k, more):
                g = 2 * j + k
                pe.wait_ge(heads_done, ONE + 4 * g + 4)
                if more:
                    nj, nk = following(j, k)
                    pe.wait_ge(v_done[nk], ONE + 2 * (nj + 1))
                else:
                    pe.wait_ge(out_done[1 - k], ONE + j + k)
                for t in range(TILES):
                    ins = pe.transpose(psM[:, t * P:(t + 1) * P], heads[:, t, :], ident[:, :])
                ins.then_inc(psM_full, 1)
                pe.wait_ge(headsT_done, ONE + g + 1)
                for t in range(TILES):
                    ins = pe.matmul(psM[:, t * D:(t + 1) * D], headsT[:, t * P:(t + 1) * P], wp[:, :], start=True, stop=True)
                ins.then_inc(psM_full, 1)

            def step(j, k, more):
                g = 2 * j + k
                nxt = following(j, k)
                pe.wait_ge(kheads_in[k], ONE + 16 * H1 * (j + 1))
                pe.wait_ge(q_done[k], ONE + j + 1)
                pe.wait_ge(v_done[k], ONE + 2 * (j + 1))
                scores(g, k, 0)
                scores(g, k, 1)
                if more:
                    turn(*nxt)
                turn_prob(g, k, 0)
                scores(g, k, 2)
                values(g, k, 0)
                if more:
                    q_and_k(*nxt)
                turn_prob(g, k, 1)
                scores(g, k, 3)
                values(g, k, 1)
                if more:
                    v(*nxt)
                turn_prob(g, k, 2)
                values(g, k, 2)
                turn_prob(g, k, 3)
                values(g, k, 3)
                project(j, k, more)

            pe.wait_ge(const_in, ONE + 16 * len(consts))
            pe.wait_ge(blank, ONE + 8)
            turn(0, 0)
            q_and_k(0, 0)
            v(0, 0)
            over_groups(pe, step)

        @block.scalar
        def _(act):
            def xnT_out(at):
                act.wait_ge(psM_full, ONE + at + 1)
                act.activation(xnT[:, :], psM[:, :], ACT.Copy).then_inc(xnT_done, 1)

            def k_out(j, k, at):
                act.wait_ge(psM_full, ONE + at + 3)
                act.wait_ge(kheads_in[1 - k], ONE + 16 * H1 * (j + k))
                act.activation(kT[:, :], psM[:, :], ACT.Identity, bias=bk[:, 0:1]).then_inc(k_done[k], 1)

            def probs(g, i):
                c, n = i % 2, 2 * g + i // 2
                act.wait_ge(low_done[c], ONE + n + 1)
                act.wait_ge(turned[c], ONE + n)
                act.activation(prob[c][:, :], low[c][:, :], ACT.Exp).then_inc(prob_done[c], 1)

            def probT_out(g, i):
                c, n = i % 2, 2 * g + i // 2
                act.wait_ge(turned[c], ONE + n + 1)
                act.wait_ge(values_done, ONE + 4 * g + max(i - 1, 0))
                act.activation(probT[c][:, 0:4, :], psP[0][:, :, :], ACT.Copy).then_inc(probT_act, 1)

            def headsT_out(at):
                act.wait_ge(psM_full, ONE + at + 1)
                act.activation(headsT[:, :], psM[:, :], ACT.Copy).then_inc(headsT_done, 1)

            def step(j, k, more):
                g = 2 * j + k
                at = used(g)
                probs(g, 0)
                if more:
                    xnT_out(at)
                probs(g, 1)
                probT_out(g, 0)
                if more:
                    k_out(*following(j, k), at)
                probs(g, 2)
                probT_out(g, 1)
                probs(g, 3)
                probT_out(g, 2)
                probT_out(g, 3)
                headsT_out(at + FRONT if more else at)

            act.wait_ge(const_in, ONE + 16 * len(consts))
            xnT_out(0)
            k_out(0, 0, 0)
            over_groups(act, step)

        @block.vector
        def _(v):
            top = Steps(v, peak_step)

            def norm(j, k):
                v.wait_ge(x_in[k], ONE + 16 * (j + 1))
                ln.vector(v, 2 * j + k, x[k], xn).then_inc(xn_done[k], 1)

            def q_out(j, k, at):
                v.wait_ge(psM_full, ONE + at + 2)
                v.tensor_scalar(qT[k][:, :], psM[:, :], bq[:, 0:1], SCALE1, ALU.add, ALU.mult).then_inc(q_done[k], 1)

            def v_out(j, k, at, n):
                v.wait_ge(psM_full, ONE + at + 4 + n)
                for half in range(2):
                    rows = slice(half * S, (half + 1) * S)
                    src = psM[rows, :].rearrange("p (b m n w) -> p b m n w", b=4, m=HP1, n=2)[:, :, :, half, :]
                    b_ = bv[rows, :].rearrange("p (m n w) -> p m n w", m=HP1, n=2)[:, :, half, :]
                    ins = v.tensor_tensor(vheads[k][rows, 4 * n:4 * n + 4, :, half, 0:DH1], src,
                                          b_.unsqueeze(1).to_broadcast([S, 4, HP1, DH1]), ALU.add)
                ins.then_inc(v_done[k], 1)

            def lower(j, k, g, i):
                c, n = i % 2, 2 * g + i // 2
                sc = psS[c][:, :].rearrange("p (h t) -> p h t", h=H1)
                if i == TILES - 1:
                    v.wait_ge(scores_end[k], ONE + j + 1)
                else:
                    v.wait_ge(scores_done[c], ONE + (g + 1 if c else n + 1))
                top(v.tensor_reduce(peak[c][:, :], sc, AX.X, ALU.max))
                v.wait_ge(prob_done[c], ONE + n)
                v.tensor_tensor(low[c][:, :].rearrange("p (h t) -> p h t", h=H1), sc,
                                peak[c][:, :].unsqueeze(2).to_broadcast([P, H1, S]), ALU.subtract).then_inc(low_done[c], 1)

            def probT_out(g, i):
                c, n = i % 2, 2 * g + i // 2
                v.wait_ge(turned[c], ONE + n + 1)
                v.tensor_copy(probT[c][:, 4:8, :], psP[1][:, :, :]).then_inc(probT_dve, 1)

            def heads_out(g, i):
                v.wait_ge(values_done, ONE + 4 * g + i + 1)
                o = psO[:, 0:H1 * VW1].rearrange("p (h w) -> p h w", w=VW1)
                top(v.reciprocal(inv[i % 2][:, :], o[:, :, DH1]))
                v.tensor_tensor(heads[:, i, :].rearrange("p (h w) -> p h w", w=DH1), o[:, :, 0:DH1],
                                inv[i % 2][:, :].unsqueeze(2).to_broadcast([P, H1, DH1]), ALU.mult).then_inc(heads_done, 1)

            def out_(j, k, at):
                v.wait_ge(psM_full, ONE + at + 2)
                v.wait_ge(xb_done[k], ONE + j + 1)
                v.wait_ge(stored[k], ONE + 16 * GB * j)
                v.tensor_tensor(out[k][:, :, :], psM[:, :].rearrange("p (t d) -> p t d", t=TILES), xb[k][:, :, :],
                                ALU.add).then_inc(out_done[k], 1)

            def step(j, k, more):
                g = 2 * j + k
                at, nxt = used(g), following(j, k)
                top.at(g * 2 * TILES)
                if more:
                    norm(*nxt)
                lower(j, k, g, 0)
                lower(j, k, g, 1)
                probT_out(g, 0)
                lower(j, k, g, 2)
                if more:
                    q_out(*nxt, at)
                heads_out(g, 0)
                probT_out(g, 1)
                lower(j, k, g, 3)
                heads_out(g, 1)
                if more:
                    v_out(*nxt, at, 0)
                    v_out(*nxt, at, 1)
                probT_out(g, 2)
                heads_out(g, 2)
                probT_out(g, 3)
                heads_out(g, 3)
                out_(j, k, at + FRONT if more else at)

            v.wait_ge(const_in, ONE + 16 * len(consts))
            v.wait_ge(blank, ONE + 8)
            norm(0, 0)
            q_out(0, 0, 0)
            v_out(0, 0, 0, 0)
            v_out(0, 0, 0, 1)
            over_groups(v, step)


def phase_ffn(nc, sems, a, s):
    UNITS = 2 * E1
    NC = len(CHUNKS1)
    with ExitStack() as ctx:
        r = Room(nc, ctx, sems, "ffn")
        ident = r.sb("ident", [P, P])
        w1 = [r.sb(f"w1{w}", [D, FF1]) for w in range(2)]
        w3 = [r.sb(f"w3{w}", [D, FF1]) for w in range(2)]
        w2 = [r.sb(f"w2{w}", [P, NC, D]) for w in range(2)]
        x = [r.sb(f"x{k}", [P, TILES, D]) for k in range(2)]
        out = [r.sb(f"out{k}", [P, TILES, D]) for k in range(2)]
        xn, xnT = r.sb("xn", [P, TILES, D]), [r.sb(f"xnT{k}", [D, GROUP]) for k in range(2)]
        ln = LayerNorm(r)
        act_g = [r.sb(f"act_g{c}", [P, GROUP]) for c in range(2)]
        hT = [[r.sb(f"hT{k}{c}", [P, GROUP]) for c in range(NC)] for k in range(2)]
        psT = r.ps("psT", [P, GROUP])
        psG = [r.ps(f"psG{c}", [P, GROUP]) for c in range(2)]
        psU = [r.ps(f"psU{c}", [P, GROUP]) for c in range(2)]
        psY = [r.ps(f"psY{k}", [P, TILES, D]) for k in range(2)]
        const_in, w_in, x_in = r.sem("const_in"), r.sem2("w_in"), r.sem2("x_in")
        xn_done, turned, xnT_done = r.sem2("xn"), r.sem("turned"), r.sem2("xnT")
        up_done, silu_done, h_done = r.sem("up"), r.sem("silu"), r.sem("h")
        y_done, out_done, stored = r.sem2("y"), r.sem2("out"), r.sem2("stored")
        block = ctx.enter_context(nc.Block())

        def following_unit(j, q):
            return (j, q + 1) if q < 3 else (j + 1, 0)

        def over_units(eng, step):
            with eng.Fori(0, UNITS // 4 - 1) as j:
                for q in range(4):
                    step(j, q, True)
            for q in range(4):
                step(UNITS // 4 - 1, q, q < 3)

        @block.sync
        def _(sp):
            r.start_at_one(sp)
            sp.dma_start(ident[:, :], a["ident"]).then_inc(const_in, 16)

            def load(j, q):
                k = q % 2
                sp.wait_ge(out_done[k], ONE + 2 * j + q // 2)
                apart(sp)
                sp.dma_start(x[k][:, :, :], tiles_of(s["x3"], 4 * j + q)).then_inc(x_in[k], 16)
                if k == 0:
                    w = q // 2
                    e = 2 * j + w
                    sp.dma_start(w1[w][:, :], a["f1"][bass.ds(e, 1)].rearrange("e d f -> (e d) f")).then_inc(w_in[w], 16)
                    sp.dma_start(w3[w][:, :], a["f3"][bass.ds(e, 1)].rearrange("e d f -> (e d) f")).then_inc(w_in[w], 16)
                    sp.dma_start(w2[w][:, :, :], a["f2"][bass.ds(e, 1)].rearrange("e p c d -> (e p) c d")).then_inc(w_in[w], 16)

            def step(j, q, more):
                if more:
                    load(*following_unit(j, q))
                k = q % 2
                sp.wait_ge(out_done[k], ONE + 2 * j + q // 2 + 1)
                apart(sp)
                sp.dma_start(tiles_of(s["out"], 4 * j + q), out[k][:, :, :]).then_inc(stored[k], 16)

            load(0, 0)
            over_units(sp, step)
            for k in range(2):
                sp.wait_ge(stored[k], ONE + 16 * (UNITS // 2))

        @block.gpsimd
        def _(pool):
            ln.power_const(pool)
            with pool.Fori(0, UNITS) as u:
                ln.gpsimd(pool, u)

        @block.tensor
        def _(pe):
            def turn(j, q):
                k, m = q % 2, 2 * j + q // 2
                pe.wait_ge(xn_done[k], ONE + m + 1)
                pe.wait_ge(xnT_done[1 - k], ONE + m + k)
                for t in range(TILES):
                    ins = pe.transpose(psT[:, t * P:(t + 1) * P], xn[:, t, :], ident[:, :])
                ins.then_inc(turned, 1)

            def up(j, q, c):
                u, k, w = 4 * j + q, q % 2, q // 2
                g = (NC * q + c) % 2
                f, m = CHUNKS1[c]
                pe.wait_ge(h_done, ONE + NC * u + max(c - 1, 0))
                pe.matmul(psG[g][0:m, :], w1[w][:, f:f + m], xnT[k][:, :], start=True, stop=True)
                pe.matmul(psU[g][0:m, :], w3[w][:, f:f + m], xnT[k][:, :], start=True, stop=True).then_inc(up_done, 1)

            def step(j, q, more):
                u, k, w = 4 * j + q, q % 2, q // 2
                pe.wait_ge(w_in[w], ONE + 48 * (j + 1))
                pe.wait_ge(xnT_done[k], ONE + 2 * j + q // 2 + 1)
                up(j, q, 0)
                up(j, q, 1)
                if more:
                    turn(*following_unit(j, q))
                up(j, q, 2)
                pe.wait_ge(h_done, ONE + NC * (u + 1))
                pe.wait_ge(out_done[k], ONE + 2 * j + q // 2)
                for t in range(TILES):
                    for c, (f, m) in enumerate(CHUNKS1):
                        ins = pe.matmul(psY[k][:, t, :], hT[k][c][0:m, t * P:(t + 1) * P], w2[w][0:m, c, :],
                                        start=(c == 0), stop=(c == NC - 1))
                ins.then_inc(y_done[k], 1)

            pe.wait_ge(const_in, ONE + 16)
            turn(0, 0)
            over_units(pe, step)

        @block.scalar
        def _(act):
            def xnT_out(j, q):
                k, m = q % 2, 2 * j + q // 2
                act.wait_ge(turned, ONE + 4 * j + q + 1)
                act.wait_ge(out_done[k], ONE + m)
                act.activation(xnT[k][:, :], psT[:, :], ACT.Copy).then_inc(xnT_done[k], 1)

            def step(j, q, more):
                u = 4 * j + q
                for c, (f, m) in enumerate(CHUNKS1):
                    g = (NC * q + c) % 2
                    act.wait_ge(up_done, ONE + NC * u + c + 1)
                    act.wait_ge(h_done, ONE + NC * u + max(c - 1, 0))
                    act.activation(act_g[g][0:m, :], psG[g][0:m, :], ACT.Silu).then_inc(silu_done, 1)
                    if more and c == 1:
                        xnT_out(*following_unit(j, q))

            xnT_out(0, 0)
            over_units(act, step)

        @block.vector
        def _(v):
            def norm(j, q):
                k, m = q % 2, 2 * j + q // 2
                v.wait_ge(x_in[k], ONE + 16 * (m + 1))
                ln.vector(v, 4 * j + q, x[k], xn).then_inc(xn_done[k], 1)

            def step(j, q, more):
                u, k, n = 4 * j + q, q % 2, 2 * j + q // 2
                if more:
                    v.wait_ge(xnT_done[k], ONE + n + 1)
                    norm(*following_unit(j, q))
                v.wait_ge(y_done[k], ONE + n)
                for c, (f, m) in enumerate(CHUNKS1):
                    g = (NC * q + c) % 2
                    v.wait_ge(silu_done, ONE + NC * u + c + 1)
                    v.tensor_tensor(hT[k][c][0:m, :], act_g[g][0:m, :], psU[g][0:m, :], ALU.mult).then_inc(h_done, 1)
                v.wait_ge(y_done[k], ONE + n + 1)
                v.wait_ge(stored[k], ONE + 16 * n)
                v.tensor_tensor(out[k][:, :, :], psY[k][:, :, :], x[k][:, :, :], ALU.add).then_inc(out_done[k], 1)

            norm(0, 0)
            over_units(v, step)


SCRATCH = {
    "xnT": ([D, TOKENS], F32),
    "gates": ([B, 2 * H0, S], F32),
    "floor": ([P, PAIRS, H0], F32),
    "m_parts": ([NSPLIT, B, H0 * S], BF16),
    "a_parts": ([NSPLIT, B, H0, S], BF16),
    "x1": ([TOKENS, D], F32),
    "x2": ([TOKENS, D], F32),
    "x3": ([TOKENS, D], F32),
}


def build(nc, a, out):
    s = {n: nc.dram_tensor(f"scratch_{n}", shape, dt).ap() for n, (shape, dt) in SCRATCH.items()}
    s["out"] = out
    with ExitStack() as sems:
        phase_gates(nc, sems, a, s)
        phase_decay(nc, sems, a, s)
        phase_mlstm(nc, sems, a, s)
        phase_experts(nc, sems, a, s)
        phase_attention(nc, sems, a, s)
        phase_ffn(nc, sems, a, s)


def bf16_bits(constant):
    return (constant.view(np.uint32) >> 16).astype(np.uint16)


def layouts(i):
    i = {n: np.asarray(v) for n, v in i.items()}
    ctx = i["ctx_1024"].reshape(TOKENS, D)
    rows = lambda v: np.broadcast_to(v, (P, v.shape[0]))
    gates = [i["L0_xattn_igate_w"], i["L0_xattn_fgate_w"]]
    gate = lambda n: np.concatenate([w[:, n * D:(n + 1) * D].T for w in gates], 1)
    units = lambda w, sw: np.concatenate([i[w], i[sw]], 0)
    ones = np.ones((TOKENS, H0, 1), np.float32)
    t = np.arange(S)
    head_of = np.repeat(np.arange(H0), S)
    keys = np.zeros((DECAY_ROWS, GROUP), np.float32)
    keys[0:S] = np.tile(np.eye(S), (1, GB))
    keys[M_ROW:] = np.tile(np.repeat(np.eye(2), S, 1), (NSPLIT, TILES))
    queries = np.zeros((DECAY_ROWS, TILES, H0 * S), np.float32)
    queries[0:S] = np.where(t[:, None] <= np.tile(t, H0)[None], 0.0, MASKED)[:, None, :]
    queries[A_ROW:M_ROW] = np.tile(np.arange(H0)[:, None] == head_of[None], (NSPLIT, 1))[:, None, :]
    first = np.tile(t == 0, H0)
    f2 = np.zeros((E1, len(CHUNKS1) * P, D), np.float32)
    f2[:, 0:FF1] = i["L1_ffn_w2"]
    return {
        "x": i["x"].reshape(TOKENS, D),
        "ctxT": ctx.T,
        "ctx_ones": np.concatenate([ctx.reshape(TOKENS, H0, DH0), ones], 2).reshape(TOKENS, H0 * VW0),
        "ident": np.eye(P, dtype=np.float32),
        "gate_wq": gate(0), "gate_wk": gate(1), "gate_wv": gate(2),
        "gate_b": np.concatenate([i["L0_xattn_igate_b"], i["L0_xattn_fgate_b"]])[:, None],
        "scan_keep": rows(np.where(first, 0.0, 1.0).astype(np.float32)),
        "scan_drop": rows(np.where(first, MASKED, 0.0).astype(np.float32)),
        "ln_scale": rows(i["L0_xattn_ln_scale"]),
        "decay_keys": bf16_bits(keys),
        "decay_queries": bf16_bits(queries),
        "router": i["L0_ffn_router_w"].T,
        "router_b": rows(i["L0_ffn_experts_bias"]),
        "iota": rows(np.arange(E0, dtype=np.float32)),
        "w1": units("L0_ffn_w1", "L0_ffn_sw1").transpose(1, 0, 2),
        "w3": units("L0_ffn_w3", "L0_ffn_sw3").transpose(1, 0, 2),
        "w2": units("L0_ffn_w2", "L0_ffn_sw2").reshape(UNITS0 * CH0, P, D).transpose(1, 0, 2),
        "wq": i["L1_xattn_Wq"].T, "wk": i["L1_xattn_Wk"].T, "wv": i["L1_xattn_Wv"].T, "wp": i["L1_xattn_Wp"].T,
        "bq": i["L1_xattn_bq"][:, None], "bk": i["L1_xattn_bk"][:, None],
        "bv": rows(i["L1_xattn_bv"]), "bp": rows(i["L1_xattn_bp"]),
        "f1": i["L1_ffn_w1"], "f3": i["L1_ffn_w3"],
        "f2": f2.reshape(E1, len(CHUNKS1), P, D).transpose(0, 2, 1, 3),
    }


def kernel(**inputs):
    import concourse.bacc as bacc
    from concourse.bass_utils import run_bass_kernel_spmd

    nc = bacc.Bacc("TRN2", target_bir_lowering=False, num_devices=1)
    arrays, aps = {}, {}
    for name, v in layouts(inputs).items():
        arrays[f"in_{name}"] = np.ascontiguousarray(v)
        aps[name] = nc.dram_tensor(f"in_{name}", v.shape, mybir.dt.from_np(v.dtype), kind="ExternalInput").ap()
    out = nc.dram_tensor("out", (TOKENS, D), F32, kind="ExternalOutput").ap()
    build(nc, aps, out)
    got = run_bass_kernel_spmd(nc, [arrays], core_ids=[0]).results[0]["out"]
    return got.reshape(E1, B, C1, D).transpose(1, 0, 2, 3).reshape(B, S, D)
```

```python
from contextlib import ExitStack

import numpy as np

import concourse.bass as bass
from concourse import mybir

F32 = mybir.dt.float32
BF16 = mybir.dt.bfloat16
U32 = mybir.dt.uint32
ACT = mybir.ActivationFunctionType
ALU = mybir.AluOpType
AX = mybir.AxisListType

B, S, D = 128, 64, 128
TOKENS = B * S
P = 128
TILES = 4
GROUP = TILES * P
GB = GROUP // S
GROUPS = TOKENS // GROUP
PAIRS = B // 2
LN_EPS = 1e-5

H0 = 8
DH0 = D // H0
VW0 = DH0 + 1
CELL_EPS = 1e-6
NSPLIT = 3
MASKED = -1.0e30
A_ROW = S
M_ROW = A_ROW + NSPLIT * H0
DECAY_ROWS = M_ROW + NSPLIT * 2

E0, HID0 = 8, 256
UNITS0 = E0 + 1
CH0 = HID0 // P

H1 = 16
DH1 = D // H1
SCALE1 = float(DH1) ** 0.5
HP1 = H1 // 2
VW1 = DH1 + 1

ONE = 1

E1, FF1 = 8, 352
C1 = S // E1
CHUNKS1 = [(c * P, min(P, FF1 - c * P)) for c in range((FF1 + P - 1) // P)]


class Steps:

    def __init__(self, eng, sem):
        self.eng, self.sem, self.base, self.n = eng, sem, 0, 0

    def at(self, base):
        self.base, self.n = base, 0

    def __call__(self, ins):
        self.n += 1
        ins.then_inc(self.sem, 1)
        self.eng.wait_ge(self.sem, ONE + self.base + self.n)


class Room:

    def __init__(self, nc, ctx, sems, phase):
        self.nc, self.ctx, self.sems, self.phase, self.all_sems = nc, ctx, sems, phase, []

    def sb(self, name, shape, dt=F32):
        return self.ctx.enter_context(self.nc.sbuf_tensor(f"{self.phase}_{name}", shape, dt))

    def ps(self, name, shape):
        return self.ctx.enter_context(self.nc.psum_tensor(f"{self.phase}_{name}", shape, F32))

    def sem(self, name):
        self.all_sems.append(self.sems.enter_context(self.nc.semaphore(f"{self.phase}_{name}")))
        return self.all_sems[-1]

    def start_at_one(self, sp):
        for sem in self.all_sems:
            sp.sem_inc(sem, ONE)

    def sem2(self, name):
        return [self.sem(f"{name}{k}") for k in range(2)]


def apart(eng):
    eng.nop(nofuse=True)


class LayerNorm:

    def __init__(self, r):
        self.sums = [r.sb(f"sums{k}", [P, TILES, 6]) for k in range(2)]
        self.mv = [r.sb(f"mv{k}", [P, TILES, 2]) for k in range(2)]
        self.rstd = [r.sb(f"rstd{k}", [P, TILES]) for k in range(2)]
        self.shifted = [r.sb(f"shifted{k}", [P, TILES]) for k in range(2)]
        self.power = r.sb("power", [P, TILES])
        self.shifted_done, self.sums_done = r.sem("shifted_done"), r.sem("sums_done")
        self.var_done, self.rstd_done = r.sem("var_done"), r.sem("rstd_done")

    def statistics(self, v, n, k, x):
        for t in range(TILES):
            ins = v.bn_stats(self.sums[k][:, t, :], x[:, t, :])
        ins.then_inc(self.sums_done, 1)
        v.wait_ge(self.sums_done, ONE + n + 1)
        apart(v)
        for t in range(TILES):
            ins = v.bn_aggr(self.mv[k][:, t, :], self.sums[k][:, t, :])
        ins.then_inc(self.var_done, 1)

    def apply(self, v, n, k, x, y):
        v.wait_ge(self.rstd_done, ONE + n + 1)
        for t in range(TILES):
            ins = v.tensor_scalar(y[:, t, :], x[:, t, :], self.mv[k][:, t, 0:1], self.rstd[k][:, t:t + 1],
                                  ALU.subtract, ALU.mult)
        return ins

    def power_const(self, pool):
        pool.memset(self.power[:, :], -0.5).then_inc(self.shifted_done, 1)

    def root(self, pool, n, k):
        pool.wait_ge(self.var_done, ONE + n + 1)
        pool.wait_ge(self.rstd_done, ONE + n)
        apart(pool)
        pool.tensor_scalar(self.shifted[k][:, :], self.mv[k][:, :, 1], LN_EPS, None, ALU.add).then_inc(self.shifted_done, 1)
        pool.wait_ge(self.shifted_done, ONE + n + 2)
        pool.tensor_tensor(self.rstd[k][:, :], self.shifted[k][:, :], self.power[:, :], ALU.pow).then_inc(self.rstd_done, 1)

    def roots(self, pool, groups):
        self.power_const(pool)
        with pool.Fori(0, groups // 2) as j:
            for k in range(2):
                self.root(pool, 2 * j + k, k)


def following(j, k):
    return (j, 1) if k == 0 else (j + 1, 0)


def before(j, k):
    return (j - 1, 1) if k == 0 else (j, 0)


def over_groups(eng, step, n=GROUPS):
    step(0, 0, True, False)
    with eng.Fori(0, n // 2 - 1) as j:
        step(j, 1, False, False)
        step(j + 1, 0, False, False)
    step(n // 2 - 1, 1, False, True)


def whole(t):
    return t[(slice(None),) * len(t.shape)]


def tiles_of(dram, g):
    return dram[bass.ds(g * GROUP, GROUP), :].rearrange("(t p) d -> p t d", p=P)


def phase_gates(nc, sems, a, s):
    with ExitStack() as ctx:
        r = Room(nc, ctx, sems, "gates")
        ident = r.sb("ident", [P, P])
        wq, wk, wv, wkv = (r.sb(n, [D, 2 * H0]) for n in ("wq", "wk", "wv", "wkv"))
        bias = r.sb("bias", [2 * H0, 1])
        x = [r.sb(f"x{k}", [P, TILES, D]) for k in range(2)]
        ctxT = [r.sb(f"ctxT{k}", [D, GROUP]) for k in range(2)]
        xn = [r.sb(f"xn{k}", [P, TILES, D]) for k in range(2)]
        xnT = [r.sb(f"xnT{k}", [D, GROUP]) for k in range(2)]
        rows = [r.sb(f"rows{k}", [2 * H0, GROUP]) for k in range(2)]
        ln = LayerNorm(r)
        psT = [r.ps(f"psT{k}", [P, GROUP]) for k in range(2)]
        psG = [r.ps(f"psG{k}", [P, GROUP]) for k in range(2)]
        const_in, wkv_done = r.sem("const_in"), r.sem("wkv_done")
        x_in, ctx_in = r.sem2("x_in"), r.sem2("ctx_in")
        xn_done, turned, xnT_done = r.sem2("xn_done"), r.sem2("turned"), r.sem2("xnT_done")
        summed, rows_done, stored = r.sem2("summed"), r.sem2("rows_done"), r.sem2("stored")
        consts = ((ident, "ident"), (wq, "gate_wq"), (wk, "gate_wk"), (wv, "gate_wv"), (bias, "gate_b"))
        block = ctx.enter_context(nc.Block())

        @block.sync
        def _(sp):
            r.start_at_one(sp)
            for dst, src in consts:
                sp.dma_start(dst[:, :], a[src]).then_inc(const_in, 16)
            with sp.Fori(0, GROUPS // 2) as j:
                for k in range(2):
                    g = 2 * j + k
                    sp.wait_ge(xn_done[k], ONE + j)
                    apart(sp)
                    sp.dma_start(x[k][:, :, :], tiles_of(a["x"], g)).then_inc(x_in[k], 16)
                    sp.wait_ge(summed[k], ONE + j)
                    apart(sp)
                    sp.dma_start(ctxT[k][:, :], a["ctxT"][:, bass.ds(g * GROUP, GROUP)]).then_inc(ctx_in[k], 16)

        @block.vector
        def _(v):
            def statistics(j, k):
                v.wait_ge(x_in[k], ONE + 16 * j + 16)
                ln.statistics(v, 2 * j + k, k, x[k])

            def step(j, k, first, last):
                if not last:
                    statistics(*following(j, k))
                v.wait_ge(turned[k], ONE + j)
                ln.apply(v, 2 * j + k, k, x[k], xn[k]).then_inc(xn_done[k], 1)

            v.wait_ge(const_in, ONE + 16 * len(consts))
            v.tensor_tensor(wkv[:, :], wk[:, :], wv[:, :], ALU.add).then_inc(wkv_done, 1)
            statistics(0, 0)
            over_groups(v, step)

        @block.tensor
        def _(pe):
            def turn(j, k):
                pe.wait_ge(xn_done[k], ONE + j + 1)
                pe.wait_ge(xnT_done[k], ONE + j)
                for t in range(TILES):
                    ins = pe.transpose(psT[k][:, t * P:(t + 1) * P], xn[k][:, t, :], ident[:, :])
                ins.then_inc(turned[k], 1)

            def step(j, k, first, last):
                pe.wait_ge(ctx_in[k], ONE + 16 * j + 16)
                pe.wait_ge(rows_done[k], ONE + j)
                pe.matmul(psG[k][0:2 * H0, :], wkv[:, :], ctxT[k][:, :], start=True, stop=False)
                pe.wait_ge(xnT_done[k], ONE + j + 1)
                pe.matmul(psG[k][0:2 * H0, :], wq[:, :], xnT[k][:, :], start=False, stop=True).then_inc(summed[k], 1)
                if not last:
                    turn(*following(j, k))

            pe.wait_ge(const_in, ONE + 16 * len(consts))
            pe.wait_ge(wkv_done, ONE + 1)
            turn(0, 0)
            over_groups(pe, step)

        @block.scalar
        def _(act):
            act.wait_ge(const_in, ONE + 16 * len(consts))
            with act.Fori(0, GROUPS // 2) as j:
                for k in range(2):
                    g = 2 * j + k
                    act.wait_ge(stored[k], ONE + 32 * j)
                    act.wait_ge(turned[k], ONE + j + 1)
                    act.activation(xnT[k][:, :], psT[k][:, :], ACT.Copy).then_inc(xnT_done[k], 1)
                    act.wait_ge(xnT_done[k], ONE + j + 1)
                    act.dma_start(s["xnT"][:, bass.ds(g * GROUP, GROUP)], xnT[k][:, :]).then_inc(stored[k], 16)
                    act.wait_ge(summed[k], ONE + j + 1)
                    act.activation(rows[k][:, :], psG[k][0:2 * H0, :], ACT.Identity,
                                   bias=bias[:, 0:1]).then_inc(rows_done[k], 1)
                    act.wait_ge(rows_done[k], ONE + j + 1)
                    act.dma_start(s["gates"][bass.ds(g * GB, GB)].rearrange("b h t -> h b t"),
                                  rows[k][:, :].rearrange("h (b t) -> h b t", b=GB)).then_inc(stored[k], 16)
            for k in range(2):
                act.wait_ge(stored[k], ONE + 32 * (GROUPS // 2))

        @block.gpsimd
        def _(pool):
            ln.roots(pool, GROUPS)


def phase_decay(nc, sems, a, s):
    N = H0 * S
    with ExitStack() as ctx:
        r = Room(nc, ctx, sems, "decay")
        ident = r.sb("ident", [P, P])
        keep, drop = r.sb("keep", [B, N]), r.sb("drop", [B, N])
        gates = r.sb("gates", [B, 2 * N])
        ig, fg = gates[:, 0:N], gates[:, N:2 * N]
        t1, t2, t3 = (r.sb(n, [B, N]) for n in ("t1", "t2", "t3"))
        logf, cs, am, peak, neg_max, neg_peak = (r.sb(n, [B, N]) for n in ("logf", "cs", "am", "peak", "nmax", "npeak"))
        m_parts = r.sb("m_parts", [B, NSPLIT, N], BF16)
        a_parts = r.sb("a_parts", [B, NSPLIT, N], BF16)
        rest = r.sb("rest", [B, N])
        floor = r.sb("floor", [P, PAIRS, H0])
        psE = r.ps("psE", [P, H0 * PAIRS])
        loaded, dve_step, for_act, act_step = r.sem("loaded"), r.sem("dve_step"), r.sem("for_act"), r.sem("act_step")
        nmax_done, turned, floor_done = r.sem("nmax_done"), r.sem("turned"), r.sem("floor_done")
        parts_done, stored = r.sem("parts_done"), r.sem("stored")
        block = ctx.enter_context(nc.Block())

        @block.sync
        def _(sp):
            r.start_at_one(sp)
            sp.dma_start(gates[:, :], s["gates"].rearrange("b h t -> b (h t)")).then_inc(loaded, 16)
            sp.dma_start(keep[:, :], a["scan_keep"]).then_inc(loaded, 16)
            sp.dma_start(drop[:, :], a["scan_drop"]).then_inc(loaded, 16)
            sp.dma_start(ident[:, :], a["ident"]).then_inc(loaded, 16)
            sp.wait_ge(floor_done, ONE + 1)
            sp.dma_start(s["floor"], floor[:, :, :]).then_inc(stored, 16)
            sp.wait_ge(parts_done, ONE + 2)
            for n in range(NSPLIT):
                sp.dma_start(s["m_parts"][n], m_parts[:, n, :]).then_inc(stored, 16)
                sp.dma_start(s["a_parts"][n].rearrange("b h t -> b (h t)"), a_parts[:, n, :]).then_inc(stored, 16)
            sp.wait_ge(stored, ONE + 16 * (1 + 2 * NSPLIT))

        @block.vector
        def _(v):
            step = Steps(v, dve_step)
            v.wait_ge(loaded, ONE + 64)
            v.scalar_tensor_tensor(out=t1[:, :], in0=fg, scalar=-1.0, in1=fg, op0=ALU.mult, op1=ALU.max).then_inc(for_act, 1)
            v.wait_ge(act_step, ONE + 1)
            v.tensor_scalar(t3[:, :], t2[:, :], 1.0, None, ALU.add).then_inc(for_act, 1)
            v.wait_ge(act_step, ONE + 2)
            step(v.scalar_tensor_tensor(out=logf[:, :], in0=fg, scalar=0.0, in1=t1[:, :], op0=ALU.min, op1=ALU.subtract))
            step(v.tensor_tensor_scan(cs[:, :], keep[:, :], logf[:, :], 0.0, ALU.mult, ALU.add))
            step(v.tensor_tensor(am[:, :], ig, cs[:, :], ALU.subtract))
            step(v.tensor_tensor_scan(peak[:, :], drop[:, :], am[:, :], 0.0, ALU.add, ALU.max))
            step(v.tensor_scalar(neg_peak[:, :], peak[:, :], -1.0, None, ALU.mult))
            v.tensor_tensor(neg_max[:, :], neg_peak[:, :], cs[:, :], ALU.subtract).then_inc(nmax_done, 1)
            for whole, parts in ((neg_peak, m_parts), (am, a_parts)):
                left = whole
                for n in range(NSPLIT):
                    ins = v.tensor_copy(parts[:, n, :], left[:, :])
                    if n == NSPLIT - 1:
                        ins.then_inc(parts_done, 1)
                        v.wait_ge(parts_done, ONE + (1 if parts is m_parts else 2))
                    else:
                        step(ins)
                        step(v.tensor_tensor(rest[:, :], left[:, :], parts[:, n, :], ALU.subtract))
                        left = rest

        @block.scalar
        def _(act):
            act.wait_ge(for_act, ONE + 1)
            act.activation(t2[:, :], t1[:, :], ACT.Exp, scale=-1.0).then_inc(act_step, 1)
            act.wait_ge(for_act, ONE + 2)
            act.activation(t1[:, :], t3[:, :], ACT.Ln).then_inc(act_step, 1)
            act.wait_ge(turned, ONE + 1)
            act.activation(floor[:, :, :], psE[:, :].rearrange("p (h i) -> p i h", h=H0), ACT.Exp).then_inc(floor_done, 1)

        @block.tensor
        def _(pe):
            pe.wait_ge(loaded, ONE + 64)
            pe.wait_ge(nmax_done, ONE + 1)
            for h in range(H0):
                for b2 in range(2):
                    ins = pe.matmul(psE[b2 * S:(b2 + 1) * S, h * PAIRS:(h + 1) * PAIRS], neg_max[:, h * S:(h + 1) * S],
                                    ident[:, b2::2], start=True, stop=True)
            ins.then_inc(turned, 1)


def phase_mlstm(nc, sems, a, s):
    N = H0 * S
    with ExitStack() as ctx:
        r = Room(nc, ctx, sems, "mlstm")
        ln_scale = r.sb("ln_scale", [P, D])
        keysT = [r.sb(f"keysT{k}", [D, GROUP]) for k in range(2)]
        qheads = [r.sb(f"qheads{k}", [D, GB, H0, S]) for k in range(2)]
        vals = [r.sb(f"vals{k}", [P, TILES, H0 * VW0]) for k in range(2)]
        x = [r.sb(f"x{k}", [P, TILES, D]) for k in range(2)]
        floor = [r.sb(f"floor{k}", [P, TILES, H0]) for k in range(2)]
        dk = [r.sb(f"dk{k}", [DECAY_ROWS, GROUP], BF16) for k in range(2)]
        dq = [r.sb(f"dq{k}", [DECAY_ROWS, TILES, N], BF16) for k in range(2)]
        decay = [r.sb(f"decay{k}", [P, N]) for k in range(2)]
        cT = [r.sb(f"cT{k}", [P, N]) for k in range(2)]
        norm, inv = r.sb("norm", [P, TILES, H0]), r.sb("inv", [P, TILES, H0])
        h = r.sb("h", [P, TILES, D])
        y, ys = r.sb("y", [P, TILES, D]), r.sb("ys", [P, TILES, D])
        out = [r.sb(f"out{k}", [P, TILES, D]) for k in range(2)]
        ln = LayerNorm(r)
        psA = [r.ps(f"psA{k}", [P, N]) for k in range(2)]
        psS = [r.ps(f"psS{k}", [P, N]) for k in range(2)]
        psV = [[r.ps(f"psV{k}{i}", [P, 512]) for i in range(2)] for k in range(2)]
        const_in, zeroed = r.sem("const_in"), r.sem("zeroed")
        pe_in, q_in, tail_in = r.sem2("pe_in"), r.sem2("q_in"), r.sem2("tail_in")
        arg_done, qk_done = r.sem("arg"), r.sem("qk")
        decay_done, cT_done = r.sem2("decay"), r.sem2("cT")
        cT_used = r.sem2("cT_used")
        group_done = r.sem2("group_done")
        h_done, tail_done, stored = (r.sem2(n) for n in ("h_done", "tail", "stored"))
        dve_step = r.sem("dve_step")
        TAIL_STEPS = 6
        block = ctx.enter_context(nc.Block())

        @block.sync
        def _(sp):
            r.start_at_one(sp)
            sp.dma_start(ln_scale[:, :], a["ln_scale"]).then_inc(const_in, 16)
            for k in range(2):
                sp.dma_start(dk[k][:, :], a["decay_keys"].bitcast(BF16)).then_inc(const_in, 16)
                sp.dma_start(dq[k][:, :, :], a["decay_queries"].bitcast(BF16)).then_inc(const_in, 16)
            sp.wait_ge(const_in, ONE + 16 * 5)

            def load(j, k):
                g = 2 * j + k
                sp.wait_ge(group_done[k], ONE + j)
                apart(sp)
                sp.dma_start(keysT[k][:, :], a["ctxT"][:, bass.ds(g * GROUP, GROUP)]).then_inc(pe_in[k], 16)
                for h_ in range(H0):
                    sp.dma_start(qheads[k][h_ * DH0:(h_ + 1) * DH0, :, h_, :],
                                 s["xnT"][h_ * DH0:(h_ + 1) * DH0, bass.ds(g * GROUP, GROUP)].rearrange(
                                     "d (b t) -> d b t", b=GB)).then_inc(q_in[k], 16)
                sp.dma_start(vals[k][:, :, :], a["ctx_ones"][bass.ds(g * GROUP, GROUP), :].rearrange(
                    "(t p) d -> p t d", p=P)).then_inc(pe_in[k], 16)
                for n in range(NSPLIT):
                    sp.dma_start(dk[k][A_ROW + n * H0:A_ROW + (n + 1) * H0, :].rearrange("h (b t) -> h b t", b=GB),
                                 s["a_parts"][n, bass.ds(g * GB, GB)].rearrange("b h t -> h b t")).then_inc(pe_in[k], 16)
                    sp.dma_start(dq[k][M_ROW + 2 * n:M_ROW + 2 * n + 2, :, :],
                                 s["m_parts"][n, bass.ds(g * GB, GB), :].rearrange("(i c) n -> c i n", c=2)).then_inc(pe_in[k], 16)
                sp.wait_ge(tail_done[k], ONE + j)
                apart(sp)
                sp.dma_start(x[k][:, :, :], tiles_of(a["x"], g)).then_inc(tail_in[k], 16)
                sp.dma_start(floor[k][:, :, :], s["floor"][:, bass.ds(g * TILES, TILES), :]).then_inc(tail_in[k], 16)

            def store(j, k):
                sp.wait_ge(tail_done[k], ONE + j + 1)
                apart(sp)
                sp.dma_start(tiles_of(s["x1"], 2 * j + k), out[k][:, :, :]).then_inc(stored[k], 16)

            def step(j, k, first, last):
                if not last:
                    load(*following(j, k))
                if not first:
                    store(*before(j, k))

            sp.wait_ge(zeroed, ONE + 2)
            load(0, 0)
            over_groups(sp, step)
            store(GROUPS // 2 - 1, 1)
            for k in range(2):
                sp.wait_ge(stored[k], ONE + 16 * (GROUPS // 2))

        @block.gpsimd
        def _(pool):
            for k in range(2):
                pool.memset(qheads[k][:, :, :, :], 0.0).then_inc(zeroed, 1)
            pool.wait_ge(zeroed, ONE + 2)

            ln.roots(pool, GROUPS)

        @block.tensor
        def _(pe):
            def scores(j, k, i):
                c = i % 2
                n = 2 * (2 * j + k) + i // 2
                pe.wait_ge(decay_done[c], ONE + n)
                pe.matmul(psA[c][:, :], dk[k][:, i * P:(i + 1) * P], dq[k][:, i, :], start=True, stop=True).then_inc(arg_done, 1)
                pe.wait_ge(cT_done[c], ONE + n)
                for b2 in range(2):
                    b = 2 * i + b2
                    ins = pe.matmul(psS[c][b2 * S:(b2 + 1) * S, :], keysT[k][:, b * S:(b + 1) * S],
                                    qheads[k][:, b, :, :].rearrange("p h t -> p (h t)"), start=True, stop=True)
                ins.then_inc(qk_done, 1)

            def values(j, k, i):
                c = i % 2
                pe.wait_ge(cT_done[c], ONE + 2 * (2 * j + k) + i // 2 + 1)
                apart(pe)
                for h_ in range(H0):
                    for b2 in range(2):
                        at = (i % 2) * H0 * VW0 + h_ * VW0
                        rows = slice(b2 * S, (b2 + 1) * S)
                        ins = pe.matmul(psV[k][i // 2][rows, at:at + VW0], cT[c][rows, h_ * S:(h_ + 1) * S],
                                        vals[k][rows, i, h_ * VW0:(h_ + 1) * VW0], start=True, stop=True)
                ins.then_inc(group_done[k] if i == TILES - 1 else cT_used[c], 1)

            def step(j, k, first, last):
                pe.wait_ge(pe_in[k], ONE + 16 * (2 + 2 * NSPLIT) * (j + 1))
                pe.wait_ge(q_in[k], ONE + 16 * H0 * (j + 1))
                scores(j, k, 0)
                if not first:
                    values(*before(j, k), TILES - 1)
                scores(j, k, 1)
                pe.wait_ge(h_done[k], ONE + j)
                for i in range(2, TILES):
                    values(j, k, i - 2)
                    scores(j, k, i)
                values(j, k, TILES - 2)

            over_groups(pe, step)
            values(GROUPS // 2 - 1, 1, TILES - 1)

        @block.scalar
        def _(act):
            with act.Fori(0, GROUPS // 2) as j:
                for k in range(2):
                    g = 2 * j + k
                    for i in range(TILES):
                        c, n = i % 2, 2 * g + i // 2
                        act.wait_ge(arg_done, ONE + TILES * g + i + 1)
                        act.wait_ge(cT_done[c], ONE + n)
                        act.activation(decay[c][:, :], psA[c][:, :], ACT.Exp).then_inc(decay_done[c], 1)

        @block.vector
        def _(v):
            steps = Steps(v, dve_step)

            def weigh(j, k, i):
                g, c = 2 * j + k, i % 2
                n = 2 * g + i // 2
                v.wait_ge(qk_done, ONE + TILES * g + i + 1)
                v.wait_ge(decay_done[c], ONE + n + 1)
                if i == 1:
                    v.wait_ge(group_done[1 - k], ONE + j + k)
                elif i == 3:
                    v.wait_ge(cT_used[1], ONE + g + 1)
                else:
                    v.wait_ge(cT_used[0], ONE + n)
                v.scalar_tensor_tensor(out=cT[c][:, :], in0=psS[c][:, :], scalar=float(DH0) ** -0.5,
                                       in1=decay[c][:, :], op0=ALU.mult, op1=ALU.mult).then_inc(cT_done[c], 1)

            def normalise(j, k):
                g = 2 * j + k
                steps.at(g * TAIL_STEPS)
                v.wait_ge(group_done[k], ONE + j + 1)
                v.wait_ge(tail_in[k], ONE + 32 * (j + 1))
                flat = [psV[k][i][:, 0:2 * H0 * VW0].rearrange("p (h w) -> p h w", w=VW0) for i in range(2)]
                halves = [slice(2 * i, 2 * i + 2) for i in range(2)]
                sums = [psV[k][i][:, 0:2 * H0 * VW0].rearrange("p (t h w) -> p t h w", t=2, h=H0)[:, :, :, DH0] for i in range(2)]
                for i in range(2):
                    ins = v.scalar_tensor_tensor(out=norm[:, halves[i], :], in0=sums[i], scalar=-1.0,
                                                 in1=floor[k][:, halves[i], :], op0=ALU.mult, op1=ALU.max)
                steps(ins)
                for i in range(2):
                    ins = v.tensor_tensor(norm[:, halves[i], :], sums[i], norm[:, halves[i], :], ALU.max)
                steps(ins)
                steps(v.tensor_scalar(norm[:, :, :], norm[:, :, :], CELL_EPS, None, ALU.add))
                steps(v.reciprocal(inv[:, :, :], norm[:, :, :]))
                for i in range(2):
                    iv = inv[:, halves[i], :].rearrange("p t h -> p (t h)").unsqueeze(2).to_broadcast([P, 2 * H0, DH0])
                    ins = v.tensor_tensor(h[:, halves[i], :].rearrange("p t (h w) -> p (t h) w", h=H0),
                                          flat[i][:, :, 0:DH0], iv, ALU.mult)
                ins.then_inc(h_done[k], 1)
                v.wait_ge(h_done[k], ONE + j + 1)
                ln.statistics(v, g, k, h)

            def finish(j, k):
                steps(ln.apply(v, 2 * j + k, k, h, y))
                steps(v.tensor_tensor(ys[:, :, :], y[:, :, :], ln_scale[:, :].unsqueeze(1).to_broadcast([P, TILES, D]), ALU.mult))
                v.wait_ge(stored[k], ONE + 16 * j)
                v.tensor_tensor(out[k][:, :, :], x[k][:, :, :], ys[:, :, :], ALU.add).then_inc(tail_done[k], 1)

            def step(j, k, first, last):
                weigh(j, k, 0)
                weigh(j, k, 1)
                if not first:
                    normalise(*before(j, k))
                weigh(j, k, 2)
                if not first:
                    finish(*before(j, k))
                weigh(j, k, 3)

            v.wait_ge(const_in, ONE + 16 * 5)
            over_groups(v, step)
            normalise(GROUPS // 2 - 1, 1)
            finish(GROUPS // 2 - 1, 1)


def phase_experts(nc, sems, a, s):
    with ExitStack() as ctx:
        r = Room(nc, ctx, sems, "experts")
        ident = r.sb("ident", [P, P])
        router, bias, iota = r.sb("router", [D, E0]), r.sb("bias", [P, E0]), r.sb("iota", [P, E0])
        w1, w3 = r.sb("w1", [D, UNITS0, HID0]), r.sb("w3", [D, UNITS0, HID0])
        w2 = r.sb("w2", [P, UNITS0 * CH0, D])
        x = [r.sb(f"x{k}", [P, TILES, D]) for k in range(2)]
        xn = [r.sb(f"xn{k}", [P, TILES, D]) for k in range(2)]
        xnT = [r.sb(f"xnT{k}", [D, GROUP]) for k in range(2)]
        ln = LayerNorm(r)
        logits, top = r.sb("logits", [P, TILES, E0]), r.sb("top", [P, TILES, 8])
        where, wheref = r.sb("where", [P, TILES, 8], U32), r.sb("wheref", [P, TILES, 8])
        gap, tanh = r.sb("gap", [P, TILES]), r.sb("tanh", [P, TILES])
        share = r.sb("share", [P, 2, TILES])
        pick = r.sb("pick", [P, 2, TILES, E0])
        cw = [r.sb(f"cw{k}", [P, TILES, E0]) for k in range(2)]
        act_g = [r.sb(f"act_g{c}", [P, GROUP]) for c in range(CH0)]
        hT = [[r.sb(f"hT{u}{c}", [P, GROUP]) for c in range(CH0)] for u in range(2)]
        psT, psR = r.ps("psT", [P, GROUP]), r.ps("psR", [P, 512])
        psG = [r.ps(f"psG{c}", [P, GROUP]) for c in range(CH0)]
        psU = [r.ps(f"psU{c}", [P, GROUP]) for c in range(CH0)]
        psY = [r.ps(f"psY{u}", [P, TILES, D]) for u in range(2)]
        const_in = r.sem("const_in")
        x_in, xn_done, turned, xnT_done = r.sem2("x_in"), r.sem2("xn"), r.sem("turned"), r.sem2("xnT")
        routed, gap_done, tanh_done = r.sem("routed"), r.sem("gap"), r.sem("tanh")
        up_done, silu_done, h_done, y_done = r.sem("up"), r.sem("silu"), r.sem2("h"), r.sem("y")
        added, stored, xnT_used = r.sem("added"), r.sem2("stored"), r.sem2("xnT_used")
        front_step = r.sem("front_step")
        consts = ((ident, "ident"), (router, "router"), (bias, "router_b"), (iota, "iota"), (w1, "w1"), (w3, "w3"), (w2, "w2"))
        LN_AT, ROUTE_AT = 2, 4
        ROUTE_STEPS = 8
        block = ctx.enter_context(nc.Block())

        @block.sync
        def _(sp):
            r.start_at_one(sp)
            for dst, src in consts:
                sp.dma_start(whole(dst), a[src]).then_inc(const_in, 16)

            def load(j, k):
                sp.wait_ge(stored[k], ONE + 16 * j)
                apart(sp)
                sp.dma_start(x[k][:, :, :], tiles_of(s["x1"], 2 * j + k)).then_inc(x_in[k], 16)

            def step(j, k, first, last):
                if not last:
                    load(*following(j, k))
                sp.wait_ge(added, ONE + (2 * j + k + 1) * UNITS0)
                apart(sp)
                sp.dma_start(tiles_of(s["x2"], 2 * j + k), x[k][:, :, :]).then_inc(stored[k], 16)

            load(0, 0)
            over_groups(sp, step)
            for k in range(2):
                sp.wait_ge(stored[k], ONE + 16 * (GROUPS // 2))

        @block.gpsimd
        def _(pool):
            ln.roots(pool, GROUPS)

        @block.tensor
        def _(pe):
            def turn(j, k):
                pe.wait_ge(xn_done[k], ONE + j + 1)
                pe.wait_ge(xnT_done[1 - k], ONE + j + k)
                for t in range(TILES):
                    ins = pe.transpose(psT[:, t * P:(t + 1) * P], xn[k][:, t, :], ident[:, :])
                ins.then_inc(turned, 1)

            def route(j, k):
                pe.wait_ge(xnT_done[k], ONE + j + 1)
                pe.wait_ge(gap_done, ONE + 2 * j + k)
                for t in range(TILES):
                    ins = pe.matmul(psR[:, t * E0:(t + 1) * E0], xnT[k][:, t * P:(t + 1) * P], router[:, :], start=True, stop=True)
                ins.then_inc(routed, 1)

            def up(g, k, e):
                for c in range(CH0):
                    pe.wait_ge(h_done[c], ONE + g * UNITS0 + e)
                    pe.matmul(psG[c][:, :], w1[:, e, c * P:(c + 1) * P], xnT[k][:, :], start=True, stop=True)
                    pe.matmul(psU[c][:, :], w3[:, e, c * P:(c + 1) * P], xnT[k][:, :], start=True, stop=True).then_inc(up_done, 1)

            def down(g, k, e):
                n = g * UNITS0 + e
                u = (k * UNITS0 + e) % 2
                for c in range(CH0):
                    pe.wait_ge(h_done[c], ONE + n + 1)
                if e >= 2:
                    pe.wait_ge(added, ONE + n - 1)
                else:
                    pe.wait_ge(added, ONE + g * UNITS0)
                for t in range(TILES):
                    for c in range(CH0):
                        ins = pe.matmul(psY[u][:, t, :], hT[u][c][:, t * P:(t + 1) * P], w2[:, e * CH0 + c, :],
                                        start=(c == 0), stop=(c == CH0 - 1))
                ins.then_inc(y_done, 1)

            def step(j, k, first, last):
                g = 2 * j + k
                for e in range(UNITS0):
                    up(g, k, e)
                    if e:
                        down(g, k, e - 1)
                    if not last and e == LN_AT:
                        turn(*following(j, k))
                    if not last and e == ROUTE_AT:
                        route(*following(j, k))
                down(g, k, UNITS0 - 1)

            pe.wait_ge(const_in, ONE + 16 * len(consts))
            turn(0, 0)
            route(0, 0)
            over_groups(pe, step)

        @block.scalar
        def _(act):
            def xnT_out(j, k):
                act.wait_ge(turned, ONE + 2 * j + k + 1)
                act.wait_ge(stored[k], ONE + 16 * j)
                act.activation(xnT[k][:, :], psT[:, :], ACT.Copy).then_inc(xnT_done[k], 1)

            def tanh_of_gap(j, k):
                act.wait_ge(gap_done, ONE + 2 * j + k + 1)
                act.activation(tanh[:, :], gap[:, :], ACT.Tanh, scale=0.5).then_inc(tanh_done, 1)

            def step(j, k, first, last):
                g = 2 * j + k
                for e in range(UNITS0):
                    for c in range(CH0):
                        act.wait_ge(up_done, ONE + CH0 * (g * UNITS0 + e) + c + 1)
                        act.wait_ge(h_done[c], ONE + g * UNITS0 + e)
                        act.activation(act_g[c][:, :], psG[c][:, :], ACT.Silu).then_inc(silu_done, 1)
                    if not last and e == LN_AT:
                        xnT_out(*following(j, k))
                    if not last and e == ROUTE_AT:
                        tanh_of_gap(*following(j, k))

            xnT_out(0, 0)
            tanh_of_gap(0, 0)
            over_groups(act, step)

        @block.vector
        def _(v):
            step_ = Steps(v, front_step)

            def statistics(j, k):
                v.wait_ge(x_in[k], ONE + 16 * (j + 1))
                ln.statistics(v, 2 * j + k, k, x[k])

            def normalise(j, k):
                ln.apply(v, 2 * j + k, k, x[k], xn[k]).then_inc(xn_done[k], 1)

            def gap_of(j, k):
                step_.at((2 * j + k) * ROUTE_STEPS)
                v.wait_ge(routed, ONE + 2 * j + k + 1)
                step_(v.tensor_tensor(logits[:, :, :], psR[:, 0:TILES * E0].rearrange("p (t e) -> p t e", t=TILES),
                                      bias[:, :].unsqueeze(1).to_broadcast([P, TILES, E0]), ALU.add))
                apart(v)
                for t in range(TILES):
                    ins = v.max(top[:, t, :], logits[:, t, :])
                step_(ins)
                v.tensor_tensor(gap[:, :], top[:, :, 0], top[:, :, 1], ALU.subtract).then_inc(gap_done, 1)
                for t in range(TILES):
                    ins = v.max_index(where[:, t, :], top[:, t, :], logits[:, t, :])
                step_(ins)
                step_(v.tensor_copy(wheref[:, :, :], where[:, :, :]))

            def weights(j, k):
                v.wait_ge(tanh_done, ONE + 2 * j + k + 1)
                step_(v.tensor_scalar(share[:, 0, :], tanh[:, :], 0.5, 0.5, ALU.mult, ALU.add))
                step_(v.tensor_scalar(share[:, 1, :], tanh[:, :], -0.5, 0.5, ALU.mult, ALU.add))
                for n in range(2):
                    for t in range(TILES):
                        ins = v.tensor_scalar(pick[:, n, t, :], iota[:, :], wheref[:, t, n:n + 1], share[:, n, t:t + 1],
                                              ALU.is_equal, ALU.mult)
                step_(ins)
                step_(v.tensor_tensor(cw[k][:, :, :], pick[:, 0, :, :], pick[:, 1, :, :], ALU.add))

            def gated(g, k, e):
                for c in range(CH0):
                    u = (k * UNITS0 + e) % 2
                    n = g * UNITS0 + e
                    v.wait_ge(silu_done, ONE + CH0 * n + c + 1)
                    v.wait_ge(y_done, ONE + (n - 1 if e >= 1 else g * UNITS0))
                    v.tensor_tensor(hT[u][c][:, :], act_g[c][:, :], psU[c][:, :], ALU.mult).then_inc(h_done[c], 1)

            def add(g, k, e):
                n = g * UNITS0 + e
                u = (k * UNITS0 + e) % 2
                v.wait_ge(y_done, ONE + n + 1)
                v.wait_ge(added, ONE + n)
                if e == E0:
                    ins = v.tensor_tensor(x[k][:, :, :], psY[u][:, :, :], x[k][:, :, :], ALU.add)
                else:
                    for t in range(TILES):
                        ins = v.scalar_tensor_tensor(out=x[k][:, t, :], in0=psY[u][:, t, :], scalar=cw[k][:, t, e:e + 1],
                                                     in1=x[k][:, t, :], op0=ALU.mult, op1=ALU.add)
                ins.then_inc(added, 1)

            def step(j, k, first, last):
                g = 2 * j + k
                for e in range(UNITS0):
                    gated(g, k, e)
                    if e:
                        add(g, k, e - 1)
                    if not last and e == LN_AT - 2:
                        statistics(*following(j, k))
                    if not last and e == LN_AT - 1:
                        normalise(*following(j, k))
                    if not last and e == ROUTE_AT:
                        gap_of(*following(j, k))
                    if not last and e == ROUTE_AT + 1:
                        weights(*following(j, k))
                add(g, k, UNITS0 - 1)

            v.wait_ge(const_in, ONE + 16 * len(consts))
            statistics(0, 0)
            normalise(0, 0)
            gap_of(0, 0)
            weights(0, 0)
            over_groups(v, step)


def phase_attention(nc, sems, a, s):
    NS = H1 * S
    with ExitStack() as ctx:
        r = Room(nc, ctx, sems, "attn")
        ident = r.sb("ident", [P, P])
        wq, wk, wv, wp = (r.sb(n, [D, D]) for n in ("wq", "wk", "wv", "wp"))
        bq, bqs, bk = (r.sb(n, [D, 1]) for n in ("bq", "bqs", "bk"))
        bv, bp = r.sb("bv", [P, D]), r.sb("bp", [P, D])
        x = [r.sb(f"x{k}", [P, TILES, D]) for k in range(2)]
        xb = [r.sb(f"xb{k}", [P, TILES, D]) for k in range(2)]
        ctxT = [r.sb(f"ctxT{k}", [D, GROUP]) for k in range(2)]
        xn, xnT = r.sb("xn", [P, TILES, D]), r.sb("xnT", [D, GROUP])
        ln = LayerNorm(r)
        qT = [r.sb(f"qT{k}", [D, GROUP]) for k in range(2)]
        kT = r.sb("kT", [D, GROUP])
        kheads = [r.sb(f"kheads{k}", [D, GB, H1, S]) for k in range(2)]
        vheads = [r.sb(f"vheads{k}", [P, GB, HP1, 2, VW1]) for k in range(2)]
        peak = [r.sb(f"peak{c}", [P, H1]) for c in range(2)]
        low = [r.sb(f"low{c}", [P, NS]) for c in range(2)]
        prob = [r.sb(f"prob{c}", [P, NS]) for c in range(2)]
        probT = [r.sb(f"probT{c}", [P, HP1, P]) for c in range(2)]
        inv = [r.sb(f"inv{c}", [P, H1]) for c in range(2)]
        heads, headsT = r.sb("heads", [P, TILES, D]), r.sb("headsT", [P, GROUP])
        out = [r.sb(f"out{k}", [P, TILES, D]) for k in range(2)]
        psS = [r.ps(f"psS{c}", [P, NS]) for c in range(2)]
        psP = r.ps("psP", [P, HP1, P])
        psO, psM = r.ps("psO", [P, 512]), r.ps("psM", [P, 512])
        const_in, bqs_done, blank, xb_done = r.sem("const_in"), r.sem("bqs"), r.sem("blank"), r.sem2("xb")
        x_in, ctx_in, xn_done, kheads_in = (r.sem2(n) for n in ("x_in", "ctx_in", "xn", "kheads"))
        front_full, back_full = r.sem("front_full"), r.sem("back_full")
        K_AT, T_AT, Q_AT, V_AT, FRONT = 1, 2, 3, 4, 5
        k_done, q_done, v_done, out_done = (r.sem2(n) for n in ("k", "q", "v", "out"))
        headsT_done, xnT_done = r.sem("headsT"), r.sem("xnT")
        scores_done = r.sem("scores")
        low_done, prob_done, turned = (r.sem2(n) for n in ("low", "prob", "turned"))
        probT_done, values_done, heads_done = (r.sem(n) for n in ("probT", "values", "heads"))
        stored, peak_step = r.sem2("stored"), r.sem("peak_step")
        STEPS = 2 * TILES
        consts = ((ident, "ident"), (wq, "wq"), (wk, "wk"), (wv, "wv"), (wp, "wp"), (bq, "bq"), (bk, "bk"), (bv, "bv"), (bp, "bp"))
        block = ctx.enter_context(nc.Block())

        @block.sync
        def _(sp):
            r.start_at_one(sp)
            for dst, src in consts:
                sp.dma_start(whole(dst), a[src]).then_inc(const_in, 16)

            def load(j, k):
                g = 2 * j + k
                sp.wait_ge(v_done[k], ONE + 2 * j)
                apart(sp)
                sp.dma_start(ctxT[k][:, :], a["ctxT"][:, bass.ds(g * GROUP, GROUP)]).then_inc(ctx_in[k], 16)
                sp.wait_ge(xn_done[k], ONE + j)
                apart(sp)
                sp.wait_ge(xb_done[k], ONE + j)
                apart(sp)
                sp.dma_start(x[k][:, :, :], tiles_of(s["x2"], g)).then_inc(x_in[k], 16)

            def spread_keys(j, k, fresh=False):
                sp.wait_ge(k_done[k], ONE + j + 1)
                apart(sp)
                if not fresh:
                    sp.wait_ge(scores_done, ONE + TILES * (2 * j + k - 1))
                    apart(sp)
                for h in range(H1):
                    sp.dma_start(kheads[k][h * DH1:(h + 1) * DH1, :, h, :],
                                 kT[h * DH1:(h + 1) * DH1, :].rearrange("d (b t) -> d b t", b=GB)).then_inc(kheads_in[k], 16)

            def store(j, k):
                sp.wait_ge(out_done[k], ONE + j + 1)
                apart(sp)
                rows = s["x3"].rearrange("(e b c) d -> b e c d", e=E1, b=B)
                for b in range(GB):
                    i, b2 = b // 2, b % 2
                    sp.dma_start(rows[bass.ds((2 * j + k) * GB + b, 1)].rearrange("b e c d -> (b e) c d"),
                                 out[k][b2 * S:(b2 + 1) * S, i, :]).then_inc(stored[k], 16)

            def step(j, k, first, last):
                if not last:
                    load(*following(j, k))
                    spread_keys(*following(j, k), first)
                if not first:
                    store(*before(j, k))

            load(0, 0)
            sp.wait_ge(blank, ONE + 8)
            spread_keys(0, 0, True)
            over_groups(sp, step)
            store(GROUPS // 2 - 1, 1)
            for k in range(2):
                sp.wait_ge(stored[k], ONE + 16 * GB * (GROUPS // 2))

        @block.gpsimd
        def _(pool):
            def front(j, k):
                ln.root(pool, 2 * j + k, k)
                pool.wait_ge(x_in[k], ONE + 16 * (j + 1))
                pool.wait_ge(out_done[k], ONE + j)
                pool.tensor_tensor(xb[k][:, :, :], x[k][:, :, :], bp[:, :].unsqueeze(1).to_broadcast([P, TILES, D]),
                                   ALU.add).then_inc(xb_done[k], 1)

            def step(j, k, first, last):
                if not last:
                    front(*following(j, k))

            ln.power_const(pool)
            for k in range(2):
                pool.memset(kheads[k][:, :, :, :], 0.0).then_inc(blank, 1)
                pool.memset(vheads[k][:, :, :, :, :], 0.0).then_inc(blank, 1)
            pool.wait_ge(blank, ONE + 4)
            for k in range(2):
                for n in range(2):
                    pool.memset(vheads[k][n * S:(n + 1) * S, :, :, n, DH1:VW1], 1.0).then_inc(blank, 1)
                    pool.wait_ge(blank, ONE + 5 + 2 * k + n)
            pool.wait_ge(const_in, ONE + 16 * len(consts))
            front(0, 0)
            over_groups(pool, step)

        @block.tensor
        def _(pe):
            def k_(j, k):
                pe.wait_ge(ctx_in[k], ONE + 16 * (j + 1))
                pe.matmul(psM[:, :], wk[:, :], ctxT[k][:, :], start=True, stop=True).then_inc(front_full, 1)

            def turn(j, k):
                pe.wait_ge(xn_done[k], ONE + j + 1)
                for t in range(TILES):
                    ins = pe.transpose(psM[:, t * P:(t + 1) * P], xn[:, t, :], ident[:, :])
                ins.then_inc(front_full, 1)

            def q_(j, k):
                pe.wait_ge(xnT_done, ONE + 2 * j + k + 1)
                pe.matmul(psM[:, :], wq[:, :], xnT[:, :], start=True, stop=True).then_inc(front_full, 1)

            def v_(j, k, n):
                if n:
                    pe.wait_ge(v_done[k], ONE + 2 * j + n)
                else:
                    pe.wait_ge(q_done[k], ONE + j + 1)
                for b in range(4):
                    rows = ctxT[k][:, (4 * n + b) * S:(4 * n + b + 1) * S]
                    for half in range(2):
                        ins = pe.matmul(psM[half * S:(half + 1) * S, b * D:(b + 1) * D], rows, wv[:, :], start=True, stop=True)
                ins.then_inc(front_full, 1)

            def turn_heads(j, k):
                pe.wait_ge(heads_done, ONE + 4 * (2 * j + k) + 4)
                for t in range(TILES):
                    ins = pe.transpose(psM[:, t * P:(t + 1) * P], heads[:, t, :], ident[:, :])
                ins.then_inc(back_full, 1)

            def project(j, k):
                pe.wait_ge(headsT_done, ONE + 2 * j + k + 1)
                for t in range(TILES):
                    ins = pe.matmul(psM[:, t * D:(t + 1) * D], headsT[:, t * P:(t + 1) * P], wp[:, :], start=True, stop=True)
                ins.then_inc(back_full, 1)

            def scores(j, k, i):
                g, c = 2 * j + k, i % 2
                pe.wait_ge(low_done[c], ONE + 2 * g + i // 2)
                for h in range(2):
                    for b2 in range(2):
                        b = 2 * i + b2
                        ins = pe.matmul(psS[c][b2 * S:(b2 + 1) * S, h * 512:(h + 1) * 512], qT[k][:, b * S:(b + 1) * S],
                                        kheads[k][:, b, h * HP1:(h + 1) * HP1, :].rearrange("p h t -> p (h t)"), start=True, stop=True)
                ins.then_inc(scores_done, 1)

            def turn_prob(j, k, i):
                g, c = 2 * j + k, i % 2
                pe.wait_ge(prob_done[c], ONE + 2 * g + i // 2 + 1)
                pe.wait_ge(probT_done, ONE + 4 * g + i)
                for m in range(HP1):
                    ins = pe.transpose(psP[:, m, :], prob[c][:, m * P:(m + 1) * P], ident[:, :])
                ins.then_inc(turned[c], 1)

            def values(j, k, i):
                g, c = 2 * j + k, i % 2
                pe.wait_ge(probT_done, ONE + 4 * g + i + 1)
                pe.wait_ge(heads_done, ONE + 4 * g + i)
                for m in range(HP1):
                    for b2 in range(2):
                        ins = pe.matmul(psO[b2 * S:(b2 + 1) * S, m * 2 * VW1:(m + 1) * 2 * VW1], probT[c][:, m, b2 * S:(b2 + 1) * S],
                                        vheads[k][:, 2 * i + b2, m, :, :].rearrange("p n w -> p (n w)"), start=True, stop=True)
                ins.then_inc(values_done, 1)

            def step(j, k, first, last):
                prev, nxt = before(j, k), following(j, k)
                pe.wait_ge(v_done[k], ONE + 2 * (j + 1))
                if not first:
                    turn_prob(*prev, TILES - 1)
                pe.wait_ge(kheads_in[k], ONE + 16 * H1 * (j + 1))
                pe.wait_ge(q_done[k], ONE + j + 1)
                scores(j, k, 0)
                if not first:
                    values(*prev, TILES - 1)
                if not last:
                    k_(*nxt)
                scores(j, k, 1)
                if not last:
                    pe.wait_ge(k_done[nxt[1]], ONE + nxt[0] + 1)
                if not first:
                    turn_heads(*prev)
                turn_prob(j, k, 0)
                scores(j, k, 2)
                if not first:
                    project(*prev)
                values(j, k, 0)
                if not last:
                    if not first:
                        pe.wait_ge(out_done[prev[1]], ONE + prev[0] + 1)
                    turn(*nxt)
                turn_prob(j, k, 1)
                scores(j, k, 3)
                if not last:
                    q_(*nxt)
                values(j, k, 1)
                if not last:
                    v_(*nxt, 0)
                turn_prob(j, k, 2)
                if not last:
                    v_(*nxt, 1)
                values(j, k, 2)

            pe.wait_ge(const_in, ONE + 16 * len(consts))
            pe.wait_ge(blank, ONE + 8)
            k_(0, 0)
            pe.wait_ge(k_done[0], ONE + 1)
            turn(0, 0)
            q_(0, 0)
            v_(0, 0, 0)
            v_(0, 0, 1)
            over_groups(pe, step)
            turn_prob(GROUPS // 2 - 1, 1, TILES - 1)
            values(GROUPS // 2 - 1, 1, TILES - 1)
            pe.wait_ge(out_done[0], ONE + GROUPS // 2)
            turn_heads(GROUPS // 2 - 1, 1)
            project(GROUPS // 2 - 1, 1)

        @block.scalar
        def _(act):
            def k_out(j, k):
                act.wait_ge(front_full, ONE + (2 * j + k) * FRONT + K_AT)
                act.wait_ge(kheads_in[1 - k], ONE + 16 * H1 * (j + k))
                act.activation(kT[:, :], psM[:, :], ACT.Identity, bias=bk[:, 0:1]).then_inc(k_done[k], 1)

            def xnT_out(j, k):
                act.wait_ge(front_full, ONE + (2 * j + k) * FRONT + T_AT)
                act.activation(xnT[:, :], psM[:, :], ACT.Copy).then_inc(xnT_done, 1)

            def q_out(j, k):
                act.wait_ge(front_full, ONE + (2 * j + k) * FRONT + Q_AT)
                act.activation(qT[k][:, :], psM[:, :], ACT.Identity, bias=bqs[:, 0:1], scale=SCALE1).then_inc(q_done[k], 1)

            def probs(j, k, i):
                c, n = i % 2, 2 * (2 * j + k) + i // 2
                act.wait_ge(low_done[c], ONE + n + 1)
                act.wait_ge(turned[c], ONE + n)
                act.activation(prob[c][:, :], low[c][:, :], ACT.Exp).then_inc(prob_done[c], 1)

            def probT_out(j, k, i):
                g, c = 2 * j + k, i % 2
                act.wait_ge(turned[c], ONE + 2 * g + i // 2 + 1)
                if i:
                    act.wait_ge(values_done, ONE + 4 * g + i - 1)
                else:
                    act.wait_ge(values_done, ONE + 4 * g)
                act.activation(probT[c][:, :, :], psP[:, :, :], ACT.Copy).then_inc(probT_done, 1)

            def headsT_out(j, k):
                act.wait_ge(back_full, ONE + 2 * (2 * j + k) + 1)
                act.activation(headsT[:, :], psM[:, :], ACT.Copy).then_inc(headsT_done, 1)

            def step(j, k, first, last):
                prev, nxt = before(j, k), following(j, k)
                if not first:
                    probT_out(*prev, TILES - 1)
                probs(j, k, 0)
                if not last:
                    k_out(*nxt)
                probs(j, k, 1)
                if not first:
                    headsT_out(*prev)
                probT_out(j, k, 0)
                probs(j, k, 2)
                if not last:
                    xnT_out(*nxt)
                probT_out(j, k, 1)
                probs(j, k, 3)
                if not last:
                    q_out(*nxt)
                probT_out(j, k, 2)

            act.wait_ge(const_in, ONE + 16 * len(consts))
            act.wait_ge(bqs_done, ONE + 1)
            k_out(0, 0)
            xnT_out(0, 0)
            q_out(0, 0)
            over_groups(act, step)
            probT_out(GROUPS // 2 - 1, 1, TILES - 1)
            headsT_out(GROUPS // 2 - 1, 1)

        @block.vector
        def _(v):
            top = Steps(v, peak_step)

            def statistics(j, k):
                v.wait_ge(x_in[k], ONE + 16 * (j + 1))
                ln.statistics(v, 2 * j + k, k, x[k])

            def normalise(j, k):
                ln.apply(v, 2 * j + k, k, x[k], xn).then_inc(xn_done[k], 1)

            def v_out(j, k, n):
                v.wait_ge(front_full, ONE + (2 * j + k) * FRONT + V_AT + n)
                for half in range(2):
                    rows = slice(half * S, (half + 1) * S)
                    src = psM[rows, :].rearrange("p (b m n w) -> p b m n w", b=4, m=HP1, n=2)[:, :, :, half, :]
                    b_ = bv[rows, :].rearrange("p (m n w) -> p m n w", m=HP1, n=2)[:, :, half, :]
                    ins = v.tensor_tensor(vheads[k][rows, 4 * n:4 * n + 4, :, half, 0:DH1], src,
                                          b_.unsqueeze(1).to_broadcast([S, 4, HP1, DH1]), ALU.add)
                ins.then_inc(v_done[k], 1)

            def lower(j, k, i):
                g, c = 2 * j + k, i % 2
                sc = psS[c][:, :].rearrange("p (h t) -> p h t", h=H1)
                v.wait_ge(scores_done, ONE + TILES * g + i + 1)
                top(v.tensor_reduce(peak[c][:, :], sc, AX.X, ALU.max))
                v.wait_ge(prob_done[c], ONE + 2 * g + i // 2)
                v.tensor_tensor(low[c][:, :].rearrange("p (h t) -> p h t", h=H1), sc,
                                peak[c][:, :].unsqueeze(2).to_broadcast([P, H1, S]), ALU.subtract).then_inc(low_done[c], 1)

            def heads_out(j, k, i):
                v.wait_ge(values_done, ONE + 4 * (2 * j + k) + i + 1)
                o = psO[:, 0:H1 * VW1].rearrange("p (h w) -> p h w", w=VW1)
                top(v.reciprocal(inv[i % 2][:, :], o[:, :, DH1]))
                v.tensor_tensor(heads[:, i, :].rearrange("p (h w) -> p h w", w=DH1), o[:, :, 0:DH1],
                                inv[i % 2][:, :].unsqueeze(2).to_broadcast([P, H1, DH1]), ALU.mult).then_inc(heads_done, 1)

            def out_(j, k):
                v.wait_ge(back_full, ONE + 2 * (2 * j + k) + 2)
                v.wait_ge(xb_done[k], ONE + j + 1)
                v.wait_ge(stored[k], ONE + 16 * GB * j)
                v.tensor_tensor(out[k][:, :, :], psM[:, :].rearrange("p (t d) -> p t d", t=TILES), xb[k][:, :, :],
                                ALU.add).then_inc(out_done[k], 1)

            def step(j, k, first, last):
                prev, nxt = before(j, k), following(j, k)
                top.at(0 if first else (2 * j + k) * STEPS - 1)
                lower(j, k, 0)
                if not first:
                    heads_out(*prev, TILES - 1)
                lower(j, k, 1)
                if not last:
                    statistics(*nxt)
                if not first:
                    out_(*prev)
                if not last:
                    normalise(*nxt)
                lower(j, k, 2)
                heads_out(j, k, 0)
                lower(j, k, 3)
                heads_out(j, k, 1)
                if not last:
                    v_out(*nxt, 0)
                    v_out(*nxt, 1)
                heads_out(j, k, 2)

            v.wait_ge(const_in, ONE + 16 * len(consts))
            v.tensor_scalar(bqs[:, :], bq[:, :], SCALE1, None, ALU.mult).then_inc(bqs_done, 1)
            v.wait_ge(blank, ONE + 8)
            statistics(0, 0)
            normalise(0, 0)
            v_out(0, 0, 0)
            v_out(0, 0, 1)
            over_groups(v, step)
            top.at(GROUPS * STEPS - 1)
            heads_out(GROUPS // 2 - 1, 1, TILES - 1)
            out_(GROUPS // 2 - 1, 1)


def phase_ffn(nc, sems, a, s):
    UNITS = 2 * E1
    NC = len(CHUNKS1)
    with ExitStack() as ctx:
        r = Room(nc, ctx, sems, "ffn")
        ident = r.sb("ident", [P, P])
        w1 = [r.sb(f"w1{w}", [D, FF1]) for w in range(2)]
        w3 = [r.sb(f"w3{w}", [D, FF1]) for w in range(2)]
        w2 = [r.sb(f"w2{w}", [P, NC, D]) for w in range(2)]
        x = [r.sb(f"x{q}", [P, TILES, D]) for q in range(4)]
        out = [r.sb(f"out{k}", [P, TILES, D]) for k in range(2)]
        xn, xnT = r.sb("xn", [P, TILES, D]), [r.sb(f"xnT{k}", [D, GROUP]) for k in range(2)]
        ln = LayerNorm(r)
        act_g = [r.sb(f"act_g{c}", [P, GROUP]) for c in range(2)]
        hT = [[r.sb(f"hT{k}{c}", [P, GROUP]) for c in range(NC)] for k in range(2)]
        psT = r.ps("psT", [P, GROUP])
        psG = [r.ps(f"psG{c}", [P, GROUP]) for c in range(2)]
        psU = [r.ps(f"psU{c}", [P, GROUP]) for c in range(2)]
        psY = [r.ps(f"psY{k}", [P, TILES, D]) for k in range(2)]
        const_in, w_in, x_in = r.sem("const_in"), r.sem2("w_in"), [r.sem(f"x_in{q}") for q in range(4)]
        xn_done, turned, xnT_done = r.sem2("xn"), r.sem("turned"), r.sem2("xnT")
        up_done, silu_done, h_done = r.sem("up"), r.sem("silu"), r.sem("h")
        y_done, out_done, stored = r.sem2("y"), r.sem2("out"), r.sem2("stored")
        block = ctx.enter_context(nc.Block())

        def ahead(j, q, n):
            return (j, q + n) if q + n < 4 else (j + 1, q + n - 4)

        def before_unit(j, q):
            return (j, q - 1) if q else (j - 1, 3)

        def over_units(eng, step):
            step(0, 0, True, 3)
            with eng.Fori(0, UNITS // 4 - 1) as j:
                for q in range(1, 4):
                    step(j, q, False, 3)
                step(j + 1, 0, False, 3)
            for q in range(1, 4):
                step(UNITS // 4 - 1, q, False, 3 - q)

        @block.sync
        def _(sp):
            r.start_at_one(sp)
            sp.dma_start(ident[:, :], a["ident"]).then_inc(const_in, 16)

            def load(j, q):
                sp.dma_start(x[q][:, :, :], tiles_of(s["x3"], 4 * j + q)).then_inc(x_in[q], 16)

            def load_weights(j, w):
                e = 2 * j + w
                sp.wait_ge(y_done[1], ONE + e - 1)
                apart(sp)
                sp.dma_start(w1[w][:, :], a["f1"][bass.ds(e, 1)].rearrange("e d f -> (e d) f")).then_inc(w_in[w], 16)
                sp.dma_start(w3[w][:, :], a["f3"][bass.ds(e, 1)].rearrange("e d f -> (e d) f")).then_inc(w_in[w], 16)
                sp.dma_start(w2[w][:, :, :], a["f2"][bass.ds(e, 1)].rearrange("e p c d -> (e p) c d")).then_inc(w_in[w], 16)

            def store(j, q):
                k = q % 2
                sp.wait_ge(out_done[k], ONE + 2 * j + q // 2 + 1)
                apart(sp)
                sp.dma_start(tiles_of(s["out"], 4 * j + q), out[k][:, :, :]).then_inc(stored[k], 16)

            def step(j, q, first, left):
                if not first:
                    store(*before_unit(j, q))
                if left >= 3:
                    load(*ahead(j, q, 3))
                if q == 0 or q == 2 and left >= 3:
                    nj, nq = ahead(j, q, 2)
                    load_weights(nj, nq // 2)

            for q in range(3):
                load(0, q)
            for dst, src in ((w1, "f1"), (w3, "f3")):
                sp.dma_start(dst[0][:, :], a[src][0]).then_inc(w_in[0], 16)
            sp.dma_start(w2[0][:, :, :], a["f2"][0]).then_inc(w_in[0], 16)
            over_units(sp, step)
            store(UNITS // 4 - 1, 3)
            for k in range(2):
                sp.wait_ge(stored[k], ONE + 16 * (UNITS // 2))

        @block.gpsimd
        def _(pool):
            ln.roots(pool, UNITS)

        @block.tensor
        def _(pe):
            def turn(j, q):
                k, m = q % 2, 2 * j + q // 2
                pe.wait_ge(xn_done[k], ONE + m + 1)
                pe.wait_ge(xnT_done[1 - k], ONE + m + k)
                for t in range(TILES):
                    ins = pe.transpose(psT[:, t * P:(t + 1) * P], xn[:, t, :], ident[:, :])
                ins.then_inc(turned, 1)

            def up(j, q, c):
                u, k, w = 4 * j + q, q % 2, q // 2
                g = (NC * q + c) % 2
                f, m = CHUNKS1[c]
                if c:
                    pe.wait_ge(h_done, ONE + NC * u + c - 1)
                else:
                    pe.wait_ge(h_done, ONE + NC * u)
                pe.matmul(psG[g][0:m, :], w1[w][:, f:f + m], xnT[k][:, :], start=True, stop=True)
                pe.matmul(psU[g][0:m, :], w3[w][:, f:f + m], xnT[k][:, :], start=True, stop=True).then_inc(up_done, 1)

            def down(j, q):
                u, k, w = 4 * j + q, q % 2, q // 2
                pe.wait_ge(h_done, ONE + NC * (u + 1))
                pe.wait_ge(out_done[k], ONE + 2 * j + q // 2)
                for t in range(TILES):
                    for c, (f, m) in enumerate(CHUNKS1):
                        ins = pe.matmul(psY[k][:, t, :], hT[k][c][0:m, t * P:(t + 1) * P], w2[w][0:m, c, :],
                                        start=(c == 0), stop=(c == NC - 1))
                ins.then_inc(y_done[k], 1)

            def step(j, q, first, left):
                k, w = q % 2, q // 2
                pe.wait_ge(w_in[w], ONE + 48 * (j + 1))
                pe.wait_ge(xnT_done[k], ONE + 2 * j + q // 2 + 1)
                up(j, q, 0)
                if not first:
                    down(*before_unit(j, q))
                up(j, q, 1)
                if left >= 1:
                    turn(*ahead(j, q, 1))
                up(j, q, 2)

            pe.wait_ge(const_in, ONE + 16)
            turn(0, 0)
            over_units(pe, step)
            down(UNITS // 4 - 1, 3)

        @block.scalar
        def _(act):
            def xnT_out(j, q):
                k, m = q % 2, 2 * j + q // 2
                act.wait_ge(turned, ONE + 4 * j + q + 1)
                act.wait_ge(y_done[k], ONE + m)
                act.activation(xnT[k][:, :], psT[:, :], ACT.Copy).then_inc(xnT_done[k], 1)

            def step(j, q, first, left):
                u = 4 * j + q
                for c, (f, m) in enumerate(CHUNKS1):
                    g = (NC * q + c) % 2
                    act.wait_ge(up_done, ONE + NC * u + c + 1)
                    if c:
                        act.wait_ge(h_done, ONE + NC * u + c - 1)
                    else:
                        act.wait_ge(h_done, ONE + NC * u)
                    act.activation(act_g[g][0:m, :], psG[g][0:m, :], ACT.Silu).then_inc(silu_done, 1)
                    if left >= 1 and c == 1:
                        xnT_out(*ahead(j, q, 1))

            xnT_out(0, 0)
            over_units(act, step)

        @block.vector
        def _(v):
            def statistics(j, q):
                v.wait_ge(x_in[q], ONE + 16 * (j + 1))
                ln.statistics(v, 4 * j + q, q % 2, x[q])

            def normalise(j, q):
                ln.apply(v, 4 * j + q, q % 2, x[q], xn).then_inc(xn_done[q % 2], 1)

            def gated(j, q, c):
                u, k = 4 * j + q, q % 2
                f, m = CHUNKS1[c]
                g = (NC * q + c) % 2
                v.wait_ge(silu_done, ONE + NC * u + c + 1)
                v.tensor_tensor(hT[k][c][0:m, :], act_g[g][0:m, :], psU[g][0:m, :], ALU.mult).then_inc(h_done, 1)

            def out_(j, q):
                k, n = q % 2, 2 * j + q // 2
                v.wait_ge(y_done[k], ONE + n + 1)
                v.wait_ge(stored[k], ONE + 16 * n)
                v.tensor_tensor(out[k][:, :, :], psY[k][:, :, :], x[q][:, :, :], ALU.add).then_inc(out_done[k], 1)

            def step(j, q, first, left):
                v.wait_ge(y_done[q % 2], ONE + 2 * j + q // 2)
                gated(j, q, 0)
                if left >= 1:
                    normalise(*ahead(j, q, 1))
                if not first:
                    out_(*before_unit(j, q))
                gated(j, q, 1)
                gated(j, q, 2)
                if left >= 2:
                    statistics(*ahead(j, q, 2))

            statistics(0, 0)
            normalise(0, 0)
            statistics(0, 1)
            over_units(v, step)
            out_(UNITS // 4 - 1, 3)


SCRATCH = {
    "xnT": ([D, TOKENS], F32),
    "gates": ([B, 2 * H0, S], F32),
    "floor": ([P, PAIRS, H0], F32),
    "m_parts": ([NSPLIT, B, H0 * S], BF16),
    "a_parts": ([NSPLIT, B, H0, S], BF16),
    "x1": ([TOKENS, D], F32),
    "x2": ([TOKENS, D], F32),
    "x3": ([TOKENS, D], F32),
}


def build(nc, a, out):
    s = {n: nc.dram_tensor(f"scratch_{n}", shape, dt).ap() for n, (shape, dt) in SCRATCH.items()}
    s["out"] = out
    with ExitStack() as sems:
        phase_gates(nc, sems, a, s)
        phase_decay(nc, sems, a, s)
        phase_mlstm(nc, sems, a, s)
        phase_experts(nc, sems, a, s)
        phase_attention(nc, sems, a, s)
        phase_ffn(nc, sems, a, s)


def bf16_bits(constant):
    return (constant.view(np.uint32) >> 16).astype(np.uint16)


def layouts(i):
    i = {n: np.asarray(v) for n, v in i.items()}
    ctx = i["ctx_1024"].reshape(TOKENS, D)
    rows = lambda v: np.broadcast_to(v, (P, v.shape[0]))
    gates = [i["L0_xattn_igate_w"], i["L0_xattn_fgate_w"]]
    gate = lambda n: np.concatenate([w[:, n * D:(n + 1) * D].T for w in gates], 1)
    units = lambda w, sw: np.concatenate([i[w], i[sw]], 0)
    ones = np.ones((TOKENS, H0, 1), np.float32)
    t = np.arange(S)
    head_of = np.repeat(np.arange(H0), S)
    keys = np.zeros((DECAY_ROWS, GROUP), np.float32)
    keys[0:S] = np.tile(np.eye(S), (1, GB))
    keys[M_ROW:] = np.tile(np.repeat(np.eye(2), S, 1), (NSPLIT, TILES))
    queries = np.zeros((DECAY_ROWS, TILES, H0 * S), np.float32)
    queries[0:S] = np.where(t[:, None] <= np.tile(t, H0)[None], 0.0, MASKED)[:, None, :]
    queries[A_ROW:M_ROW] = np.tile(np.arange(H0)[:, None] == head_of[None], (NSPLIT, 1))[:, None, :]
    first = np.tile(t == 0, H0)
    f2 = np.zeros((E1, len(CHUNKS1) * P, D), np.float32)
    f2[:, 0:FF1] = i["L1_ffn_w2"]
    return {
        "x": i["x"].reshape(TOKENS, D),
        "ctxT": ctx.T,
        "ctx_ones": np.concatenate([ctx.reshape(TOKENS, H0, DH0), ones], 2).reshape(TOKENS, H0 * VW0),
        "ident": np.eye(P, dtype=np.float32),
        "gate_wq": gate(0), "gate_wk": gate(1), "gate_wv": gate(2),
        "gate_b": np.concatenate([i["L0_xattn_igate_b"], i["L0_xattn_fgate_b"]])[:, None],
        "scan_keep": rows(np.where(first, 0.0, 1.0).astype(np.float32)),
        "scan_drop": rows(np.where(first, MASKED, 0.0).astype(np.float32)),
        "ln_scale": rows(i["L0_xattn_ln_scale"]),
        "decay_keys": bf16_bits(keys),
        "decay_queries": bf16_bits(queries),
        "router": i["L0_ffn_router_w"].T,
        "router_b": rows(i["L0_ffn_experts_bias"]),
        "iota": rows(np.arange(E0, dtype=np.float32)),
        "w1": units("L0_ffn_w1", "L0_ffn_sw1").transpose(1, 0, 2),
        "w3": units("L0_ffn_w3", "L0_ffn_sw3").transpose(1, 0, 2),
        "w2": units("L0_ffn_w2", "L0_ffn_sw2").reshape(UNITS0 * CH0, P, D).transpose(1, 0, 2),
        "wq": i["L1_xattn_Wq"].T, "wk": i["L1_xattn_Wk"].T, "wv": i["L1_xattn_Wv"].T, "wp": i["L1_xattn_Wp"].T,
        "bq": i["L1_xattn_bq"][:, None], "bk": i["L1_xattn_bk"][:, None],
        "bv": rows(i["L1_xattn_bv"]), "bp": rows(i["L1_xattn_bp"]),
        "f1": i["L1_ffn_w1"], "f3": i["L1_ffn_w3"],
        "f2": f2.reshape(E1, len(CHUNKS1), P, D).transpose(0, 2, 1, 3),
    }


def kernel(**inputs):
    import concourse.bacc as bacc
    from concourse.bass_utils import run_bass_kernel_spmd

    nc = bacc.Bacc("TRN2", target_bir_lowering=False, num_devices=1)
    arrays, aps = {}, {}
    for name, v in layouts(inputs).items():
        arrays[f"in_{name}"] = np.ascontiguousarray(v)
        aps[name] = nc.dram_tensor(f"in_{name}", v.shape, mybir.dt.from_np(v.dtype), kind="ExternalInput").ap()
    out = nc.dram_tensor("out", (TOKENS, D), F32, kind="ExternalOutput").ap()
    build(nc, aps, out)
    got = run_bass_kernel_spmd(nc, [arrays], core_ids=[0]).results[0]["out"]
    return got.reshape(E1, B, C1, D).transpose(1, 0, 2, 3).reshape(B, S, D)
```

```python
from contextlib import ExitStack

import numpy as np

import concourse.bass as bass
from concourse import mybir

F32 = mybir.dt.float32
BF16 = mybir.dt.bfloat16
F16 = mybir.dt.float16
U32 = mybir.dt.uint32
ACT = mybir.ActivationFunctionType
ALU = mybir.AluOpType
AX = mybir.AxisListType

B, S, D = 128, 64, 128
TOKENS = B * S
P = 128
TILES = 4
GROUP = TILES * P
GB = GROUP // S
GROUPS = TOKENS // GROUP
PAIRS = B // 2
LN_EPS = 1e-5

H0 = 8
DH0 = D // H0
HP0 = H0 // 2
VW0 = DH0 + 1
CELL_EPS = 1e-6
NSPLIT = 3
MASKED = -1.0e30
A_ROW = S
M_ROW = A_ROW + NSPLIT * 2 * HP0
DECAY_ROWS = M_ROW + NSPLIT * 2

E0, HID0 = 8, 256
UNITS0 = E0 + 1
CH0 = HID0 // P

W_TOP, X_SCALE = 512.0, 64.0
H_TOP = 60000.0
TINY = 1e-15

H1 = 16
DH1 = D // H1
SCALE1 = float(DH1) ** 0.5
HP1 = H1 // 2
VW1 = DH1 + 1

ONE = 1

E1, FF1 = 8, 352
C1 = S // E1
CHUNKS1 = [(c * P, min(P, FF1 - c * P)) for c in range((FF1 + P - 1) // P)]


class Steps:

    def __init__(self, eng, sem):
        self.eng, self.sem, self.base, self.n = eng, sem, 0, 0

    def at(self, base):
        self.base, self.n = base, 0

    def __call__(self, ins):
        self.n += 1
        ins.then_inc(self.sem, 1)
        self.eng.wait_ge(self.sem, ONE + self.base + self.n)


class Room:

    def __init__(self, nc, ctx, sems, phase):
        self.nc, self.ctx, self.sems, self.phase, self.all_sems = nc, ctx, sems, phase, []

    def sb(self, name, shape, dt=F32):
        return self.ctx.enter_context(self.nc.sbuf_tensor(f"{self.phase}_{name}", shape, dt))

    def ps(self, name, shape):
        return self.ctx.enter_context(self.nc.psum_tensor(f"{self.phase}_{name}", shape, F32))

    def sem(self, name):
        self.all_sems.append(self.sems.enter_context(self.nc.semaphore(f"{self.phase}_{name}")))
        return self.all_sems[-1]

    def start_at_one(self, sp):
        for sem in self.all_sems:
            sp.sem_inc(sem, ONE)

    def sem2(self, name):
        return [self.sem(f"{name}{k}") for k in range(2)]


def apart(eng):
    eng.nop(nofuse=True)


class SplitWeights:

    def __init__(self, nc, ctx, sems):
        r = self.room = Room(nc, ctx, sems, "split")
        N = UNITS0 * HID0
        self.names = ("w1", "w3", "w2")
        self.raw, self.hi, self.lo = ([r.sb(f"{n}_{part}", [P, N], dt) for n in self.names]
                                      for part, dt in (("raw", F32), ("hi", F16), ("lo", F16)))
        self.tops, self.top = r.sb("tops", [P, 3]), r.sb("top", [P, 2])
        self.one, self.scales = r.sb("one", [1, 2]), r.sb("scales", [1, 4])
        self.ones, self.all, self.square = r.sb("ones", [1, P]), r.sb("all", [P, 4]), r.sb("square", [P, 1])
        self.unscale, self.to_hidden, self.y_unscale = (r.sb(n, [P, 1]) for n in ("unscale", "to_hidden", "y_unscale"))
        self.half, self.minus_half = r.sb("half", [P, 1]), r.sb("minus_half", [P, 1])
        self.ident = r.sb("ident", [P, P])
        self.loaded, self.step = r.sem("loaded"), r.sem("step")
        self.fed = r.sem("fed")

    def load(self, sp, a):
        self.room.start_at_one(sp)
        sp.dma_start(self.ident[:, :], a["ident"]).then_inc(self.loaded, 16)
        for w, name in enumerate(self.names):
            sp.dma_start(self.raw[w][:, :], a[name].rearrange("d e f -> d (e f)")).then_inc(self.loaded, 16)

    def prepare_vector(self, v, ps):
        step = Steps(v, self.step)
        step(v.memset(self.ones[:, :], 1.0))
        v.wait_ge(self.loaded, ONE + 16 * 4)
        for w in range(3):
            ins = v.tensor_reduce(self.tops[:, w:w + 1], self.raw[w][:, :], AX.X, ALU.max, apply_absolute_value=True)
        step(ins)
        step(v.tensor_reduce(self.top[:, 0:1], self.tops[:, 0:2], AX.X, ALU.max))
        step(v.tensor_copy(self.top[:, 1:2], self.tops[:, 2:3]))
        v.wait_ge(self.fed, ONE + 1)
        step(v.tensor_reduce(self.one[:, :], ps[0:1, 0:2 * P].rearrange("o (n p) -> o n p", n=2), AX.X, ALU.max))
        step(v.tensor_scalar(self.scales[:, 2:4], self.one[:, :], TINY, 1.0 / W_TOP, ALU.max, ALU.mult))
        step(v.reciprocal(self.scales[:, 0:2], self.scales[:, 2:4]))
        v.wait_ge(self.fed, ONE + 2)
        step(v.tensor_copy(self.all[:, :], ps[:, 0:4]))
        bound = (D * W_TOP) ** 2 / H_TOP
        v.tensor_scalar(self.unscale[:, :], self.all[:, 2:3], 1.0 / X_SCALE, None, ALU.mult)
        v.tensor_scalar(self.to_hidden[:, :], self.all[:, 0:1], 1.0 / (X_SCALE * bound), None, ALU.mult)
        step(v.tensor_tensor(self.square[:, :], self.all[:, 2:3], self.all[:, 2:3], ALU.mult))
        step(v.scalar_tensor_tensor(out=self.y_unscale[:, :], in0=self.square[:, :], scalar=bound, in1=self.all[:, 3:4],
                                    op0=ALU.mult, op1=ALU.mult))
        v.tensor_scalar(self.half[:, :], self.y_unscale[:, :], 0.5, None, ALU.mult)
        v.tensor_scalar(self.minus_half[:, :], self.y_unscale[:, :], -0.5, None, ALU.mult)
        for w in range(3):
            v.wait_ge(self.fed, ONE + 2 + w + 1)
            ins = v.scalar_tensor_tensor(out=self.lo[w][:, :], in0=self.raw[w][:, :], scalar=self.scale_of(w),
                                         in1=self.hi[w][:, :], op0=ALU.mult, op1=ALU.subtract)
        step(ins)

    def prepare_tensor(self, pe, ps):
        pe.wait_ge(self.step, ONE + 4)
        for n in range(2):
            ins = pe.matmul(ps[0:1, n * P:(n + 1) * P], self.top[:, n:n + 1], self.ident[:, :], start=True, stop=True)
        ins.then_inc(self.fed, 1)
        pe.wait_ge(self.step, ONE + 7)
        pe.matmul(ps[:, 0:4], self.ones[:, :], self.scales[:, :], start=True, stop=True).then_inc(self.fed, 1)
        pe.wait_ge(self.step, ONE + 8)

    def prepare_scalar(self, act):
        act.wait_ge(self.step, ONE + 8)
        for w in range(3):
            act.activation(self.hi[w][:, :], self.raw[w][:, :], ACT.Identity, scale=self.scale_of(w)).then_inc(self.fed, 1)

    def scale_of(self, w):
        n = 1 if w == 2 else 0
        return self.all[:, n:n + 1]

    def up(self, pe, ps, w, cols, x_hi, x_lo):
        pe.matmul(ps, self.hi[w][:, cols], x_hi, start=True, stop=False)
        pe.matmul(ps, self.hi[w][:, cols], x_lo, start=False, stop=False)
        return pe.matmul(ps, self.lo[w][:, cols], x_hi, start=False, stop=True)

    def down(self, pe, ps, chunk, h_hi, h_lo, first, last):
        cols = slice(chunk * D, (chunk + 1) * D)
        pe.matmul(ps, h_hi, self.hi[2][:, cols], start=first, stop=False)
        pe.matmul(ps, h_hi, self.lo[2][:, cols], start=False, stop=False)
        return pe.matmul(ps, h_lo, self.hi[2][:, cols], start=False, stop=last)


class HeadBuffers:

    def __init__(self, nc, ctx, sems):
        r = self.room = Room(nc, ctx, sems, "heads")
        self.keys0 = [r.sb(f"keys0{k}", [D, GB, 2, S]) for k in range(2)]
        self.queries0 = [r.sb(f"queries0{k}", [D, GB, HP0, S]) for k in range(2)]
        self.queries1 = [r.sb(f"queries1{k}", [D, GB, 2, S]) for k in range(2)]
        self.keys1 = [r.sb(f"keys1{k}", [D, GB, HP1, S]) for k in range(2)]
        self.vheads = [r.sb(f"vheads{k}", [P, GB, HP1, 2, VW1]) for k in range(2)]

    def clear(self, pool, blank):
        for k in range(2):
            pool.memset(self.vheads[k][:, :, :, :, :], 0.0).then_inc(blank, 1)
        pool.wait_ge(blank, ONE + 2)
        for k in range(2):
            for n in range(2):
                pool.memset(self.vheads[k][n * S:(n + 1) * S, :, :, n, DH1:VW1], 1.0).then_inc(blank, 1)
                pool.wait_ge(blank, ONE + 3 + 2 * k + n)
        for k in range(2):
            for t in (self.keys0[k], self.queries0[k], self.queries1[k], self.keys1[k]):
                pool.memset(t[:, :, :, :], 0.0).then_inc(blank, 1)
        pool.wait_ge(blank, ONE + 14)


class LayerNorm:

    def __init__(self, r):
        self.sums = [r.sb(f"sums{k}", [P, TILES, 6]) for k in range(2)]
        self.mv = [r.sb(f"mv{k}", [P, TILES, 2]) for k in range(2)]
        self.rstd = [r.sb(f"rstd{k}", [P, TILES]) for k in range(2)]
        self.shifted = [r.sb(f"shifted{k}", [P, TILES]) for k in range(2)]
        self.power = r.sb("power", [P, TILES])
        self.shifted_done, self.sums_done = r.sem("shifted_done"), r.sem("sums_done")
        self.var_done, self.rstd_done = r.sem("var_done"), r.sem("rstd_done")

    def statistics(self, v, n, k, x):
        for t in range(TILES):
            ins = v.bn_stats(self.sums[k][:, t, :], x[:, t, :])
        ins.then_inc(self.sums_done, 1)
        v.wait_ge(self.sums_done, ONE + n + 1)
        apart(v)
        for t in range(TILES):
            ins = v.bn_aggr(self.mv[k][:, t, :], self.sums[k][:, t, :])
        ins.then_inc(self.var_done, 1)

    def apply(self, v, n, k, x, y):
        v.wait_ge(self.rstd_done, ONE + n + 1)
        for t in range(TILES):
            ins = v.tensor_scalar(y[:, t, :], x[:, t, :], self.mv[k][:, t, 0:1], self.rstd[k][:, t:t + 1],
                                  ALU.subtract, ALU.mult)
        return ins

    def power_const(self, pool):
        pool.memset(self.power[:, :], -0.5).then_inc(self.shifted_done, 1)

    def root(self, pool, n, k):
        pool.wait_ge(self.var_done, ONE + n + 1)
        pool.wait_ge(self.rstd_done, ONE + n)
        apart(pool)
        pool.tensor_scalar(self.shifted[k][:, :], self.mv[k][:, :, 1], LN_EPS, None, ALU.add).then_inc(self.shifted_done, 1)
        pool.wait_ge(self.shifted_done, ONE + n + 2)
        pool.tensor_tensor(self.rstd[k][:, :], self.shifted[k][:, :], self.power[:, :], ALU.pow).then_inc(self.rstd_done, 1)

    def roots(self, pool, groups):
        self.power_const(pool)
        with pool.Fori(0, groups // 2) as j:
            for k in range(2):
                self.root(pool, 2 * j + k, k)


def following(j, k):
    return (j, 1) if k == 0 else (j + 1, 0)


def before(j, k):
    return (j - 1, 1) if k == 0 else (j, 0)


def over_groups(eng, step, n=GROUPS):
    step(0, 0, True, False)
    with eng.Fori(0, n // 2 - 1) as j:
        step(j, 1, False, False)
        step(j + 1, 0, False, False)
    step(n // 2 - 1, 1, False, True)


def ahead(j, q, n):
    return (j, q + n) if q + n < 4 else (j + 1, q + n - 4)


def before_it(j, q):
    return (j, q - 1) if q else (j - 1, 3)


def over_fours(eng, step, n=GROUPS):
    step(0, 0, True, 3)
    with eng.Fori(0, n // 4 - 1) as j:
        for q in range(1, 4):
            step(j, q, False, 3)
        step(j + 1, 0, False, 3)
    for q in range(1, 4):
        step(n // 4 - 1, q, False, 3 - q)


def whole(t):
    return t[(slice(None),) * len(t.shape)]


def tiles_of(dram, g):
    return dram[bass.ds(g * GROUP, GROUP), :].rearrange("(t p) d -> p t d", p=P)


def phase_gates(nc, sems, a, s):
    with ExitStack() as ctx:
        r = Room(nc, ctx, sems, "gates")
        ident = r.sb("ident", [P, P])
        wq, wk, wv, wkv = (r.sb(n, [D, 2 * H0]) for n in ("wq", "wk", "wv", "wkv"))
        bias = r.sb("bias", [2 * H0, 1])
        x = [r.sb(f"x{q}", [P, TILES, D]) for q in range(4)]
        ctxT = [r.sb(f"ctxT{k}", [D, GROUP]) for k in range(2)]
        xn = [r.sb(f"xn{k}", [P, TILES, D]) for k in range(2)]
        xnT = [r.sb(f"xnT{k}", [D, GROUP]) for k in range(2)]
        rows = [r.sb(f"rows{k}", [2 * H0, GROUP]) for k in range(2)]
        ln = LayerNorm(r)
        psT = [r.ps(f"psT{k}", [P, GROUP]) for k in range(2)]
        psG = [r.ps(f"psG{k}", [P, GROUP]) for k in range(2)]
        const_in = r.sem("const_in")
        x_in, ctx_in = [r.sem(f"x_in{q}") for q in range(4)], r.sem2("ctx_in")
        xn_done, turned, summed = r.sem2("xn_done"), r.sem2("turned"), r.sem2("summed")
        copied = r.sem2("copied")
        xnT_stored, rows_stored = r.sem2("xnT_stored"), r.sem2("rows_stored")
        consts = ((ident, "ident"), (wq, "gate_wq"), (wk, "gate_wk"), (wv, "gate_wv"), (bias, "gate_b"))
        block = ctx.enter_context(nc.Block())

        @block.sync
        def _(sp):
            r.start_at_one(sp)

            def load_x(j, q):
                sp.dma_start(x[q][:, :, :], tiles_of(a["x"], 4 * j + q)).then_inc(x_in[q], 16)

            def load_ctx(j, q):
                k = q % 2
                sp.wait_ge(summed[k], ONE + 2 * j + q // 2)
                apart(sp)
                sp.dma_start(ctxT[k][:, :], a["ctxT"][:, bass.ds((4 * j + q) * GROUP, GROUP)]).then_inc(ctx_in[k], 16)

            def step(j, q, first, left):
                if left >= 3:
                    if not first:
                        bj, bq = before_it(j, q)
                        sp.wait_ge(xn_done[bq % 2], ONE + 2 * bj + bq // 2 + 1)
                        apart(sp)
                    load_x(*ahead(j, q, 3))
                if left >= 1:
                    load_ctx(*ahead(j, q, 1))

            load_x(0, 0)
            for dst, src in consts:
                sp.dma_start(dst[:, :], a[src]).then_inc(const_in, 16)
            load_x(0, 1)
            load_ctx(0, 0)
            load_x(0, 2)
            over_fours(sp, step)

        @block.vector
        def _(v):
            def statistics(j, q):
                v.wait_ge(x_in[q], ONE + 16 * j + 16)
                ln.statistics(v, 4 * j + q, q % 2, x[q])

            def step(j, q, first, left):
                k = q % 2
                if left >= 1:
                    statistics(*ahead(j, q, 1))
                v.wait_ge(turned[k], ONE + 2 * j + q // 2)
                ln.apply(v, 4 * j + q, k, x[q], xn[k]).then_inc(xn_done[k], 1)

            statistics(0, 0)
            v.wait_ge(const_in, ONE + 16 * len(consts))
            v.tensor_tensor(wkv[:, :], wk[:, :], wv[:, :], ALU.add).then_inc(const_in, 1)
            over_fours(v, step)

        @block.tensor
        def _(pe):
            def turn(j, k):
                pe.wait_ge(xn_done[k], ONE + j + 1)
                pe.wait_ge(copied[k], ONE + 2 * j)
                for t in range(TILES):
                    ins = pe.transpose(psT[k][:, t * P:(t + 1) * P], xn[k][:, t, :], ident[:, :])
                ins.then_inc(turned[k], 1)

            def step(j, k, first, last):
                pe.wait_ge(ctx_in[k], ONE + 16 * j + 16)
                pe.wait_ge(copied[k], ONE + 2 * j)
                pe.matmul(psG[k][0:2 * H0, :], wkv[:, :], ctxT[k][:, :], start=True, stop=False)
                if not last:
                    turn(*following(j, k))
                pe.wait_ge(copied[k], ONE + 2 * j + 1)
                pe.matmul(psG[k][0:2 * H0, :], wq[:, :], xnT[k][:, :], start=False, stop=True).then_inc(summed[k], 1)

            pe.wait_ge(const_in, ONE + 16 * len(consts) + 1)
            turn(0, 0)
            over_groups(pe, step)

        @block.scalar
        def _(act):
            def xnT_out(j, k):
                act.wait_ge(xnT_stored[k], ONE + 16 * j)
                act.wait_ge(turned[k], ONE + j + 1)
                act.activation(xnT[k][:, :], psT[k][:, :], ACT.Copy).then_inc(copied[k], 1)
                act.wait_ge(copied[k], ONE + 2 * j + 1)
                act.dma_start(s["xnT"][:, bass.ds((2 * j + k) * GROUP, GROUP)], xnT[k][:, :]).then_inc(xnT_stored[k], 16)

            def step(j, k, first, last):
                if not last:
                    xnT_out(*following(j, k))
                act.wait_ge(rows_stored[k], ONE + 16 * j)
                act.wait_ge(summed[k], ONE + j + 1)
                act.activation(rows[k][:, :], psG[k][0:2 * H0, :], ACT.Identity, bias=bias[:, 0:1]).then_inc(copied[k], 1)
                act.wait_ge(copied[k], ONE + 2 * j + 2)
                act.dma_start(s["gates"][bass.ds((2 * j + k) * GB, GB)].rearrange("b h t -> h b t"),
                              rows[k][:, :].rearrange("h (b t) -> h b t", b=GB)).then_inc(rows_stored[k], 16)

            act.wait_ge(const_in, ONE + 16 * len(consts))
            xnT_out(0, 0)
            over_groups(act, step)
            for k in range(2):
                act.wait_ge(xnT_stored[k], ONE + 16 * (GROUPS // 2))
                act.wait_ge(rows_stored[k], ONE + 16 * (GROUPS // 2))

        @block.gpsimd
        def _(pool):
            ln.roots(pool, GROUPS)


def phase_decay(nc, sems, a, s, split, heads):
    N = H0 * S
    with ExitStack() as ctx:
        r = Room(nc, ctx, sems, "decay")
        ident = r.sb("ident", [P, P])
        keep, drop = r.sb("keep", [B, N]), r.sb("drop", [B, N])
        gates = r.sb("gates", [B, 2 * N])
        ig, fg = gates[:, 0:N], gates[:, N:2 * N]
        t1, t2, t3 = (r.sb(n, [B, N]) for n in ("t1", "t2", "t3"))
        logf, cs, am, peak, neg_max, neg_peak = (r.sb(n, [B, N]) for n in ("logf", "cs", "am", "peak", "nmax", "npeak"))
        m_parts = r.sb("m_parts", [B, NSPLIT, N], BF16)
        a_parts = r.sb("a_parts", [B, NSPLIT, N], BF16)
        rest = r.sb("rest", [B, N])
        floor = r.sb("floor", [P, PAIRS, H0])
        psE = r.ps("psE", [P, H0 * PAIRS])
        loaded, dve_step, dve_done, act_step = r.sem("loaded"), r.sem("dve_step"), r.sem("dve_done"), r.sem("act_step")
        turned, floor_done = r.sem("turned"), r.sem("floor_done")
        parts_done, stored = r.sem("parts_done"), r.sem("stored")
        blank = r.sem("blank")
        block = ctx.enter_context(nc.Block())

        @block.gpsimd
        def _(pool):
            heads.clear(pool, blank)

        @block.sync
        def _(sp):
            r.start_at_one(sp)
            sp.dma_start(gates[:, :], s["gates"].rearrange("b h t -> b (h t)")).then_inc(loaded, 16)
            sp.dma_start(keep[:, :], a["scan_keep"]).then_inc(loaded, 16)
            sp.dma_start(drop[:, :], a["scan_drop"]).then_inc(loaded, 16)
            sp.dma_start(ident[:, :], a["ident"]).then_inc(loaded, 16)
            split.load(sp, a)
            sp.wait_ge(floor_done, ONE + 1)
            sp.dma_start(s["floor"], floor[:, :, :]).then_inc(stored, 16)
            sp.wait_ge(parts_done, ONE + 2)
            for n in range(NSPLIT):
                for c in range(2):
                    at = (2 * n + c) * HP0
                    sp.dma_start(s["a_rows"][at:at + HP0, :].rearrange("m (i z) -> i m z", z=P),
                                 a_parts[c::2, n, :].rearrange("i (m z) -> i m z", z=P)).then_inc(stored, 16)
                    sp.dma_start(s["m_rows"][2 * n + c].rearrange("(b m t) -> b m t", m=HP0, t=S),
                                 m_parts[:, n, :].rearrange("b (m h t) -> b m h t", m=HP0, h=2)[:, :, c, :]).then_inc(stored, 16)
            sp.wait_ge(stored, ONE + 16 * (1 + 4 * NSPLIT))

        @block.vector
        def _(v):
            step = Steps(v, dve_step)
            v.wait_ge(loaded, ONE + 64)
            v.scalar_tensor_tensor(out=t1[:, :], in0=fg, scalar=-1.0, in1=fg, op0=ALU.mult, op1=ALU.max).then_inc(dve_done, 1)
            v.wait_ge(act_step, ONE + 1)
            v.tensor_scalar(t3[:, :], t2[:, :], 1.0, None, ALU.add).then_inc(dve_done, 1)
            v.wait_ge(act_step, ONE + 2)
            step(v.scalar_tensor_tensor(out=logf[:, :], in0=fg, scalar=0.0, in1=t1[:, :], op0=ALU.min, op1=ALU.subtract))
            step(v.tensor_tensor_scan(cs[:, :], keep[:, :], logf[:, :], 0.0, ALU.mult, ALU.add))
            step(v.tensor_tensor(am[:, :], ig, cs[:, :], ALU.subtract))
            step(v.tensor_tensor_scan(peak[:, :], drop[:, :], am[:, :], 0.0, ALU.add, ALU.max))
            step(v.tensor_scalar(neg_peak[:, :], peak[:, :], -1.0, None, ALU.mult))
            v.tensor_tensor(neg_max[:, :], neg_peak[:, :], cs[:, :], ALU.subtract).then_inc(dve_done, 1)
            for whole, parts in ((neg_peak, m_parts), (am, a_parts)):
                left = whole
                for n in range(NSPLIT):
                    ins = v.tensor_copy(parts[:, n, :], left[:, :])
                    if n == NSPLIT - 1:
                        ins.then_inc(parts_done, 1)
                        v.wait_ge(parts_done, ONE + (1 if parts is m_parts else 2))
                    else:
                        step(ins)
                        step(v.tensor_tensor(rest[:, :], left[:, :], parts[:, n, :], ALU.subtract))
                        left = rest

        @block.scalar
        def _(act):
            act.wait_ge(dve_done, ONE + 1)
            act.activation(t2[:, :], t1[:, :], ACT.Exp, scale=-1.0).then_inc(act_step, 1)
            act.wait_ge(dve_done, ONE + 2)
            act.activation(t1[:, :], t3[:, :], ACT.Ln).then_inc(act_step, 1)
            act.wait_ge(turned, ONE + 1)
            act.activation(floor[:, :, :], psE[:, :].rearrange("p (h i) -> p i h", h=H0), ACT.Exp).then_inc(floor_done, 1)

        @block.tensor
        def _(pe):
            pe.wait_ge(loaded, ONE + 64)
            pe.wait_ge(dve_done, ONE + 3)
            for h in range(H0):
                for b2 in range(2):
                    ins = pe.matmul(psE[b2 * S:(b2 + 1) * S, h * PAIRS:(h + 1) * PAIRS], neg_max[:, h * S:(h + 1) * S],
                                    ident[:, b2::2], start=True, stop=True)
            ins.then_inc(turned, 1)


def phase_mlstm(nc, sems, a, s, split, heads):
    N = H0 * S
    with ExitStack() as ctx:
        r = Room(nc, ctx, sems, "mlstm")
        ln_scale = r.sb("ln_scale", [P, D])
        keys, queries = heads.keys0, heads.queries0
        vals = [r.sb(f"vals{k}", [P, GB, HP0, 2 * VW0]) for k in range(2)]
        x = [r.sb(f"x{k}", [P, TILES, D]) for k in range(2)]
        floor = [r.sb(f"floor{k}", [P, TILES, H0]) for k in range(2)]
        dk = [r.sb(f"dk{k}", [DECAY_ROWS, GROUP], BF16) for k in range(2)]
        dq = [r.sb(f"dq{k}", [DECAY_ROWS, TILES, N], BF16) for k in range(2)]
        decay = [r.sb(f"decay{k}", [P, N]) for k in range(2)]
        cT = [r.sb(f"cT{k}", [P, N]) for k in range(2)]
        norm, inv = r.sb("norm", [P, TILES, H0]), r.sb("inv", [P, TILES, H0])
        h = r.sb("h", [P, TILES, D])
        y, ys = r.sb("y", [P, TILES, D]), r.sb("ys", [P, TILES, D])
        out = [r.sb(f"out{k}", [P, TILES, D]) for k in range(2)]
        ln = LayerNorm(r)
        psA = [r.ps(f"psA{k}", [P, N]) for k in range(2)]
        psS = [r.ps(f"psS{k}", [P, N]) for k in range(2)]
        psV = [[r.ps(f"psV{k}{i}", [P, 512]) for i in range(2)] for k in range(2)]
        const_in = r.sem("const_in")
        pe_in, q_in, tail_in = r.sem2("pe_in"), r.sem2("q_in"), r.sem2("tail_in")
        arg_done, qk_done = r.sem("arg"), r.sem("qk")
        decay_done, cT_done = r.sem2("decay"), r.sem2("cT")
        cT_used = r.sem2("cT_used")
        group_done = r.sem2("group_done")
        h_done, tail_done, stored = (r.sem2(n) for n in ("h_done", "tail", "stored"))
        dve_step = r.sem("dve_step")
        TAIL_STEPS = 6
        block = ctx.enter_context(nc.Block())

        @block.sync
        def _(sp):
            r.start_at_one(sp)
            sp.dma_start(ln_scale[:, :], a["ln_scale"]).then_inc(const_in, 16)
            for k in range(2):
                sp.dma_start(dk[k][:, :], a["decay_keys"].bitcast(BF16)).then_inc(const_in, 16)
                sp.dma_start(dq[k][:, :, :], a["decay_queries"].bitcast(BF16)).then_inc(const_in, 16)
            sp.wait_ge(const_in, ONE + 16 * 5)

            def load(j, k, fresh=False):
                g = 2 * j + k
                if not fresh:
                    sp.wait_ge(qk_done, ONE + TILES * (g - 1))
                    apart(sp)
                for h_ in range(H0):
                    at = (h_ % 2 * HP0 + h_ // 2) * DH0
                    sp.dma_start(queries[k][at:at + DH0, :, h_ // 2, :],
                                 s["xnT"][h_ * DH0:(h_ + 1) * DH0, bass.ds(g * GROUP, GROUP)].rearrange(
                                     "d (b t) -> d b t", b=GB)).then_inc(q_in[k], 16)
                for n in range(2):
                    rows = slice(n * D // 2, (n + 1) * D // 2)
                    sp.dma_start(keys[k][rows, :, n, :], a["ctxT_n"][rows, bass.ds(g * GROUP, GROUP)].rearrange(
                        "d (b t) -> d b t", b=GB)).then_inc(pe_in[k], 16)
                sp.dma_start(dk[k][A_ROW:M_ROW, :], s["a_rows"][:, bass.ds(g * GROUP, GROUP)]).then_inc(pe_in[k], 16)
                sp.dma_start(dq[k][M_ROW:DECAY_ROWS, :, :].rearrange("r i n -> r (i n)"),
                             s["m_rows"][:, bass.ds(g * TILES * N, TILES * N)]).then_inc(pe_in[k], 16)
                sp.wait_ge(group_done[k], ONE + j)
                apart(sp)
                sp.dma_start(vals[k][:, :, :, :], a["values"][:, bass.ds(g * GB, GB)]).then_inc(pe_in[k], 16)
                sp.wait_ge(tail_done[k], ONE + j)
                apart(sp)
                sp.dma_start(x[k][:, :, :], tiles_of(a["x"], g)).then_inc(tail_in[k], 16)
                sp.dma_start(floor[k][:, :, :], s["floor"][:, bass.ds(g * TILES, TILES), :]).then_inc(tail_in[k], 16)

            def store(j, k):
                sp.wait_ge(tail_done[k], ONE + j + 1)
                apart(sp)
                sp.dma_start(tiles_of(s["x1"], 2 * j + k), out[k][:, :, :]).then_inc(stored[k], 16)

            def step(j, k, first, last):
                if not last:
                    load(*following(j, k), first)
                if not first:
                    store(*before(j, k))

            load(0, 0, True)
            over_groups(sp, step)
            store(GROUPS // 2 - 1, 1)
            for k in range(2):
                sp.wait_ge(stored[k], ONE + 16 * (GROUPS // 2))

        @block.gpsimd
        def _(pool):
            ln.roots(pool, GROUPS)

        @block.tensor
        def _(pe):
            def scores(j, k, i):
                c = i % 2
                n = 2 * (2 * j + k) + i // 2
                pe.wait_ge(decay_done[c], ONE + n)
                pe.matmul(psA[c][:, :], dk[k][:, i * P:(i + 1) * P], dq[k][:, i, :], start=True, stop=True).then_inc(arg_done, 1)
                pe.wait_ge(cT_done[c], ONE + n)
                for b2 in range(2):
                    b = 2 * i + b2
                    ins = pe.matmul(psS[c][:, b2 * HP0 * S:(b2 + 1) * HP0 * S], keys[k][:, b, :, :].rearrange("p n t -> p (n t)"),
                                    queries[k][:, b, :, :].rearrange("p m t -> p (m t)"), start=True, stop=True)
                ins.then_inc(qk_done, 1)

            def values(j, k, i):
                c = i % 2
                pe.wait_ge(cT_done[c], ONE + 2 * (2 * j + k) + i // 2 + 1)
                apart(pe)
                for m in range(HP0):
                    for b2 in range(2):
                        at, col = (i % 2) * H0 * VW0 + 2 * m * VW0, (b2 * HP0 + m) * S
                        ins = pe.matmul(psV[k][i // 2][b2 * S:(b2 + 1) * S, at:at + 2 * VW0], cT[c][:, col:col + S],
                                        vals[k][:, 2 * i + b2, m, :], start=True, stop=True)
                ins.then_inc(group_done[k] if i == TILES - 1 else cT_used[c], 1)

            def step(j, k, first, last):
                pe.wait_ge(pe_in[k], ONE + 16 * 5 * (j + 1))
                pe.wait_ge(q_in[k], ONE + 16 * H0 * (j + 1))
                scores(j, k, 0)
                if not first:
                    values(*before(j, k), TILES - 1)
                scores(j, k, 1)
                pe.wait_ge(h_done[k], ONE + j)
                for i in range(2, TILES):
                    values(j, k, i - 2)
                    scores(j, k, i)
                values(j, k, TILES - 2)

            split.prepare_tensor(pe, psS[0])
            over_groups(pe, step)
            values(GROUPS // 2 - 1, 1, TILES - 1)

        @block.scalar
        def _(act):
            split.prepare_scalar(act)
            with act.Fori(0, GROUPS // 2) as j:
                for k in range(2):
                    g = 2 * j + k
                    for i in range(TILES):
                        c, n = i % 2, 2 * g + i // 2
                        act.wait_ge(arg_done, ONE + TILES * g + i + 1)
                        act.wait_ge(cT_done[c], ONE + n)
                        act.activation(decay[c][:, :], psA[c][:, :], ACT.Exp).then_inc(decay_done[c], 1)

        @block.vector
        def _(v):
            steps = Steps(v, dve_step)

            def weigh(j, k, i):
                g, c = 2 * j + k, i % 2
                n = 2 * g + i // 2
                v.wait_ge(qk_done, ONE + TILES * g + i + 1)
                v.wait_ge(decay_done[c], ONE + n + 1)
                if i == 1:
                    v.wait_ge(group_done[1 - k], ONE + j + k)
                elif i == 3:
                    v.wait_ge(cT_used[1], ONE + g + 1)
                else:
                    v.wait_ge(cT_used[0], ONE + n)
                v.scalar_tensor_tensor(out=cT[c][:, :], in0=psS[c][:, :], scalar=float(DH0) ** -0.5,
                                       in1=decay[c][:, :], op0=ALU.mult, op1=ALU.mult).then_inc(cT_done[c], 1)

            def normalise(j, k):
                g = 2 * j + k
                steps.at(g * TAIL_STEPS)
                v.wait_ge(group_done[k], ONE + j + 1)
                v.wait_ge(tail_in[k], ONE + 32 * (j + 1))
                flat = [psV[k][i][:, 0:2 * H0 * VW0].rearrange("p (h w) -> p h w", w=VW0) for i in range(2)]
                halves = [slice(2 * i, 2 * i + 2) for i in range(2)]
                sums = [psV[k][i][:, 0:2 * H0 * VW0].rearrange("p (t h w) -> p t h w", t=2, h=H0)[:, :, :, DH0] for i in range(2)]
                for i in range(2):
                    ins = v.scalar_tensor_tensor(out=norm[:, halves[i], :], in0=sums[i], scalar=-1.0,
                                                 in1=floor[k][:, halves[i], :], op0=ALU.mult, op1=ALU.max)
                steps(ins)
                for i in range(2):
                    ins = v.tensor_tensor(norm[:, halves[i], :], sums[i], norm[:, halves[i], :], ALU.max)
                steps(ins)
                steps(v.tensor_scalar(norm[:, :, :], norm[:, :, :], CELL_EPS, None, ALU.add))
                steps(v.reciprocal(inv[:, :, :], norm[:, :, :]))
                for i in range(2):
                    iv = inv[:, halves[i], :].rearrange("p t h -> p (t h)").unsqueeze(2).to_broadcast([P, 2 * H0, DH0])
                    ins = v.tensor_tensor(h[:, halves[i], :].rearrange("p t (h w) -> p (t h) w", h=H0),
                                          flat[i][:, :, 0:DH0], iv, ALU.mult)
                ins.then_inc(h_done[k], 1)
                v.wait_ge(h_done[k], ONE + j + 1)
                ln.statistics(v, g, k, h)

            def finish(j, k):
                steps(ln.apply(v, 2 * j + k, k, h, y))
                steps(v.tensor_tensor(ys[:, :, :], y[:, :, :], ln_scale[:, :].unsqueeze(1).to_broadcast([P, TILES, D]), ALU.mult))
                v.wait_ge(stored[k], ONE + 16 * j)
                v.tensor_tensor(out[k][:, :, :], x[k][:, :, :], ys[:, :, :], ALU.add).then_inc(tail_done[k], 1)

            def step(j, k, first, last):
                weigh(j, k, 0)
                weigh(j, k, 1)
                if not first:
                    normalise(*before(j, k))
                weigh(j, k, 2)
                if not first:
                    finish(*before(j, k))
                weigh(j, k, 3)

            split.prepare_vector(v, psS[0])
            v.wait_ge(const_in, ONE + 16 * 5)
            over_groups(v, step)
            normalise(GROUPS // 2 - 1, 1)
            finish(GROUPS // 2 - 1, 1)


def phase_experts(nc, sems, a, s, sw):
    with ExitStack() as ctx:
        r = Room(nc, ctx, sems, "experts")
        ident = r.sb("ident", [P, P])
        router, bias, iota = r.sb("router", [D, E0]), r.sb("bias", [P, E0]), r.sb("iota", [P, E0])
        x = [r.sb(f"x{k}", [P, TILES, D]) for k in range(2)]
        xn = [r.sb(f"xn{k}", [P, TILES, D]) for k in range(2)]
        xnT = [r.sb(f"xnT{k}", [D, GROUP]) for k in range(2)]
        x_hi = [r.sb(f"x_hi{k}", [D, GROUP], F16) for k in range(2)]
        x_lo = [r.sb(f"x_lo{k}", [D, GROUP], F16) for k in range(2)]
        ln = LayerNorm(r)
        logits, top = r.sb("logits", [P, TILES, E0]), r.sb("top", [P, TILES, 8])
        where, wheref = r.sb("where", [P, TILES, 8], U32), r.sb("wheref", [P, TILES, 8])
        gap, tanh = r.sb("gap", [P, TILES]), r.sb("tanh", [P, TILES])
        share = r.sb("share", [P, 2, TILES])
        pick = r.sb("pick", [P, 2, TILES, E0])
        cw = [r.sb(f"cw{k}", [P, TILES, E0]) for k in range(2)]
        act_g = [r.sb(f"act_g{c}", [P, GROUP]) for c in range(CH0)]
        hid = [[r.sb(f"hid{u}{c}", [P, GROUP]) for c in range(CH0)] for u in range(2)]
        h_hi = [[r.sb(f"h_hi{u}{c}", [P, GROUP], F16) for c in range(CH0)] for u in range(3)]
        h_lo = [[r.sb(f"h_lo{u}{c}", [P, GROUP], F16) for c in range(CH0)] for u in range(3)]
        psT, psR = r.ps("psT", [P, GROUP]), r.ps("psR", [P, 512])
        psG = [r.ps(f"psG{c}", [P, GROUP]) for c in range(CH0)]
        psU = [r.ps(f"psU{c}", [P, GROUP]) for c in range(CH0)]
        psY = [r.ps(f"psY{u}", [P, TILES, D]) for u in range(2)]
        const_in = r.sem("const_in")
        x_in, xn_done, turned, xnT_done = r.sem2("x_in"), r.sem2("xn"), r.sem("turned"), r.sem2("xnT")
        routed, gap_done, tanh_done = r.sem("routed"), r.sem("gap"), r.sem("tanh")
        up_done, silu_done, h_done, y_done = r.sem("up"), r.sem("silu"), r.sem2("h"), r.sem("y")
        added, stored = r.sem("added"), r.sem2("stored")
        x_lo_done, hi_done, lo_done = r.sem("x_lo"), r.sem2("hi"), r.sem2("lo")
        front_step = r.sem("front_step")
        consts = ((ident, "ident"), (router, "router"), (bias, "router_b"), (iota, "iota"))
        LN_AT, ROUTE_AT = 5, 7
        ROUTE_STEPS = 8
        LAG = 2
        two = lambda k, e: (k * UNITS0 + e) % 2
        three = lambda k, e: (k * UNITS0 + e) % 3

        def lagging(g, k, e):
            return (g, k, e - LAG) if e >= LAG else (g - 1, 1 - k, e - LAG + UNITS0)
        block = ctx.enter_context(nc.Block())

        @block.sync
        def _(sp):
            r.start_at_one(sp)

            def load(j, k):
                sp.wait_ge(stored[k], ONE + 16 * j)
                apart(sp)
                sp.dma_start(x[k][:, :, :], tiles_of(s["x1"], 2 * j + k)).then_inc(x_in[k], 16)

            def step(j, k, first, last):
                if not first:
                    store(*before(j, k))
                if not last:
                    load(*following(j, k))

            def store(j, k):
                sp.wait_ge(added, ONE + (2 * j + k + 1) * UNITS0)
                apart(sp)
                sp.dma_start(tiles_of(s["x2"], 2 * j + k), x[k][:, :, :]).then_inc(stored[k], 16)

            load(0, 0)
            for dst, src in consts:
                sp.dma_start(whole(dst), a[src]).then_inc(const_in, 16)
            over_groups(sp, step)
            store(GROUPS // 2 - 1, 1)
            for k in range(2):
                sp.wait_ge(stored[k], ONE + 16 * (GROUPS // 2))

        @block.gpsimd
        def _(pool):
            def low_part(g, k, e):
                n = g * UNITS0 + e
                for c in range(CH0):
                    pool.wait_ge(hi_done[c], ONE + n + 1)
                    pool.tensor_tensor(h_lo[three(k, e)][c][:, :], hid[two(k, e)][c][:, :], h_hi[three(k, e)][c][:, :],
                                       ALU.subtract).then_inc(lo_done[c], 1)

            def step(j, k, first, last):
                for e in range(UNITS0):
                    low_part(2 * j + k, k, e)
                    if not last and e == LN_AT - 2:
                        nj, nk = following(j, k)
                        ln.root(pool, 2 * nj + nk, nk)

            ln.power_const(pool)
            ln.root(pool, 0, 0)
            over_groups(pool, step)

        @block.tensor
        def _(pe):
            def turn(j, k):
                pe.wait_ge(xn_done[k], ONE + j + 1)
                pe.wait_ge(xnT_done[1 - k], ONE + j + k)
                for t in range(TILES):
                    ins = pe.transpose(psT[:, t * P:(t + 1) * P], xn[k][:, t, :], ident[:, :])
                ins.then_inc(turned, 1)

            def route(j, k):
                pe.wait_ge(xnT_done[k], ONE + j + 1)
                pe.wait_ge(gap_done, ONE + 2 * j + k)
                for t in range(TILES):
                    ins = pe.matmul(psR[:, t * E0:(t + 1) * E0], xnT[k][:, t * P:(t + 1) * P], router[:, :], start=True, stop=True)
                ins.then_inc(routed, 1)

            def up(g, k, e):
                for c in range(CH0):
                    pe.wait_ge(h_done[c], ONE + g * UNITS0 + e)
                    cols = slice(e * HID0 + c * P, e * HID0 + (c + 1) * P)
                    sw.up(pe, psG[c][:, :], 0, cols, x_hi[k][:, :], x_lo[k][:, :])
                    sw.up(pe, psU[c][:, :], 1, cols, x_hi[k][:, :], x_lo[k][:, :]).then_inc(up_done, 1)

            def down(g, k, e, fresh=False):
                n, u = g * UNITS0 + e, three(k, e)
                for c in range(CH0):
                    pe.wait_ge(lo_done[c], ONE + n + 1)
                if not fresh:
                    pe.wait_ge(added, ONE + n - 1)
                for t in range(TILES):
                    for c in range(CH0):
                        ins = sw.down(pe, psY[two(k, e)][:, t, :], e * CH0 + c, h_hi[u][c][:, t * P:(t + 1) * P],
                                      h_lo[u][c][:, t * P:(t + 1) * P], c == 0, c == CH0 - 1)
                ins.then_inc(y_done, 1)

            def step(j, k, first, last):
                g = 2 * j + k
                pe.wait_ge(x_lo_done, ONE + g + 1)
                for e in range(UNITS0):
                    up(g, k, e)
                    if e >= LAG or not first:
                        down(*lagging(g, k, e), first and e == LAG)
                    if not last and e == LN_AT:
                        turn(*following(j, k))
                    if not last and e == ROUTE_AT:
                        route(*following(j, k))

            pe.wait_ge(const_in, ONE + 16 * len(consts))
            turn(0, 0)
            route(0, 0)
            over_groups(pe, step)
            for e in range(UNITS0 - LAG, UNITS0):
                down(GROUPS - 1, 1, e)

        @block.scalar
        def _(act):
            def xnT_out(j, k):
                act.wait_ge(turned, ONE + 2 * j + k + 1)
                act.wait_ge(stored[k], ONE + 16 * j)
                act.activation(x_hi[k][:, :], psT[:, :], ACT.Copy, scale=X_SCALE)
                act.activation(xnT[k][:, :], psT[:, :], ACT.Copy).then_inc(xnT_done[k], 1)

            def tanh_of_gap(j, k):
                act.wait_ge(gap_done, ONE + 2 * j + k + 1)
                act.activation(tanh[:, :], gap[:, :], ACT.Tanh, scale=0.5).then_inc(tanh_done, 1)

            def high_part(g, k, e, c, fresh=False):
                n = g * UNITS0 + e
                act.wait_ge(h_done[c], ONE + n + 1)
                if not fresh:
                    act.wait_ge(y_done, ONE + n - 2)
                act.activation(h_hi[three(k, e)][c][:, :], hid[two(k, e)][c][:, :], ACT.Copy).then_inc(hi_done[c], 1)

            def step(j, k, first, last):
                g = 2 * j + k
                for e in range(UNITS0):
                    for c in range(CH0):
                        act.wait_ge(up_done, ONE + CH0 * (g * UNITS0 + e) + c + 1)
                        act.wait_ge(h_done[c], ONE + g * UNITS0 + e)
                        act.activation(act_g[c][:, :], psG[c][:, :], ACT.Silu, scale=sw.unscale[:, 0:1]).then_inc(silu_done, 1)
                        if c:
                            high_part(g, k, e, 0, first and e < 2)
                        elif e:
                            high_part(g, k, e - 1, 1, first and e < 3)
                        elif not first:
                            high_part(g - 1, 1 - k, UNITS0 - 1, 1)
                    if not last and e == LN_AT:
                        xnT_out(*following(j, k))
                    if not last and e == ROUTE_AT:
                        tanh_of_gap(*following(j, k))

            xnT_out(0, 0)
            tanh_of_gap(0, 0)
            over_groups(act, step)
            high_part(GROUPS - 1, 1, UNITS0 - 1, 1)

        @block.vector
        def _(v):
            step_ = Steps(v, front_step)

            def statistics(j, k):
                v.wait_ge(x_in[k], ONE + 16 * (j + 1))
                ln.statistics(v, 2 * j + k, k, x[k])

            def normalise(j, k):
                ln.apply(v, 2 * j + k, k, x[k], xn[k]).then_inc(xn_done[k], 1)

            def low_part(j, k):
                v.wait_ge(xnT_done[k], ONE + j + 1)
                v.scalar_tensor_tensor(out=x_lo[k][:, :], in0=xnT[k][:, :], scalar=X_SCALE, in1=x_hi[k][:, :],
                                       op0=ALU.mult, op1=ALU.subtract).then_inc(x_lo_done, 1)

            def gap_of(j, k):
                step_.at((2 * j + k) * ROUTE_STEPS)
                v.wait_ge(routed, ONE + 2 * j + k + 1)
                step_(v.tensor_tensor(logits[:, :, :], psR[:, 0:TILES * E0].rearrange("p (t e) -> p t e", t=TILES),
                                      bias[:, :].unsqueeze(1).to_broadcast([P, TILES, E0]), ALU.add))
                apart(v)
                for t in range(TILES):
                    ins = v.max(top[:, t, :], logits[:, t, :])
                step_(ins)
                v.tensor_tensor(gap[:, :], top[:, :, 0], top[:, :, 1], ALU.subtract).then_inc(gap_done, 1)
                for t in range(TILES):
                    ins = v.max_index(where[:, t, :], top[:, t, :], logits[:, t, :])
                step_(ins)
                step_(v.tensor_copy(wheref[:, :, :], where[:, :, :]))

            def weights(j, k):
                v.wait_ge(tanh_done, ONE + 2 * j + k + 1)
                half, minus_half = sw.half[:, 0:1], sw.minus_half[:, 0:1]
                step_(v.tensor_scalar(share[:, 0, :], tanh[:, :], half, half, ALU.mult, ALU.add))
                step_(v.tensor_scalar(share[:, 1, :], tanh[:, :], minus_half, half, ALU.mult, ALU.add))
                for n in range(2):
                    for t in range(TILES):
                        ins = v.tensor_scalar(pick[:, n, t, :], iota[:, :], wheref[:, t, n:n + 1], share[:, n, t:t + 1],
                                              ALU.is_equal, ALU.mult)
                step_(ins)
                step_(v.tensor_tensor(cw[k][:, :, :], pick[:, 0, :, :], pick[:, 1, :, :], ALU.add))

            def gated(g, k, e, first):
                for c in range(CH0):
                    n = g * UNITS0 + e
                    v.wait_ge(silu_done, ONE + CH0 * n + c + 1)
                    if e or not first:
                        v.wait_ge(lo_done[c], ONE + n - 1)
                    v.scalar_tensor_tensor(out=hid[two(k, e)][c][:, :], in0=psU[c][:, :], scalar=sw.to_hidden[:, 0:1],
                                           in1=act_g[c][:, :], op0=ALU.mult, op1=ALU.mult).then_inc(h_done[c], 1)

            def add(g, k, e):
                n = g * UNITS0 + e
                u = two(k, e)
                v.wait_ge(y_done, ONE + n + 1)
                v.wait_ge(added, ONE + n)
                if e == E0:
                    ins = v.scalar_tensor_tensor(out=x[k][:, :, :], in0=psY[u][:, :, :], scalar=sw.y_unscale[:, 0:1],
                                                 in1=x[k][:, :, :], op0=ALU.mult, op1=ALU.add)
                else:
                    for t in range(TILES):
                        ins = v.scalar_tensor_tensor(out=x[k][:, t, :], in0=psY[u][:, t, :], scalar=cw[k][:, t, e:e + 1],
                                                     in1=x[k][:, t, :], op0=ALU.mult, op1=ALU.add)
                ins.then_inc(added, 1)

            def step(j, k, first, last):
                g = 2 * j + k
                for e in range(UNITS0):
                    gated(g, k, e, first)
                    if e >= LAG or not first:
                        add(*lagging(g, k, e))
                    if not last and e == LN_AT - 2:
                        statistics(*following(j, k))
                    if not last and e == LN_AT - 1:
                        normalise(*following(j, k))
                    if not last and e == ROUTE_AT - 1:
                        low_part(*following(j, k))
                    if not last and e == ROUTE_AT:
                        gap_of(*following(j, k))
                    if not last and e == ROUTE_AT + 1:
                        weights(*following(j, k))

            v.wait_ge(const_in, ONE + 16 * len(consts))
            statistics(0, 0)
            normalise(0, 0)
            low_part(0, 0)
            gap_of(0, 0)
            weights(0, 0)
            over_groups(v, step)
            for e in range(UNITS0 - LAG, UNITS0):
                add(GROUPS - 1, 1, e)


def phase_attention(nc, sems, a, s, hb):
    NS = H1 * S
    with ExitStack() as ctx:
        r = Room(nc, ctx, sems, "attn")
        ident = r.sb("ident", [P, P])
        wq, wk, wv, wp = (r.sb(n, [D, D]) for n in ("wq", "wk", "wv", "wp"))
        bq, bqs, bk = (r.sb(n, [D, 1]) for n in ("bq", "bqs", "bk"))
        bv, bp = r.sb("bv", [P, D]), r.sb("bp", [P, D])
        x = [r.sb(f"x{k}", [P, TILES, D]) for k in range(2)]
        xb = [r.sb(f"xb{k}", [P, TILES, D]) for k in range(2)]
        ctxT = [r.sb(f"ctxT{k}", [D, GROUP]) for k in range(2)]
        xn, xnT = r.sb("xn", [P, TILES, D]), r.sb("xnT", [D, GROUP])
        ln = LayerNorm(r)
        queries, kheads, vheads = hb.queries1, hb.keys1, hb.vheads
        kT = r.sb("kT", [D, GROUP])
        peak = [r.sb(f"peak{c}", [P, H1]) for c in range(2)]
        low = [r.sb(f"low{c}", [P, NS]) for c in range(2)]
        prob = [r.sb(f"prob{c}", [P, NS]) for c in range(2)]
        probT = [r.sb(f"probT{c}", [P, HP1, P]) for c in range(2)]
        inv = [r.sb(f"inv{c}", [P, H1]) for c in range(2)]
        heads, headsT = r.sb("heads", [P, TILES, D]), r.sb("headsT", [P, GROUP])
        out = [r.sb(f"out{k}", [P, TILES, D]) for k in range(2)]
        psS = [r.ps(f"psS{c}", [P, NS]) for c in range(2)]
        psP = r.ps("psP", [P, HP1, P])
        psO, psM = r.ps("psO", [P, 512]), r.ps("psM", [P, 512])
        const_in, xb_done = r.sem("const_in"), r.sem2("xb")
        x_in, ctx_in, xn_done, kheads_in = (r.sem2(n) for n in ("x_in", "ctx_in", "xn", "kheads"))
        front_full, back_full = r.sem("front_full"), r.sem("back_full")
        K_AT, T_AT, Q_AT, V_AT, FRONT = 1, 2, 3, 4, 4
        k_done, q_done, v_done, out_done = (r.sem2(n) for n in ("k", "q", "v", "out"))
        headsT_done, xnT_done = r.sem("headsT"), r.sem("xnT")
        scores_done = r.sem("scores")
        low_done, prob_done, turned = (r.sem2(n) for n in ("low", "prob", "turned"))
        probT_done, values_done, heads_done = (r.sem(n) for n in ("probT", "values", "heads"))
        stored, peak_step = r.sem2("stored"), r.sem("peak_step")
        STEPS = 2 * TILES
        consts = ((ident, "ident"), (wq, "wq"), (wk, "wk"), (wv, "wv"), (wp, "wp"), (bq, "bq"), (bk, "bk"), (bv, "bv"), (bp, "bp"))
        block = ctx.enter_context(nc.Block())

        @block.sync
        def _(sp):
            r.start_at_one(sp)

            def load(j, k):
                g = 2 * j + k
                sp.wait_ge(v_done[k], ONE + j)
                apart(sp)
                sp.dma_start(ctxT[k][:, :], a["ctxT"][:, bass.ds(g * GROUP, GROUP)]).then_inc(ctx_in[k], 16)
                sp.wait_ge(xn_done[k], ONE + j)
                apart(sp)
                sp.wait_ge(xb_done[k], ONE + j)
                apart(sp)
                sp.dma_start(x[k][:, :, :], tiles_of(s["x2"], g)).then_inc(x_in[k], 16)

            def spread_keys(j, k, fresh=False):
                sp.wait_ge(k_done[k], ONE + j + 1)
                apart(sp)
                if not fresh:
                    sp.wait_ge(scores_done, ONE + TILES * (2 * j + k - 1))
                    apart(sp)
                for h in range(H1):
                    sp.dma_start(kheads[k][h * DH1:(h + 1) * DH1, :, h % HP1, :],
                                 kT[h * DH1:(h + 1) * DH1, :].rearrange("d (b t) -> d b t", b=GB)).then_inc(kheads_in[k], 16)

            def store(j, k):
                sp.wait_ge(out_done[k], ONE + j + 1)
                apart(sp)
                rows = s["x3"].rearrange("(e b c) d -> b e c d", e=E1, b=B)
                for b in range(GB):
                    i, b2 = b // 2, b % 2
                    sp.dma_start(rows[bass.ds((2 * j + k) * GB + b, 1)].rearrange("b e c d -> (b e) c d"),
                                 out[k][b2 * S:(b2 + 1) * S, i, :]).then_inc(stored[k], 16)

            def step(j, k, first, last):
                if not last:
                    load(*following(j, k))
                    spread_keys(*following(j, k), first)
                if not first:
                    store(*before(j, k))

            load(0, 0)
            for dst, src in consts:
                sp.dma_start(whole(dst), a[src]).then_inc(const_in, 16)
            spread_keys(0, 0, True)
            over_groups(sp, step)
            store(GROUPS // 2 - 1, 1)
            for k in range(2):
                sp.wait_ge(stored[k], ONE + 16 * GB * (GROUPS // 2))

        @block.gpsimd
        def _(pool):
            def front(j, k):
                ln.root(pool, 2 * j + k, k)
                pool.wait_ge(x_in[k], ONE + 16 * (j + 1))
                pool.wait_ge(out_done[k], ONE + j)
                pool.tensor_tensor(xb[k][:, :, :], x[k][:, :, :], bp[:, :].unsqueeze(1).to_broadcast([P, TILES, D]),
                                   ALU.add).then_inc(xb_done[k], 1)

            def step(j, k, first, last):
                if not last:
                    front(*following(j, k))

            ln.power_const(pool)
            pool.wait_ge(const_in, ONE + 16 * len(consts))
            front(0, 0)
            over_groups(pool, step)

        @block.tensor
        def _(pe):
            def k_(j, k):
                pe.wait_ge(ctx_in[k], ONE + 16 * (j + 1))
                pe.matmul(psM[:, :], wk[:, :], ctxT[k][:, :], start=True, stop=True).then_inc(front_full, 1)

            def turn(j, k):
                pe.wait_ge(xn_done[k], ONE + j + 1)
                for t in range(TILES):
                    ins = pe.transpose(psM[:, t * P:(t + 1) * P], xn[:, t, :], ident[:, :])
                ins.then_inc(front_full, 1)

            def q_(j, k):
                pe.wait_ge(xnT_done, ONE + 2 * j + k + 1)
                pe.matmul(psM[:, :], wq[:, :], xnT[:, :], start=True, stop=True).then_inc(front_full, 1)

            def v_(j, k):
                pe.wait_ge(q_done[k], ONE + j + 1)
                for b in range(GB):
                    for half in range(2):
                        ins = pe.matmul(psM[half * S:(half + 1) * S, b * S:(b + 1) * S], ctxT[k][:, b * S:(b + 1) * S],
                                        wv[:, half * HP1 * DH1:(half + 1) * HP1 * DH1], start=True, stop=True)
                ins.then_inc(front_full, 1)

            def turn_heads(j, k):
                pe.wait_ge(heads_done, ONE + 4 * (2 * j + k) + 4)
                for t in range(TILES):
                    ins = pe.transpose(psM[:, t * P:(t + 1) * P], heads[:, t, :], ident[:, :])
                ins.then_inc(back_full, 1)

            def project(j, k):
                pe.wait_ge(headsT_done, ONE + 2 * j + k + 1)
                for t in range(TILES):
                    ins = pe.matmul(psM[:, t * D:(t + 1) * D], headsT[:, t * P:(t + 1) * P], wp[:, :], start=True, stop=True)
                ins.then_inc(back_full, 1)

            def scores(j, k, i):
                g, c = 2 * j + k, i % 2
                pe.wait_ge(low_done[c], ONE + 2 * g + i // 2)
                for b2 in range(2):
                    b = 2 * i + b2
                    ins = pe.matmul(psS[c][:, b2 * HP1 * S:(b2 + 1) * HP1 * S], queries[k][:, b, :, :].rearrange("p n t -> p (n t)"),
                                    kheads[k][:, b, :, :].rearrange("p m t -> p (m t)"), start=True, stop=True)
                ins.then_inc(scores_done, 1)

            def turn_prob(j, k, i):
                g, c = 2 * j + k, i % 2
                pe.wait_ge(prob_done[c], ONE + 2 * g + i // 2 + 1)
                pe.wait_ge(probT_done, ONE + 4 * g + i)
                for m in range(HP1):
                    ins = pe.transpose(psP[:, m, :], prob[c][:, m * P:(m + 1) * P], ident[:, :])
                ins.then_inc(turned[c], 1)

            def values(j, k, i):
                g, c = 2 * j + k, i % 2
                pe.wait_ge(probT_done, ONE + 4 * g + i + 1)
                pe.wait_ge(heads_done, ONE + 4 * g + i)
                for m in range(HP1 // 2):
                    for n in range(2):
                        for b2 in range(2):
                            at = 2 * m + n
                            ins = pe.matmul(psO[b2 * S:(b2 + 1) * S, at * 2 * VW1:(at + 1) * 2 * VW1],
                                            probT[c][:, b2 * HP1 // 2 + m, n * S:(n + 1) * S],
                                            vheads[k][:, 2 * i + b2, at, :, :].rearrange("p n w -> p (n w)"), start=True, stop=True)
                ins.then_inc(values_done, 1)

            def step(j, k, first, last):
                prev, nxt = before(j, k), following(j, k)
                pe.wait_ge(v_done[k], ONE + j + 1)
                if not first:
                    turn_prob(*prev, TILES - 1)
                pe.wait_ge(kheads_in[k], ONE + 16 * H1 * (j + 1))
                pe.wait_ge(q_done[k], ONE + j + 1)
                scores(j, k, 0)
                if not last:
                    k_(*nxt)
                if not first:
                    values(*prev, TILES - 1)
                scores(j, k, 1)
                if not last:
                    pe.wait_ge(k_done[nxt[1]], ONE + nxt[0] + 1)
                if not first:
                    turn_heads(*prev)
                turn_prob(j, k, 0)
                scores(j, k, 2)
                if not first:
                    project(*prev)
                values(j, k, 0)
                if not last:
                    if not first:
                        pe.wait_ge(out_done[prev[1]], ONE + prev[0] + 1)
                    turn(*nxt)
                turn_prob(j, k, 1)
                scores(j, k, 3)
                if not last:
                    q_(*nxt)
                values(j, k, 1)
                turn_prob(j, k, 2)
                if not last:
                    v_(*nxt)
                values(j, k, 2)

            pe.wait_ge(const_in, ONE + 16 * len(consts))
            k_(0, 0)
            pe.wait_ge(k_done[0], ONE + 1)
            turn(0, 0)
            q_(0, 0)
            v_(0, 0)
            over_groups(pe, step)
            turn_prob(GROUPS // 2 - 1, 1, TILES - 1)
            values(GROUPS // 2 - 1, 1, TILES - 1)
            pe.wait_ge(out_done[0], ONE + GROUPS // 2)
            turn_heads(GROUPS // 2 - 1, 1)
            project(GROUPS // 2 - 1, 1)

        @block.scalar
        def _(act):
            def k_out(j, k):
                act.wait_ge(front_full, ONE + (2 * j + k) * FRONT + K_AT)
                act.wait_ge(kheads_in[1 - k], ONE + 16 * H1 * (j + k))
                act.activation(kT[:, :], psM[:, :], ACT.Identity, bias=bk[:, 0:1]).then_inc(k_done[k], 1)

            def xnT_out(j, k):
                act.wait_ge(front_full, ONE + (2 * j + k) * FRONT + T_AT)
                act.activation(xnT[:, :], psM[:, :], ACT.Copy).then_inc(xnT_done, 1)

            def q_out(j, k):
                act.wait_ge(front_full, ONE + (2 * j + k) * FRONT + Q_AT)
                for n in range(2):
                    rows = slice(n * D // 2, (n + 1) * D // 2)
                    ins = act.activation(queries[k][rows, :, n, :], psM[rows, :].rearrange("p (b t) -> p b t", b=GB),
                                         ACT.Identity, bias=bqs[rows, 0:1], scale=SCALE1)
                ins.then_inc(q_done[k], 1)

            def probs(j, k, i):
                c, n = i % 2, 2 * (2 * j + k) + i // 2
                act.wait_ge(low_done[c], ONE + n + 1)
                act.wait_ge(turned[c], ONE + n)
                act.activation(prob[c][:, :], low[c][:, :], ACT.Exp).then_inc(prob_done[c], 1)

            def probT_out(j, k, i):
                g, c = 2 * j + k, i % 2
                act.wait_ge(turned[c], ONE + 2 * g + i // 2 + 1)
                if i:
                    act.wait_ge(values_done, ONE + 4 * g + i - 1)
                else:
                    act.wait_ge(values_done, ONE + 4 * g)
                act.activation(probT[c][:, :, :], psP[:, :, :], ACT.Copy).then_inc(probT_done, 1)

            def headsT_out(j, k):
                act.wait_ge(back_full, ONE + 2 * (2 * j + k) + 1)
                act.activation(headsT[:, :], psM[:, :], ACT.Copy).then_inc(headsT_done, 1)

            def step(j, k, first, last):
                prev, nxt = before(j, k), following(j, k)
                if not first:
                    probT_out(*prev, TILES - 1)
                if not last:
                    k_out(*nxt)
                probs(j, k, 0)
                if not first:
                    headsT_out(*prev)
                probT_out(j, k, 0)
                probs(j, k, 1)
                if not last:
                    xnT_out(*nxt)
                probT_out(j, k, 1)
                probs(j, k, 2)
                if not last:
                    q_out(*nxt)
                probs(j, k, 3)
                probT_out(j, k, 2)

            act.wait_ge(const_in, ONE + 16 * len(consts) + 1)
            k_out(0, 0)
            xnT_out(0, 0)
            q_out(0, 0)
            over_groups(act, step)
            probT_out(GROUPS // 2 - 1, 1, TILES - 1)
            headsT_out(GROUPS // 2 - 1, 1)

        @block.vector
        def _(v):
            top = Steps(v, peak_step)

            def statistics(j, k):
                v.wait_ge(x_in[k], ONE + 16 * (j + 1))
                ln.statistics(v, 2 * j + k, k, x[k])

            def normalise(j, k):
                ln.apply(v, 2 * j + k, k, x[k], xn).then_inc(xn_done[k], 1)

            def v_out(j, k):
                v.wait_ge(front_full, ONE + (2 * j + k) * FRONT + V_AT)
                for half in range(2):
                    rows, cols = slice(half * S, (half + 1) * S), slice(half * HP1 * DH1, (half + 1) * HP1 * DH1)
                    ins = v.tensor_tensor(vheads[k][rows, :, :, half, 0:DH1],
                                          psM[rows, :].rearrange("p (b m w) -> p b m w", b=GB, m=HP1),
                                          bv[rows, cols].rearrange("p (m w) -> p m w", m=HP1).unsqueeze(1).to_broadcast(
                                              [S, GB, HP1, DH1]), ALU.add)
                ins.then_inc(v_done[k], 1)

            def lower(j, k, i):
                g, c = 2 * j + k, i % 2
                sc = psS[c][:, :].rearrange("p (h t) -> p h t", h=H1)
                v.wait_ge(scores_done, ONE + TILES * g + i + 1)
                top(v.tensor_reduce(peak[c][:, :], sc, AX.X, ALU.max))
                v.wait_ge(prob_done[c], ONE + 2 * g + i // 2)
                v.tensor_tensor(low[c][:, :].rearrange("p (h t) -> p h t", h=H1), sc,
                                peak[c][:, :].unsqueeze(2).to_broadcast([P, H1, S]), ALU.subtract).then_inc(low_done[c], 1)

            def heads_out(j, k, i):
                v.wait_ge(values_done, ONE + 4 * (2 * j + k) + i + 1)
                o = psO[:, 0:H1 * VW1].rearrange("p (h w) -> p h w", w=VW1)
                top(v.reciprocal(inv[i % 2][:, :], o[:, :, DH1]))
                v.tensor_tensor(heads[:, i, :].rearrange("p (h w) -> p h w", w=DH1), o[:, :, 0:DH1],
                                inv[i % 2][:, :].unsqueeze(2).to_broadcast([P, H1, DH1]), ALU.mult).then_inc(heads_done, 1)

            def out_(j, k):
                v.wait_ge(back_full, ONE + 2 * (2 * j + k) + 2)
                v.wait_ge(xb_done[k], ONE + j + 1)
                v.wait_ge(stored[k], ONE + 16 * GB * j)
                v.tensor_tensor(out[k][:, :, :], psM[:, :].rearrange("p (t d) -> p t d", t=TILES), xb[k][:, :, :],
                                ALU.add).then_inc(out_done[k], 1)

            def step(j, k, first, last):
                prev, nxt = before(j, k), following(j, k)
                top.at(0 if first else (2 * j + k) * STEPS - 1)
                lower(j, k, 0)
                if not first:
                    heads_out(*prev, TILES - 1)
                if not last:
                    statistics(*nxt)
                lower(j, k, 1)
                if not last:
                    normalise(*nxt)
                if not first:
                    out_(*prev)
                lower(j, k, 2)
                heads_out(j, k, 0)
                lower(j, k, 3)
                heads_out(j, k, 1)
                if not last:
                    v_out(*nxt)
                heads_out(j, k, 2)

            v.wait_ge(const_in, ONE + 16 * len(consts))
            v.tensor_scalar(bqs[:, :], bq[:, :], SCALE1, None, ALU.mult).then_inc(const_in, 1)
            statistics(0, 0)
            normalise(0, 0)
            v_out(0, 0)
            over_groups(v, step)
            top.at(GROUPS * STEPS - 1)
            heads_out(GROUPS // 2 - 1, 1, TILES - 1)
            out_(GROUPS // 2 - 1, 1)


def phase_ffn(nc, sems, a, s):
    UNITS = 2 * E1
    NC = len(CHUNKS1)
    with ExitStack() as ctx:
        r = Room(nc, ctx, sems, "ffn")
        ident = r.sb("ident", [P, P])
        w1 = [r.sb(f"w1{w}", [D, FF1]) for w in range(2)]
        w3 = [r.sb(f"w3{w}", [D, FF1]) for w in range(2)]
        w2 = [r.sb(f"w2{w}", [P, NC, D]) for w in range(2)]
        x = [r.sb(f"x{q}", [P, TILES, D]) for q in range(4)]
        out = [r.sb(f"out{k}", [P, TILES, D]) for k in range(2)]
        xn, xnT = r.sb("xn", [P, TILES, D]), [r.sb(f"xnT{k}", [D, GROUP]) for k in range(2)]
        ln = LayerNorm(r)
        act_g = [r.sb(f"act_g{c}", [P, GROUP]) for c in range(2)]
        hT = [[r.sb(f"hT{k}{c}", [P, GROUP]) for c in range(NC)] for k in range(2)]
        psT = r.ps("psT", [P, GROUP])
        psG = [r.ps(f"psG{c}", [P, GROUP]) for c in range(2)]
        psU = [r.ps(f"psU{c}", [P, GROUP]) for c in range(2)]
        psY = [r.ps(f"psY{k}", [P, TILES, D]) for k in range(2)]
        const_in, w_in, x_in = r.sem("const_in"), r.sem2("w_in"), [r.sem(f"x_in{q}") for q in range(4)]
        xn_done, turned, xnT_done = r.sem2("xn"), r.sem("turned"), r.sem2("xnT")
        up_done, silu_done, h_done = r.sem("up"), r.sem("silu"), r.sem("h")
        y_done, out_done, stored = r.sem2("y"), r.sem2("out"), r.sem2("stored")
        block = ctx.enter_context(nc.Block())

        @block.sync
        def _(sp):
            r.start_at_one(sp)
            sp.dma_start(ident[:, :], a["ident"]).then_inc(const_in, 16)

            def load(j, q):
                sp.dma_start(x[q][:, :, :], tiles_of(s["x3"], 4 * j + q)).then_inc(x_in[q], 16)

            def load_weights(j, w):
                e = 2 * j + w
                sp.wait_ge(y_done[1], ONE + e - 1)
                apart(sp)
                sp.dma_start(w1[w][:, :], a["f1"][bass.ds(e, 1)].rearrange("e d f -> (e d) f")).then_inc(w_in[w], 16)
                sp.dma_start(w3[w][:, :], a["f3"][bass.ds(e, 1)].rearrange("e d f -> (e d) f")).then_inc(w_in[w], 16)
                sp.dma_start(w2[w][:, :, :], a["f2"][bass.ds(e, 1)].rearrange("e p c d -> (e p) c d")).then_inc(w_in[w], 16)

            def store(j, q):
                k = q % 2
                sp.wait_ge(out_done[k], ONE + 2 * j + q // 2 + 1)
                apart(sp)
                sp.dma_start(tiles_of(s["out"], 4 * j + q), out[k][:, :, :]).then_inc(stored[k], 16)

            def step(j, q, first, left):
                if not first:
                    store(*before_it(j, q))
                if left >= 3:
                    load(*ahead(j, q, 3))
                if q == 0 or q == 2 and left >= 3:
                    nj, nq = ahead(j, q, 2)
                    load_weights(nj, nq // 2)

            for q in range(3):
                load(0, q)
            for dst, src in ((w1, "f1"), (w3, "f3")):
                sp.dma_start(dst[0][:, :], a[src][0]).then_inc(w_in[0], 16)
            sp.dma_start(w2[0][:, :, :], a["f2"][0]).then_inc(w_in[0], 16)
            over_fours(sp, step, UNITS)
            store(UNITS // 4 - 1, 3)
            for k in range(2):
                sp.wait_ge(stored[k], ONE + 16 * (UNITS // 2))

        @block.gpsimd
        def _(pool):
            ln.roots(pool, UNITS)

        @block.tensor
        def _(pe):
            def turn(j, q):
                k, m = q % 2, 2 * j + q // 2
                pe.wait_ge(xn_done[k], ONE + m + 1)
                pe.wait_ge(xnT_done[1 - k], ONE + m + k)
                for t in range(TILES):
                    ins = pe.transpose(psT[:, t * P:(t + 1) * P], xn[:, t, :], ident[:, :])
                ins.then_inc(turned, 1)

            def up(j, q, c):
                u, k, w = 4 * j + q, q % 2, q // 2
                g = (NC * q + c) % 2
                f, m = CHUNKS1[c]
                if c:
                    pe.wait_ge(h_done, ONE + NC * u + c - 1)
                else:
                    pe.wait_ge(h_done, ONE + NC * u)
                pe.matmul(psG[g][0:m, :], w1[w][:, f:f + m], xnT[k][:, :], start=True, stop=True)
                pe.matmul(psU[g][0:m, :], w3[w][:, f:f + m], xnT[k][:, :], start=True, stop=True).then_inc(up_done, 1)

            def down(j, q):
                u, k, w = 4 * j + q, q % 2, q // 2
                pe.wait_ge(h_done, ONE + NC * (u + 1))
                pe.wait_ge(out_done[k], ONE + 2 * j + q // 2)
                for t in range(TILES):
                    for c, (f, m) in enumerate(CHUNKS1):
                        ins = pe.matmul(psY[k][:, t, :], hT[k][c][0:m, t * P:(t + 1) * P], w2[w][0:m, c, :],
                                        start=(c == 0), stop=(c == NC - 1))
                ins.then_inc(y_done[k], 1)

            def step(j, q, first, left):
                k, w = q % 2, q // 2
                pe.wait_ge(w_in[w], ONE + 48 * (j + 1))
                pe.wait_ge(xnT_done[k], ONE + 2 * j + q // 2 + 1)
                up(j, q, 0)
                if not first:
                    down(*before_it(j, q))
                up(j, q, 1)
                if left >= 1:
                    turn(*ahead(j, q, 1))
                up(j, q, 2)

            pe.wait_ge(const_in, ONE + 16)
            turn(0, 0)
            over_fours(pe, step, UNITS)
            down(UNITS // 4 - 1, 3)

        @block.scalar
        def _(act):
            def xnT_out(j, q):
                k, m = q % 2, 2 * j + q // 2
                act.wait_ge(turned, ONE + 4 * j + q + 1)
                act.wait_ge(y_done[k], ONE + m)
                act.activation(xnT[k][:, :], psT[:, :], ACT.Copy).then_inc(xnT_done[k], 1)

            def step(j, q, first, left):
                u = 4 * j + q
                for c, (f, m) in enumerate(CHUNKS1):
                    g = (NC * q + c) % 2
                    act.wait_ge(up_done, ONE + NC * u + c + 1)
                    if c:
                        act.wait_ge(h_done, ONE + NC * u + c - 1)
                    else:
                        act.wait_ge(h_done, ONE + NC * u)
                    act.activation(act_g[g][0:m, :], psG[g][0:m, :], ACT.Silu).then_inc(silu_done, 1)
                    if left >= 1 and c == 1:
                        xnT_out(*ahead(j, q, 1))

            xnT_out(0, 0)
            over_fours(act, step, UNITS)

        @block.vector
        def _(v):
            def statistics(j, q):
                v.wait_ge(x_in[q], ONE + 16 * (j + 1))
                ln.statistics(v, 4 * j + q, q % 2, x[q])

            def normalise(j, q):
                ln.apply(v, 4 * j + q, q % 2, x[q], xn).then_inc(xn_done[q % 2], 1)

            def gated(j, q, c):
                u, k = 4 * j + q, q % 2
                f, m = CHUNKS1[c]
                g = (NC * q + c) % 2
                v.wait_ge(silu_done, ONE + NC * u + c + 1)
                v.tensor_tensor(hT[k][c][0:m, :], act_g[g][0:m, :], psU[g][0:m, :], ALU.mult).then_inc(h_done, 1)

            def out_(j, q):
                k, n = q % 2, 2 * j + q // 2
                v.wait_ge(y_done[k], ONE + n + 1)
                v.wait_ge(stored[k], ONE + 16 * n)
                v.tensor_tensor(out[k][:, :, :], psY[k][:, :, :], x[q][:, :, :], ALU.add).then_inc(out_done[k], 1)

            def step(j, q, first, left):
                v.wait_ge(y_done[q % 2], ONE + 2 * j + q // 2)
                gated(j, q, 0)
                if left >= 1:
                    normalise(*ahead(j, q, 1))
                if not first:
                    out_(*before_it(j, q))
                gated(j, q, 1)
                gated(j, q, 2)
                if left >= 2:
                    statistics(*ahead(j, q, 2))

            statistics(0, 0)
            normalise(0, 0)
            statistics(0, 1)
            over_fours(v, step, UNITS)
            out_(UNITS // 4 - 1, 3)


SCRATCH = {
    "xnT": ([D, TOKENS], F32),
    "gates": ([B, 2 * H0, S], F32),
    "floor": ([P, PAIRS, H0], F32),
    "m_rows": ([NSPLIT * 2, B * HP0 * S], BF16),
    "a_rows": ([NSPLIT * 2 * HP0, TOKENS], BF16),
    "x1": ([TOKENS, D], F32),
    "x2": ([TOKENS, D], F32),
    "x3": ([TOKENS, D], F32),
}


def build(nc, a, out):
    s = {n: nc.dram_tensor(f"scratch_{n}", shape, dt).ap() for n, (shape, dt) in SCRATCH.items()}
    s["out"] = out
    with ExitStack() as sems:
        phase_gates(nc, sems, a, s)
        with ExitStack() as shared:
            heads = HeadBuffers(nc, shared, sems)
            with ExitStack() as weights:
                split = SplitWeights(nc, weights, sems)
                phase_decay(nc, sems, a, s, split, heads)
                phase_mlstm(nc, sems, a, s, split, heads)
                phase_experts(nc, sems, a, s, split)
            phase_attention(nc, sems, a, s, heads)
        phase_ffn(nc, sems, a, s)


def bf16_bits(constant):
    return (constant.view(np.uint32) >> 16).astype(np.uint16)


def layouts(i):
    i = {n: np.asarray(v) for n, v in i.items()}
    ctx = i["ctx_1024"].reshape(TOKENS, D)
    rows = lambda v: np.broadcast_to(v, (P, v.shape[0]))
    gates = [i["L0_xattn_igate_w"], i["L0_xattn_fgate_w"]]
    gate = lambda n: np.concatenate([w[:, n * D:(n + 1) * D].T for w in gates], 1)
    units = lambda w, sw: np.concatenate([i[w], i[sw]], 0)
    values = np.zeros((2, S, B, HP0, 2, VW0), np.float32)
    for h in range(2):
        values[h, :, :, :, h, 0:DH0] = ctx.reshape(B, S, HP0, 2, DH0)[:, :, :, h].transpose(1, 0, 2, 3)
        values[h, :, :, :, h, DH0] = 1.0
    t = np.arange(S)
    pair_of = np.repeat(np.arange(2 * HP0), S)
    keys = np.zeros((DECAY_ROWS, GROUP), np.float32)
    keys[0:S] = np.tile(np.eye(S), (1, 2 * TILES))
    keys[M_ROW:] = np.tile(np.repeat(np.eye(2), S, 1), (NSPLIT, TILES))
    queries = np.zeros((DECAY_ROWS, TILES, H0 * S), np.float32)
    queries[0:S] = np.where(t[:, None] <= np.tile(t, H0)[None], 0.0, MASKED)[:, None, :]
    queries[A_ROW:M_ROW] = np.tile(np.arange(2 * HP0)[:, None] == pair_of[None], (NSPLIT, 1))[:, None, :]
    first = np.tile(t == 0, H0)
    by_n = lambda w, pairs: np.swapaxes(w.reshape(w.shape[:-1] + (pairs, 2, -1)), -3, -2).reshape(w.shape)
    fours = lambda w: w.reshape(w.shape[:-1] + (HP1 // 2, 2, 2, DH1))
    by_m2 = lambda w: np.swapaxes(fours(w), -4, -3).reshape(w.shape)
    as_summed = lambda w: np.swapaxes(fours(w), -3, -2).reshape(w.shape)
    f2 = np.zeros((E1, len(CHUNKS1) * P, D), np.float32)
    f2[:, 0:FF1] = i["L1_ffn_w2"]
    return {
        "x": i["x"].reshape(TOKENS, D),
        "ctxT": ctx.T,
        "ctxT_n": by_n(ctx, HP0).T,
        "values": values.reshape(P, B, HP0, 2 * VW0),
        "ident": np.eye(P, dtype=np.float32),
        "gate_wq": gate(0), "gate_wk": gate(1), "gate_wv": gate(2),
        "gate_b": np.concatenate([i["L0_xattn_igate_b"], i["L0_xattn_fgate_b"]])[:, None],
        "scan_keep": rows(np.where(first, 0.0, 1.0).astype(np.float32)),
        "scan_drop": rows(np.where(first, MASKED, 0.0).astype(np.float32)),
        "ln_scale": rows(i["L0_xattn_ln_scale"]),
        "decay_keys": bf16_bits(keys),
        "decay_queries": bf16_bits(queries),
        "router": i["L0_ffn_router_w"].T,
        "router_b": rows(i["L0_ffn_experts_bias"]),
        "iota": rows(np.arange(E0, dtype=np.float32)),
        "w1": units("L0_ffn_w1", "L0_ffn_sw1").transpose(1, 0, 2),
        "w3": units("L0_ffn_w3", "L0_ffn_sw3").transpose(1, 0, 2),
        "w2": units("L0_ffn_w2", "L0_ffn_sw2").reshape(UNITS0 * CH0, P, D).transpose(1, 0, 2),
        "wq": by_n(i["L1_xattn_Wq"].T, HP1), "wk": by_n(i["L1_xattn_Wk"].T, HP1),
        "wv": by_m2(i["L1_xattn_Wv"].T), "wp": as_summed(i["L1_xattn_Wp"]).T,
        "bq": by_n(i["L1_xattn_bq"], HP1)[:, None], "bk": by_n(i["L1_xattn_bk"], HP1)[:, None],
        "bv": rows(by_m2(i["L1_xattn_bv"])), "bp": rows(i["L1_xattn_bp"]),
        "f1": i["L1_ffn_w1"], "f3": i["L1_ffn_w3"],
        "f2": f2.reshape(E1, len(CHUNKS1), P, D).transpose(0, 2, 1, 3),
    }


def kernel(**inputs):
    import concourse.bacc as bacc
    from concourse.bass_utils import run_bass_kernel_spmd

    nc = bacc.Bacc("TRN2", target_bir_lowering=False, num_devices=1)
    arrays, aps = {}, {}
    for name, v in layouts(inputs).items():
        arrays[f"in_{name}"] = np.ascontiguousarray(v)
        aps[name] = nc.dram_tensor(f"in_{name}", v.shape, mybir.dt.from_np(v.dtype), kind="ExternalInput").ap()
    out = nc.dram_tensor("out", (TOKENS, D), F32, kind="ExternalOutput").ap()
    build(nc, aps, out)
    got = run_bass_kernel_spmd(nc, [arrays], core_ids=[0]).results[0]["out"]
    return got.reshape(E1, B, C1, D).transpose(1, 0, 2, 3).reshape(B, S, D)
```
